# Optimizing a Trainium2 kernel written in Bass

```python
import numpy as np
import jax
import jax.numpy as jnp

def _softmax(x, axis=-1):
    return jax.nn.softmax(x, axis=axis)

def _gelu(x):
    return jax.nn.gelu(x, approximate=True)

def _silu(x):
    return jax.nn.silu(x)

def _sigmoid(x):
    return jax.nn.sigmoid(x)

def _layernorm(x, axis=-1, eps=1e-05):
    m = jnp.mean(x, axis=axis, keepdims=True)
    v = jnp.var(x, axis=axis, keepdims=True)
    return (x - m) / jnp.sqrt(v + eps)

def _scatter_add(tgt, idx, src, axis=0):
    return tgt.at[idx].add(src)

def _segment_sum(src, seg, n):
    return jax.ops.segment_sum(src, seg, n)
kernel_name = 'mk_sandwich_d2_jaxref_r8_403c8e'

def setup_inputs(seed: int=0):
    np.random.seed(seed)
    _w = jnp.asarray

    def _L0_attn_setup():
        import jax, jax.numpy as jnp
        import numpy as np
        NUM_HEADS = 16
        NUM_KV_HEADS = 4
        ROPE_BASE = 10000.0

        def _rotate_half(x):
            x1 = x[..., ::2]
            x2 = x[..., 1::2]
            return jnp.stack((-x2, x1), axis=-1).reshape(x.shape)

        def apply_rope(x, positions, base):
            head_dim = x.shape[-1]
            inv_freq = 1.0 / base ** (jnp.arange(0, head_dim, 2, dtype=jnp.float32) / head_dim)
            freqs = positions.astype(jnp.float32)[:, None] * inv_freq[None, :]
            cos = jnp.repeat(jnp.cos(freqs), 2, axis=-1)[None, :, None, :]
            sin = jnp.repeat(jnp.sin(freqs), 2, axis=-1)[None, :, None, :]
            return x * cos + _rotate_half(x) * sin
        key = jax.random.key(seed)
        ks = jax.random.split(key, 9)
        B, S, H = (2, 256, 256)
        kvdim = NUM_KV_HEADS * (H // NUM_HEADS)
        s = 0.02
        return {'x': jax.random.normal(ks[0], (B, S, H), jnp.float32), 'Wq': jax.random.normal(ks[1], (H, H), jnp.float32) * s, 'bq': jnp.zeros((H,), jnp.float32), 'Wk': jax.random.normal(ks[2], (kvdim, H), jnp.float32) * s, 'bk': jnp.zeros((kvdim,), jnp.float32), 'Wv': jax.random.normal(ks[3], (kvdim, H), jnp.float32) * s, 'bv': jnp.zeros((kvdim,), jnp.float32), 'Wo': jax.random.normal(ks[4], (H, H), jnp.float32) * s, 'bo': jnp.zeros((H,), jnp.float32)}
    _L0_attn_in = _L0_attn_setup()

    def _L0_ffn_setup():
        import jax, jax.numpy as jnp
        import numpy as np
        DIM = 256
        INTER = 176
        N_EXPERTS = 16
        TOP_K = 2
        N_SHARED = 2
        SHARED_INTER = N_SHARED * INTER

        def _swiglu(t, wa, wb, wo):
            h = jax.nn.silu(t @ wa.T) * (t @ wb.T)
            return h @ wo.T
        key = jax.random.key(seed)
        ks = jax.random.split(key, 9)
        s = 0.02
        return {'x': jax.random.normal(ks[0], (4, 256, DIM), dtype=jnp.float32), 'gate_w': jax.random.normal(ks[1], (N_EXPERTS, DIM), dtype=jnp.float32) * s, 'w1': jax.random.normal(ks[2], (N_EXPERTS, INTER, DIM), dtype=jnp.float32) * s, 'w2': jax.random.normal(ks[3], (N_EXPERTS, DIM, INTER), dtype=jnp.float32) * s, 'w3': jax.random.normal(ks[4], (N_EXPERTS, INTER, DIM), dtype=jnp.float32) * s, 'sw1': jax.random.normal(ks[5], (SHARED_INTER, DIM), dtype=jnp.float32) * s, 'sw2': jax.random.normal(ks[6], (DIM, SHARED_INTER), dtype=jnp.float32) * s, 'sw3': jax.random.normal(ks[7], (SHARED_INTER, DIM), dtype=jnp.float32) * s}
    _L0_ffn_in = _L0_ffn_setup()

    def _L1_attn_setup():
        import jax, jax.numpy as jnp
        import numpy as np
        D_MODEL = 256
        D_STATE = 16
        D_CONV = 4
        EXPAND = 2
        D_INNER = EXPAND * D_MODEL
        HEAD_DIM = 64
        N_HEADS = D_INNER // HEAD_DIM
        N_GROUPS = 1
        CONV_DIM = D_INNER + 2 * N_GROUPS * D_STATE
        IN_DIM = D_INNER + CONV_DIM + N_HEADS
        BATCH, SEQ = (2, 512)
        EPS = 1e-05
        key = jax.random.key(seed)
        ks = jax.random.split(key, 8)
        s = 0.02
        return {'hidden_states': jax.random.normal(ks[0], (BATCH, SEQ, D_MODEL), jnp.float32), 'W_in': jax.random.normal(ks[1], (D_MODEL, IN_DIM), jnp.float32) * s, 'conv_w': jax.random.normal(ks[2], (CONV_DIM, D_CONV), jnp.float32) * s, 'conv_b': jnp.zeros((CONV_DIM,), jnp.float32), 'A_log': jnp.log(jax.random.uniform(ks[3], (N_HEADS,), jnp.float32, 1.0, 16.0)), 'D_skip': jnp.ones((N_HEADS,), jnp.float32), 'dt_bias': jnp.ones((N_HEADS,), jnp.float32), 'norm_w': jnp.ones((D_INNER,), jnp.float32), 'W_out': jax.random.normal(ks[4], (D_INNER, D_MODEL), jnp.float32) * s}
    _L1_attn_in = _L1_attn_setup()

    def _L1_ffn_setup():
        import jax, jax.numpy as jnp
        import numpy as np
        H = 256
        IM = 128
        E = 16
        K = 8
        N_SHARED = 2
        IS = IM * N_SHARED
        B, L = (1, 256)
        SCALE = 2.5
        W_INIT = 0.02
        key = jax.random.key(seed)
        ks = jax.random.split(key, 9)
        return {'hidden_states': jax.random.normal(ks[0], (B, L, H), jnp.float32), 'gate_w': jax.random.normal(ks[1], (E, H), jnp.float32) * W_INIT, 'Wg': jax.random.normal(ks[2], (E, H, IM), jnp.float32) * W_INIT, 'Wu': jax.random.normal(ks[3], (E, H, IM), jnp.float32) * W_INIT, 'Wd': jax.random.normal(ks[4], (E, IM, H), jnp.float32) * W_INIT, 'sWg': jax.random.normal(ks[5], (H, IS), jnp.float32) * W_INIT, 'sWu': jax.random.normal(ks[6], (H, IS), jnp.float32) * W_INIT, 'sWd': jax.random.normal(ks[7], (IS, H), jnp.float32) * W_INIT}
    _L1_ffn_in = _L1_ffn_setup()
    _d = {'L0_attn_x': _L0_attn_in['x'], 'L0_attn_Wq': _L0_attn_in['Wq'], 'L0_attn_bq': _L0_attn_in['bq'], 'L0_attn_Wk': _L0_attn_in['Wk'], 'L0_attn_bk': _L0_attn_in['bk'], 'L0_attn_Wv': _L0_attn_in['Wv'], 'L0_attn_bv': _L0_attn_in['bv'], 'L0_attn_Wo': _L0_attn_in['Wo'], 'L0_attn_bo': _L0_attn_in['bo'], 'L0_ffn_gate_w': _L0_ffn_in['gate_w'], 'L0_ffn_w1': _L0_ffn_in['w1'], 'L0_ffn_w2': _L0_ffn_in['w2'], 'L0_ffn_w3': _L0_ffn_in['w3'], 'L0_ffn_sw1': _L0_ffn_in['sw1'], 'L0_ffn_sw2': _L0_ffn_in['sw2'], 'L0_ffn_sw3': _L0_ffn_in['sw3'], 'L1_attn_W_in': _L1_attn_in['W_in'], 'L1_attn_conv_w': _L1_attn_in['conv_w'], 'L1_attn_conv_b': _L1_attn_in['conv_b'], 'L1_attn_A_log': _L1_attn_in['A_log'], 'L1_attn_D_skip': _L1_attn_in['D_skip'], 'L1_attn_dt_bias': _L1_attn_in['dt_bias'], 'L1_attn_norm_w': _L1_attn_in['norm_w'], 'L1_attn_W_out': _L1_attn_in['W_out'], 'L1_ffn_gate_w': _L1_ffn_in['gate_w'], 'L1_ffn_Wg': _L1_ffn_in['Wg'], 'L1_ffn_Wu': _L1_ffn_in['Wu'], 'L1_ffn_Wd': _L1_ffn_in['Wd'], 'L1_ffn_sWg': _L1_ffn_in['sWg'], 'L1_ffn_sWu': _L1_ffn_in['sWu'], 'L1_ffn_sWd': _L1_ffn_in['sWd']}
    _x0 = _d['L0_attn_x']
    _d['L0_attn_x'] = jax.random.normal(jax.random.fold_in(jax.random.key(seed), 1), (16, 256, 256), dtype=_x0.dtype)
    del _x0
    return _d

def reference(L0_attn_x, L0_attn_Wq, L0_attn_bq, L0_attn_Wk, L0_attn_bk, L0_attn_Wv, L0_attn_bv, L0_attn_Wo, L0_attn_bo, L0_ffn_gate_w, L0_ffn_w1, L0_ffn_w2, L0_ffn_w3, L0_ffn_sw1, L0_ffn_sw2, L0_ffn_sw3, L1_attn_W_in, L1_attn_conv_w, L1_attn_conv_b, L1_attn_A_log, L1_attn_D_skip, L1_attn_dt_bias, L1_attn_norm_w, L1_attn_W_out, L1_ffn_gate_w, L1_ffn_Wg, L1_ffn_Wu, L1_ffn_Wd, L1_ffn_sWg, L1_ffn_sWu, L1_ffn_sWd):

    def _L0_attn_ref(x, Wq, bq, Wk, bk, Wv, bv, Wo, bo):
        import jax, jax.numpy as jnp
        import numpy as np
        NUM_HEADS = 16
        NUM_KV_HEADS = 4
        ROPE_BASE = 10000.0

        def _rotate_half(x):
            x1 = x[..., ::2]
            x2 = x[..., 1::2]
            return jnp.stack((-x2, x1), axis=-1).reshape(x.shape)

        def apply_rope(x, positions, base):
            head_dim = x.shape[-1]
            inv_freq = 1.0 / base ** (jnp.arange(0, head_dim, 2, dtype=jnp.float32) / head_dim)
            freqs = positions.astype(jnp.float32)[:, None] * inv_freq[None, :]
            cos = jnp.repeat(jnp.cos(freqs), 2, axis=-1)[None, :, None, :]
            sin = jnp.repeat(jnp.sin(freqs), 2, axis=-1)[None, :, None, :]
            return x * cos + _rotate_half(x) * sin
        B, S, hidden = x.shape
        head_dim = hidden // NUM_HEADS
        scale = head_dim ** (-0.5)
        rep = NUM_HEADS // NUM_KV_HEADS
        positions = jnp.arange(S)
        q = (x @ Wq.T + bq).reshape(B, S, NUM_HEADS, head_dim)
        k = (x @ Wk.T + bk).reshape(B, S, NUM_KV_HEADS, head_dim)
        v = (x @ Wv.T + bv).reshape(B, S, NUM_KV_HEADS, head_dim)
        q = apply_rope(q, positions, ROPE_BASE)
        k = apply_rope(k, positions, ROPE_BASE)
        k = jnp.repeat(k, rep, axis=2)
        v = jnp.repeat(v, rep, axis=2)
        scores = jnp.einsum('bthd,bshd->bhts', q, k) * scale
        causal = jnp.tril(jnp.ones((S, S), dtype=bool))
        scores = jnp.where(causal[None, None, :, :], scores, -jnp.inf)
        probs = jax.nn.softmax(scores, axis=-1)
        attended = jnp.einsum('bhts,bshd->bthd', probs, v).reshape(B, S, hidden)
        return attended @ Wo.T + bo

    def _L0_ffn_ref(x, gate_w, w1, w2, w3, sw1, sw2, sw3):
        import jax, jax.numpy as jnp
        import numpy as np
        DIM = 256
        INTER = 176
        N_EXPERTS = 16
        TOP_K = 2
        N_SHARED = 2
        SHARED_INTER = N_SHARED * INTER

        def _swiglu(t, wa, wb, wo):
            h = jax.nn.silu(t @ wa.T) * (t @ wb.T)
            return h @ wo.T
        shape = x.shape
        t = x.reshape(-1, DIM)
        scores = jax.nn.softmax(t @ gate_w.T, axis=-1)
        weights, indices = jax.lax.top_k(scores, TOP_K)
        y = jnp.zeros_like(t)
        for e in range(N_EXPERTS):
            w_e = jnp.sum(jnp.where(indices == e, weights, 0.0), axis=-1)
            y = y + _swiglu(t, w1[e], w3[e], w2[e]) * w_e[:, None]
        z = _swiglu(t, sw1, sw3, sw2)
        return (y + z).reshape(shape)

    def _L1_attn_ref(hidden_states, W_in, conv_w, conv_b, A_log, D_skip, dt_bias, norm_w, W_out):
        import jax, jax.numpy as jnp
        import numpy as np
        D_MODEL = 256
        D_STATE = 16
        D_CONV = 4
        EXPAND = 2
        D_INNER = EXPAND * D_MODEL
        HEAD_DIM = 64
        N_HEADS = D_INNER // HEAD_DIM
        N_GROUPS = 1
        CONV_DIM = D_INNER + 2 * N_GROUPS * D_STATE
        IN_DIM = D_INNER + CONV_DIM + N_HEADS
        BATCH, SEQ = (2, 512)
        EPS = 1e-05
        b, l, _ = hidden_states.shape
        zxbcdt = jnp.einsum('bld,di->bli', hidden_states, W_in)
        gate = zxbcdt[..., :D_INNER]
        xBC = zxbcdt[..., D_INNER:D_INNER + CONV_DIM]
        dt = zxbcdt[..., D_INNER + CONV_DIM:]
        xpad = jnp.pad(xBC, ((0, 0), (D_CONV - 1, 0), (0, 0)))
        conv = conv_b
        for k in range(D_CONV):
            conv = conv + xpad[:, k:k + l, :] * conv_w[:, k]
        xBC = jax.nn.silu(conv)
        x = xBC[..., :D_INNER].reshape(b, l, N_HEADS, HEAD_DIM)
        Bm = xBC[..., D_INNER:D_INNER + D_STATE]
        Cm = xBC[..., D_INNER + D_STATE:]
        dt = jax.nn.softplus(dt + dt_bias)
        A = -jnp.exp(A_log)
        dA = jnp.exp(dt * A)
        xs = x.transpose(1, 0, 2, 3)
        Bs = Bm.transpose(1, 0, 2)
        Cs = Cm.transpose(1, 0, 2)
        dts = dt.transpose(1, 0, 2)
        dAs = dA.transpose(1, 0, 2)
        h0 = jnp.zeros((b, N_HEADS, HEAD_DIM, D_STATE), hidden_states.dtype)

        def step(h, inp):
            x_t, B_t, C_t, dt_t, dA_t = inp
            h = h * dA_t[:, :, None, None] + (dt_t[:, :, None] * x_t)[..., None] * B_t[:, None, None, :]
            y = jnp.einsum('bhpn,bn->bhp', h, C_t)
            return (h, y)
        _, ys = jax.lax.scan(step, h0, (xs, Bs, Cs, dts, dAs))
        y = ys.transpose(1, 0, 2, 3) + D_skip[None, None, :, None] * x
        y = y.reshape(b, l, D_INNER)
        y = y * jax.nn.silu(gate)
        var = jnp.mean(y * y, axis=-1, keepdims=True)
        y = y * jax.lax.rsqrt(var + EPS) * norm_w
        return jnp.einsum('bld,do->blo', y, W_out)

    def _L1_ffn_ref(hidden_states, gate_w, Wg, Wu, Wd, sWg, sWu, sWd):
        import jax, jax.numpy as jnp
        import numpy as np
        H = 256
        IM = 128
        E = 16
        K = 8
        N_SHARED = 2
        IS = IM * N_SHARED
        B, L = (1, 256)
        SCALE = 2.5
        W_INIT = 0.02
        orig_shape = hidden_states.shape
        h = hidden_states.reshape(-1, H)
        T = h.shape[0]
        shared = jax.nn.silu(h @ sWg) * (h @ sWu) @ sWd
        router_logits = h @ gate_w.T
        routing_weights = jax.nn.sigmoid(router_logits)
        topk_w, topk_idx = jax.lax.top_k(routing_weights, K)
        topk_w = topk_w / (jnp.sum(topk_w, axis=-1, keepdims=True) + 1e-06)
        topk_w = topk_w * SCALE
        comb = jnp.zeros((T, E), h.dtype).at[jnp.arange(T)[:, None], topk_idx].add(topk_w)
        g = jnp.einsum('th,ehi->eti', h, Wg)
        u = jnp.einsum('th,ehi->eti', h, Wu)
        eo = jnp.einsum('eti,eih->eth', jax.nn.silu(g) * u, Wd)
        routed = jnp.einsum('eth,te->th', eo, comb)
        return (shared + routed).reshape(orig_shape)
    x = L0_attn_x
    x = x + _layernorm(_L0_attn_ref(_layernorm(x, axis=-1), L0_attn_Wq, L0_attn_bq, L0_attn_Wk, L0_attn_bk, L0_attn_Wv, L0_attn_bv, L0_attn_Wo, L0_attn_bo), axis=-1)
    x = x + _layernorm(_L0_ffn_ref(_layernorm(x, axis=-1), L0_ffn_gate_w, L0_ffn_w1, L0_ffn_w2, L0_ffn_w3, L0_ffn_sw1, L0_ffn_sw2, L0_ffn_sw3), axis=-1)
    x = x + _layernorm(_L1_attn_ref(_layernorm(x, axis=-1), L1_attn_W_in, L1_attn_conv_w, L1_attn_conv_b, L1_attn_A_log, L1_attn_D_skip, L1_attn_dt_bias, L1_attn_norm_w, L1_attn_W_out), axis=-1)
    x = x + _layernorm(_L1_ffn_ref(_layernorm(x, axis=-1), L1_ffn_gate_w, L1_ffn_Wg, L1_ffn_Wu, L1_ffn_Wd, L1_ffn_sWg, L1_ffn_sWu, L1_ffn_sWd), axis=-1)
    return x

_drawn_inputs = setup_inputs


def setup_inputs(seed=0):
    import zlib

    import numpy as np

    out = dict(_drawn_inputs(seed))
    spreads = {'L0_attn_bq': (0.0, 0.796),
     'L0_attn_bk': (0.0, 0.8),
     'L0_attn_bv': (0.0, 0.1),
     'L0_attn_bo': (0.0, 0.1),
     'L1_attn_conv_b': (0.0, 0.1),
     'L1_attn_D_skip': (1.0, 0.2),
     'L1_attn_dt_bias': (1.0, 0.6),
     'L1_attn_norm_w': (1.0, 0.2)}
    factors = {'L0_attn_Wq': 2.759, 'L1_attn_A_log': 64.0}
    for name, (base, spread) in spreads.items():
        noise = np.random.default_rng([zlib.crc32(name.encode()), seed]).standard_normal(out[name].shape)
        drawn = base * np.exp(spread * noise) if base else spread * noise
        out[name] = jnp.asarray(drawn.astype(out[name].dtype))
    for name, factor in factors.items():
        out[name] = (out[name] * factor).astype(out[name].dtype)
    return out
```

```python
from contextlib import ExitStack

import numpy as np

import concourse.bass as bass
from concourse import mybir

F32 = mybir.dt.float32
BF16 = mybir.dt.bfloat16
U32 = mybir.dt.uint32
ALU = mybir.AluOpType
ACT = mybir.ActivationFunctionType
AX = mybir.AxisListType

P = 128
B, S, D = 16, 256, 256
TILES = B * S // P
SEQ_TILES = S // P
KD = D // P
E = 16
EPS = 1e-5
BANK = 512


class Chain:

    def __init__(self, eng, sem):
        self.eng, self.sem, self.count, self.turns = eng, sem, 0, 0

    def link(self, ins):
        ins.then_inc(self.sem, 1)
        self.count += 1
        self.eng.wait_ge(self.sem, self.count + self.turns)


def own_wait(k, eng):
    k.nc.vector.memset(k.spare[:], 0.0)


def begun(count):
    return not isinstance(count, int) or count > 0


def cols(tile, t, width=D):
    return tile[:, bass.ds(t * width, width)]


def go_through(layer, eng, step, chain=None, links=0):
    for s in layer.head():
        step(*s)
    before = chain.count if chain else 0
    with eng.Fori(0, layer.turns) as it:
        if chain:
            chain.turns = it * links
        for s in layer.pair(it):
            step(*s)
    if chain:
        assert chain.count - before == links, chain.count - before
        chain.turns, chain.count = 0, before + layer.turns * links
    for s in layer.rest():
        step(*s)


class Moe:
    turns = (TILES - 4) // 2
    """One mixture-of-experts layer: its shapes, buffers and semaphores.

    The shared part is cut into two more experts of the routed ones' width, whose weight is 1.
    `units` groups of experts go through the first product one at a time; what comes out,
    `chunks` pieces of 128 columns, goes in `groups` of four through a transpose and the second.
    """

    def __init__(self, k, name, inter, per_unit, top_k, softmax, scale, w_up, w_down, w_gate, loads):
        self.k, self.name, self.inter, self.per_unit, self.top_k = k, name, inter, per_unit, top_k
        self.softmax, self.scale = softmax, scale
        self.w_up, self.w_down, self.w_gate, self.loads = w_up, w_down, w_gate, loads
        self.finished = TILES
        self.units = (E + 2) // per_unit
        self.unit_w = inter * per_unit
        self.total = inter * (E + 2)
        self.chunks = -(-self.total // P)
        self.groups = -(-self.chunks // 4)
        self.last_unit = [(min((g + 1) * 4 * P, self.total) - 1) // self.unit_w for g in range(self.groups)]
        self.xn_ready = k.sem(name + "_xn_ready")
        self.xT_full = k.sem(name + "_xT_full")
        self.xT_ready = k.sem(name + "_xT_ready")
        self.var_ready = k.sem(name + "_var_ready")
        self.rstd_ready = k.sem(name + "_rstd_ready")
        self.logits_full = k.sem(name + "_logits_full")
        self.top_ready = k.sem(name + "_top_ready")
        self.exp_ready = k.sem(name + "_exp_ready")
        self.up_full = k.sem(name + "_up_full")
        self.silu_ready = k.sem(name + "_silu_ready")
        self.h_ready = k.sem(name + "_h_ready")
        self.hT_full = k.sem(name + "_hT_full")
        self.hT_ready = k.sem(name + "_hT_ready")
        self.down_done = k.sem(name + "_down_done")
        self.post_var = k.sem(name + "_post_var")
        self.post_rstd = k.sem(name + "_post_rstd")
        self.y_used = k.sem(name + "_y_used")
        self.x_done = k.sem(name + "_x_done")
        self.dve_step = k.sem(name + "_dve_step")

    def buffers(self, sb):
        n = self.name
        self.h = sb(n + "_h", [P, 2, self.chunks * P])
        self.hT = sb(n + "_hT", [P, 2, 4, P])
        self.silu = sb(n + "_silu", [P, 3, self.unit_w])
        self.xn = sb(n + "_xn", [P, D])
        self.xT = sb(n + "_xT", [P, 2, KD, P])
        self.comb = sb(n + "_comb", [P, 2, E + 2])
        self.stat = sb(n + "_stat", [P, 6])
        self.mv = sb(n + "_mv", [P, 2])
        self.rstd = sb(n + "_rstd", [P, 1])
        self.pstat = sb(n + "_pstat", [P, 6])
        self.pmv = sb(n + "_pmv", [P, 2])
        self.prstd = sb(n + "_prstd", [P, 1])
        self.z = sb(n + "_z", [P, D])
        self.exp = sb(n + "_exp", [P, E])
        self.score = sb(n + "_score", [P, E])
        self.top_neg = sb(n + "_top_neg", [P, 1])
        self.den = sb(n + "_den", [P, 1])
        self.rden = sb(n + "_rden", [P, 1])
        self.top = sb(n + "_top", [P, 8])
        self.topi = sb(n + "_topi", [P, 8], U32)
        self.topf = sb(n + "_topf", [P, 8])
        self.part = sb(n + "_part", [P, E])

    def pieces(self, g):
        return [(c, min(P, self.total - c * P)) for c in range(4 * g, min(4 * g + 4, self.chunks))]

    def tile(self, t, par, first, last):
        for u in range(self.units):
            yield "up", t, par, u
            if not last and u in (3, 5, 6, 7):
                yield {3: "norm", 5: "turn_x", 6: "logits", 7: "route"}[u], t + 1, 1 - par, 0
            for g, unit in enumerate(self.last_unit):
                for what, at in (("down", unit + 3), ("turn", unit + 2)):
                    if at == u:
                        yield what, t, par, g
                    if at == u + self.units and not first:
                        yield what, t - 1, 1 - par, g
            if u == 5 and not first:
                yield "post", t - 1, 1 - par, 0

    def head(self):
        yield from ((what, 0, 0, 0) for what in ("norm", "turn_x", "logits", "route"))
        yield from self.tile(0, 0, True, False)
        yield from self.tile(1, 1, False, False)

    def pair(self, it):
        yield from self.tile(2 * it + 2, 0, False, False)
        yield from self.tile(2 * it + 3, 1, False, False)

    def rest(self):
        t = TILES - 1
        yield from self.tile(t - 1, 0, False, False)
        yield from self.tile(t, 1, False, True)
        for at in range(self.units, self.units + 4):
            for g, unit in enumerate(self.last_unit):
                if unit + 3 == at:
                    yield "down", t, 1, g
                if unit + 2 == at:
                    yield "turn", t, 1, g
        yield "post", t, 1, 0


def moe_tensor(k, m, pe):
    U, G = m.units, m.groups
    nc = k.nc

    def step(what, t, par, i):
        n, g = t * U + i, t * G + i
        if what == "turn_x":
            pe.wait_ge(m.xn_ready, t + 1)
            if begun(t):
                pe.wait_ge(m.exp_ready, t)
            for c in range(KD):
                last = nc.tensor.transpose(k.bank[:, 7, c * P:(c + 1) * P], m.xn[:, c * P:(c + 1) * P], k.ident[:])
            last.then_inc(m.xT_full, 1)
        if what == "logits":
            pe.wait_ge(m.xT_ready, t + 1)
            for c in range(KD):
                last = nc.tensor.matmul(k.bank[:, 7, D:D + E], m.xT[:, par, c, :], m.w_gate[:, c, :],
                                        start=(c == 0), stop=(c == KD - 1))
            last.then_inc(m.logits_full, 1)
        if what == "up":
            pe.wait_ge(m.xT_ready, t + 1)
            if begun(n - 2):
                pe.wait_ge(m.h_ready, n - 2)
            W = 2 * m.unit_w
            for c in range(KD):
                last = nc.tensor.matmul(k.bank[:, i % 3, 0:W], m.xT[:, par, c, :], m.w_up[:, c, i * W:(i + 1) * W],
                                        start=(c == 0), stop=(c == KD - 1))
            last.then_inc(m.up_full, 1)
        if what == "turn":
            bank = 3 + (par * G + i) % 2
            pe.wait_ge(m.h_ready, t * U + m.last_unit[i] + 1)
            if begun(g - 1):
                pe.wait_ge(m.hT_ready, g - 1)
            for j, (c, w) in enumerate(m.pieces(i)):
                last = nc.tensor.transpose(k.bank[0:w, bank, j * P:(j + 1) * P], m.h[:, par, c * P:c * P + w], k.ident[:])
            last.then_inc(m.hT_full, 1)
        if what == "down":
            pe.wait_ge(m.hT_ready, g + 1)
            if i == 0:
                if begun(t - 1):
                    pe.wait_ge(m.y_used, t - 1)
            for j, (c, w) in enumerate(m.pieces(i)):
                last = nc.tensor.matmul(k.bank[:, 5 + par, 0:D], m.hT[0:w, (par * G + i) % 2, j, :],
                                        m.w_down[0:w, c, :], start=(c == 0), stop=(c == m.chunks - 1))
            last.then_inc(m.down_done, 1)

    for sem, count in m.loads:
        pe.wait_ge(sem, count)
    go_through(m, pe, step)


def moe_scalar(k, m, act):
    U, G = m.units, m.groups
    nc = k.nc

    def step(what, t, par, i):
        n, g = t * U + i, t * G + i
        if what == "turn_x":
            act.wait_ge(m.xT_full, t + 1)
            if begun((t - 1) * U):
                act.wait_ge(m.up_full, (t - 1) * U)
            nc.scalar.copy(m.xT[:, par, :, :].rearrange("p c t -> p (c t)"), k.bank[:, 7, 0:D]).then_inc(m.xT_ready, 1)
        if what == "route":
            if m.softmax:
                act.wait_ge(m.top_ready, t + 1)
                nc.scalar.activation(m.exp[:], k.bank[:, 7, D:D + E], ACT.Exp, bias=m.top_neg[:],
                                     accum_out=m.den[:]).then_inc(m.exp_ready, 1)
            else:
                act.wait_ge(m.logits_full, t + 1)
                nc.scalar.activation(m.exp[:], k.bank[:, 7, D:D + E], ACT.Exp, scale=-1.0).then_inc(m.exp_ready, 1)
        if what == "up":
            act.wait_ge(m.up_full, n + 1)
            if begun(n - 2):
                act.wait_ge(m.h_ready, n - 2)
            nc.scalar.activation(m.silu[:, i % 3, :], k.bank[:, i % 3, 0:m.unit_w], ACT.Silu).then_inc(m.silu_ready, 1)
        if what == "turn":
            act.wait_ge(m.hT_full, g + 1)
            if begun(g - 1):
                act.wait_ge(m.down_done, g - 1)
            w = max(w for _, w in m.pieces(i))
            full = len(m.pieces(i)) * P
            nc.scalar.copy(m.hT[0:w, (par * G + i) % 2, :, :].rearrange("p c t -> p (c t)")[:, 0:full],
                           k.bank[0:w, 3 + (par * G + i) % 2, 0:full]).then_inc(m.hT_ready, 1)

    go_through(m, act, step)


def moe_vector(k, m, dve):
    U, G = m.units, m.groups
    nc = k.nc
    chain = Chain(dve, m.dve_step)
    link = chain.link
    chain.link(nc.vector.memset(m.comb[:, :, E:E + 2], 1.0))

    def route(t, par):
        score, comb = m.score, m.comb[:, par, 0:E]
        logits = k.bank[:, 7, D:D + E]
        dve.wait_ge(m.logits_full, t + 1)
        if m.softmax:
            nc.vector.tensor_reduce(m.top_neg[:], logits, AX.X, ALU.max, negate=True).then_inc(m.top_ready, 1)
            dve.wait_ge(m.exp_ready, t + 1)
            link(nc.vector.reciprocal(m.rden[:], m.den[:]))
            link(nc.vector.tensor_scalar(score[:], m.exp[:], m.rden[:], None, ALU.mult))
            own_wait(k, dve)
            link(nc.vector.max(m.top[:], score[:]))
            own_wait(k, dve)
            link(nc.vector.max_index(m.topi[:], m.top[:], score[:]))
            link(nc.vector.tensor_copy(m.topf[:], m.topi[:]))
            link(nc.vector.tensor_scalar(m.part[:], k.expert_no[:], m.topf[:, 0:1], m.top[:, 0:1], ALU.is_equal, ALU.mult))
            link(nc.vector.tensor_scalar(comb, k.expert_no[:], m.topf[:, 1:2], m.top[:, 1:2], ALU.is_equal, ALU.mult))
            link(nc.vector.tensor_tensor(comb, comb, m.part[:], ALU.add))
        else:
            dve.wait_ge(m.exp_ready, t + 1)
            link(nc.vector.tensor_scalar(m.part[:], m.exp[:], 1.0, None, ALU.add))
            link(nc.vector.reciprocal(score[:], m.part[:]))
            own_wait(k, dve)
            link(nc.vector.max(m.top[:], score[:]))
            own_wait(k, dve)
            link(nc.vector.match_replace(m.part[:], m.top[:], score[:], 0.0))
            link(nc.vector.reduce_sum(m.den[:], m.top[:], AX.X))
            link(nc.vector.tensor_scalar(m.den[:], m.den[:], 1e-6, None, ALU.add))
            link(nc.vector.reciprocal(m.rden[:], m.den[:]))
            link(nc.vector.tensor_tensor(comb, score[:], m.part[:], ALU.subtract))
            link(nc.vector.tensor_scalar(comb, comb, m.rden[:], m.scale, ALU.mult, ALU.mult))

    def step(what, t, par, i):
        n = t * U + i
        if what == "norm":
            x = cols(k.x, t)
            link(nc.vector.bn_stats(m.stat[:], x))
            own_wait(k, dve)
            link(nc.vector.bn_aggr(m.mv[:], m.stat[:]))
            nc.vector.tensor_scalar(m.mv[:, 1:2], m.mv[:, 1:2], EPS, None, ALU.add).then_inc(m.var_ready, 1)
            dve.wait_ge(m.rstd_ready, t + 1)
            if begun(t):
                dve.wait_ge(m.xT_full, t)
            nc.vector.tensor_scalar(m.xn[:], x, m.mv[:, 0:1], m.rstd[:], ALU.subtract, ALU.mult).then_inc(m.xn_ready, 1)
        if what == "route":
            route(t, par)
        if what == "up":
            dve.wait_ge(m.silu_ready, n + 1)
            if i == 0:
                if begun((t - 1) * G):
                    dve.wait_ge(m.hT_full, (t - 1) * G)
            for e in range(m.per_unit):
                a, b = e * m.inter, m.unit_w + e * m.inter
                ex = i * m.per_unit + e
                last = nc.vector.scalar_tensor_tensor(
                    m.h[:, par, ex * m.inter:(ex + 1) * m.inter], m.silu[:, i % 3, a:a + m.inter],
                    m.comb[:, par, ex:ex + 1], k.bank[:, i % 3, b:b + m.inter], ALU.mult, ALU.mult)
            last.then_inc(m.h_ready, 1)
        if what == "post":
            y = k.bank[:, 5 + par, 0:D]
            dve.wait_ge(m.down_done, (t + 1) * G)
            link(nc.vector.bn_stats(m.pstat[:], y))
            own_wait(k, dve)
            link(nc.vector.bn_aggr(m.pmv[:], m.pstat[:]))
            nc.vector.tensor_scalar(m.pmv[:, 1:2], m.pmv[:, 1:2], EPS, None, ALU.add).then_inc(m.post_var, 1)
            dve.wait_ge(m.post_rstd, t + 1)
            nc.vector.tensor_scalar(m.z[:], y, m.pmv[:, 0:1], m.prstd[:], ALU.subtract, ALU.mult).then_inc(m.y_used, 1)
            dve.wait_ge(m.y_used, t + 1)
            x = cols(k.x, t)
            nc.vector.tensor_tensor(x, x, m.z[:], ALU.add).then_inc(m.x_done, 1)

    links = 2 * (2 + 2 + (8 if m.softmax else 9))
    go_through(m, dve, step, chain, links)
    dve.wait_ge(m.x_done, TILES)


def moe_pool(k, m, pool):
    def step(what, t, par, i):
        if what == "norm":
            pool.wait_ge(m.var_ready, t + 1)
            k.nc.gpsimd.tensor_tensor(m.rstd[:], m.mv[:, 1:2], k.minus_half[:, 0:1], ALU.pow).then_inc(m.rstd_ready, 1)
        if what == "post":
            pool.wait_ge(m.post_var, t + 1)
            k.nc.gpsimd.tensor_tensor(m.prstd[:], m.pmv[:, 1:2], k.minus_half[:, 0:1], ALU.pow).then_inc(m.post_rstd, 1)

    go_through(m, pool, step)


HEADS, KV = 16, 4
HD = D // HEADS
REP = HEADS // KV
SLOT = 32
NQ = HEADS * HD
NKV = KV * HD
NQK = NQ + NKV
NQKV = NQ + 2 * NKV
SCALE = float(HD) ** -0.5
MASKED = -1e30
OW = HD + 1


class Attention:

    def __init__(self, k, a):
        self.k, self.a = k, a
        self.loaded = k.sem("attn_loaded")
        self.tables = k.sem("attn_tables")
        self.tables_step = k.sem("attn_tables_step")
        self.var_ready = k.sem("attn_var_ready")
        self.rstd_ready = k.sem("attn_rstd_ready")
        self.xn_ready = k.sem("attn_xn_ready")
        self.xT_full = k.sem("attn_xT_full")
        self.xT_ready = k.sem("attn_xT_ready")
        self.qkv_full = k.sem("attn_qkv_full")
        self.qkv_read = k.sem("attn_qkv_read")
        self.rope_ready = k.sem("attn_rope_ready")
        self.qT_full = k.sem("attn_qT_full")
        self.qT_ready = k.sem("attn_qT_ready")
        self.kT_full = k.sem("attn_kT_full")
        self.kT_ready = k.sem("attn_kT_ready")
        self.scores_full = k.sem("attn_scores_full")
        self.max_ready = k.sem("attn_max_ready")
        self.qm_ready = k.sem("attn_qm_ready")
        self.qmT_full = k.sem("attn_qmT_full")
        self.qmT_ready = k.sem("attn_qmT_ready")
        self.probs_full = k.sem("attn_probs_full")
        self.probs_ready = k.sem("attn_probs_ready")
        self.probs_used = k.sem("attn_probs_used")
        self.att_ready = k.sem("attn_att_ready")
        self.attT_full = k.sem("attn_attT_full")
        self.attT_ready = k.sem("attn_attT_ready")
        self.proj_full = k.sem("attn_proj_full")
        self.post_var = k.sem("attn_post_var")
        self.post_rstd = k.sem("attn_post_rstd")
        self.proj_used = k.sem("attn_proj_used")
        self.x_done = k.sem("attn_x_done")
        self.dve_step = k.sem("attn_dve_step")

    def weights(self, sb):
        self.w_qkv = sb("w_qkv", [P, KD, NQKV])
        self.b_qkv = sb("b_qkv", [P, NQKV])
        self.w_o = sb("w_o", [P, KD, D])
        self.b_o = sb("b_o", [P, D])
        self.cos = sb("cos", [P, SEQ_TILES, HD])
        self.sin = sb("sin", [P, SEQ_TILES, 2, HD // 2])

    def buffers(self, sb):
        self.mask_q = sb("mask_q", [P, REP, P], BF16)
        self.mask_k = sb("mask_k", [P, REP, P], BF16)
        self.stat = sb("attn_stat", [P, SEQ_TILES, 6])
        self.mv = sb("attn_mv", [P, SEQ_TILES, 2])
        self.rstd = sb("attn_rstd", [P, SEQ_TILES])
        self.pstat = sb("attn_pstat", [P, SEQ_TILES, 6])
        self.pmv = sb("attn_pmv", [P, SEQ_TILES, 2])
        self.prstd = sb("attn_prstd", [P, SEQ_TILES])
        self.xn = sb("attn_xn", [P, SEQ_TILES, D])
        self.xT = sb("attn_xT", [P, KD, S])
        self.qkv = sb("attn_qkv", [P, SEQ_TILES, NQKV])
        self.rot_a = sb("rot_a", [P, NQK])
        self.rot_b = sb("rot_b", [P, NQK])
        self.q = sb("q_slots", [P, 2, SEQ_TILES, REP, KV, SLOT])
        self.kk = sb("k_slots", [P, SEQ_TILES, KV, SLOT])
        self.v = sb("v_slots", [P, 2, SEQ_TILES, KV, OW])
        self.qT = sb("qT", [P, 2, SEQ_TILES, REP, P])
        self.kT = sb("kT", [P, 2, S])
        self.qmT = sb("qmT", [P, SEQ_TILES, REP, P])
        self.probs = sb("probs", [P, 2, SEQ_TILES, REP, P])
        self.rden = sb("rden", [P, SEQ_TILES, HEADS])
        self.att = sb("att", [P, SEQ_TILES, D])
        self.attT = sb("attT", [P, KD, S])
        self.y = sb("attn_y", [P, SEQ_TILES, D])
        self.z = sb("attn_z", [P, SEQ_TILES, D])

    def load(self, sp):
        a = self.a
        for dst, src in ((self.w_qkv[:], a["w_qkv"].rearrange("c p n -> p c n")), (self.b_qkv[:], a["b_qkv"]),
                         (self.w_o[:], a["w_o"].rearrange("c p n -> p c n")), (self.b_o[:], a["b_o"]),
                         (self.cos[:], a["cos"]), (self.sin[:], a["sin"])):
            sp.dma_start(dst, src).then_inc(self.loaded, 16)

    LOADS = 6 * 16


def attention_layout(i):
    def rows(v):
        return np.broadcast_to(v, (P, v.shape[0]))

    w = np.concatenate([i["L0_attn_Wq"], i["L0_attn_Wk"], i["L0_attn_Wv"]]).T
    b = np.concatenate([i["L0_attn_bq"], i["L0_attn_bk"], i["L0_attn_bv"]])
    inv = (np.float32(1.0) / np.float32(10000.0) ** (np.arange(0, HD, 2, dtype=np.float32) / np.float32(HD)))
    freqs = np.arange(S, dtype=np.float32)[:, None] * inv.astype(np.float32)[None, :]
    cos = np.repeat(np.cos(freqs), 2, axis=-1).reshape(SEQ_TILES, P, HD).transpose(1, 0, 2)
    sin = np.sin(freqs).reshape(SEQ_TILES, P, HD // 2).transpose(1, 0, 2)
    return {
        "w_qkv": w.reshape(KD, P, NQKV), "b_qkv": rows(b),
        "w_o": i["L0_attn_Wo"].T.reshape(KD, P, D), "b_o": rows(i["L0_attn_bo"]),
        "cos": cos.astype(np.float32), "sin": np.stack([-sin, sin], axis=2).astype(np.float32),
    }


SEQS = B
UNITS = SEQ_TILES * KV


def attention_order(t, par, first, last):
    before, after = (t - 1, 1 - par), (t + 1, 1 - par)

    def of(which, *steps):
        for what, i in steps:
            yield what, which[0], which[1], i

    here = (t, par)
    yield from of(here, ("scores", 0), ("scores", 1))
    if not first:
        yield from of(before, ("att", 0))
    yield from of(here, ("scores", 2))
    if not first:
        yield from of(before, ("turn_att", 0))
    yield from of(here, ("scores", 3))
    if not last:
        yield from of(after, ("norm", 0))
    if not first:
        yield from of(before, ("proj", 0))
    yield from of(here, ("scores", 4), ("scores", 5), ("turn_m", 0))
    if not first:
        yield from of(before, ("post", 0))
    if not last:
        yield from of(after, ("turn_x", 0))
    yield from of(here, ("scores", 6), ("scores", 7))
    if not last:
        yield from of(after, ("qkv", 0))
    yield from of(here, ("probs", 0))
    if not last:
        yield from of(after, ("rope", 0))
    yield from of(here, ("probs", 1), ("av", 0), ("turn_m", 1), ("probs", 2), ("av", 1))
    if not last:
        yield from of(after, ("qkv", 1))
    yield from of(here, ("probs", 3), ("av", 2))
    if not last:
        yield from of(after, ("rope", 1), ("turn_q", 0))
    yield from of(here, ("probs", 4), ("av", 3))
    if not last:
        yield from of(after, ("turn_q", 1))
    yield from of(here, ("probs", 5), ("av", 4))
    if not last:
        yield from of(after, ("turn_k", 0))
    yield from of(here, ("probs", 6), ("av", 5), ("probs", 7), ("av", 6), ("av", 7))


def attention_head(self):
    for what, i in (("norm", 0), ("turn_x", 0), ("qkv", 0), ("rope", 0), ("qkv", 1), ("rope", 1),
                    ("turn_q", 0), ("turn_q", 1), ("turn_k", 0)):
        yield what, 0, 0, i
    yield from attention_order(0, 0, True, False)
    yield from attention_order(1, 1, False, False)


def attention_pair(self, it):
    yield from attention_order(2 * it + 2, 0, False, False)
    yield from attention_order(2 * it + 3, 1, False, False)


def attention_rest(self):
    yield from attention_order(SEQS - 2, 0, False, False)
    yield from attention_order(SEQS - 1, 1, False, True)
    for what in ("att", "turn_att", "proj", "post"):
        yield what, SEQS - 1, 1, 0


Attention.head, Attention.pair, Attention.rest = attention_head, attention_pair, attention_rest
Attention.turns = (SEQS - 4) // 2
Attention.finished = SEQS


def is_last(t, n):
    return isinstance(t, int) and t == n - 1


def attention_tensor(k, m, pe):
    nc = k.nc

    def step(what, t, par, i):
        qb, g = divmod(i, KV)
        rows = slice(SLOT * g, SLOT * g + HD)
        rows_m = slice(SLOT * g, SLOT * g + HD + 1)
        pair = 2 * (i % 2)
        if what == "turn_x":
            pe.wait_ge(m.xn_ready, t + 1)
            if begun(t - 1):
                pe.wait_ge(m.attT_ready, t - 1)
            for c in range(KD):
                for j in range(SEQ_TILES):
                    last = nc.tensor.transpose(k.bank[:, 6, (c * SEQ_TILES + j) * P:(c * SEQ_TILES + j + 1) * P],
                                               m.xn[:, j, c * P:(c + 1) * P], k.ident[:])
            last.then_inc(m.xT_full, 1)
        if what == "qkv":
            pe.wait_ge(m.xT_ready, t + 1)
            if begun(2 * t + i):
                pe.wait_ge(m.qkv_read, 2 * t + i)
            for c in range(KD):
                last = nc.tensor.matmul(k.bank[:, 6, 0:NQKV], m.xT[:, c, i * P:(i + 1) * P], m.w_qkv[:, c, :],
                                        start=(c == 0), stop=(c == KD - 1))
            last.then_inc(m.qkv_full, 1)
        if what == "turn_q":
            pe.wait_ge(m.rope_ready, 2 * t + i + 1)
            if i == 0:
                if begun(2 * t):
                    pe.wait_ge(m.qmT_ready, 2 * t)
            else:
                pe.wait_ge(m.qkv_read, 2 * t + 2)
            for r in range(REP):
                last = nc.tensor.transpose(k.bank[:, 7 - i, r * P:(r + 1) * P],
                                           m.q[:, par, i, r].rearrange("p g s -> p (g s)"), k.ident[:])
            last.then_inc(m.qT_full, 1)
        if what == "turn_k":
            pe.wait_ge(m.rope_ready, 2 * t + 2)
            pe.wait_ge(m.qT_ready, 2 * t + 1)
            for j in range(SEQ_TILES):
                last = nc.tensor.transpose(k.bank[:, 7, j * P:(j + 1) * P],
                                           m.kk[:, j].rearrange("p g s -> p (g s)"), k.ident[:])
            last.then_inc(m.kT_full, 1)
        if what == "scores":
            pe.wait_ge(m.qT_ready, 2 * t + qb + 1)
            pe.wait_ge(m.kT_ready, t + 1)
            if i < 2:
                if begun(UNITS * t + i - 1):
                    pe.wait_ge(m.probs_ready, UNITS * t + i - 1)
            else:
                if begun(UNITS * t + i - 1):
                    pe.wait_ge(m.max_ready, UNITS * t + i - 1)
            keys = (qb + 1) * P
            for half in range(qb + 1):
                per = REP // (qb + 1)
                to = k.bank[:, pair + half, :].rearrange("p (r n) -> p r n", r=per)
                nc.tensor.matmul(to[:, :, keys - P:keys], k.ident_b[:], m.mask_q[:, 0:per, :], start=True, stop=False,
                                 skip_group_check=True)
                for r in range(per):
                    last = nc.tensor.matmul(to[:, r, :], m.qT[rows, par, qb, half * per + r, :],
                                            m.kT[rows, par, 0:keys], start=False, stop=(r == per - 1),
                                            skip_group_check=True)
            last.then_inc(m.scores_full, 1)
        if what == "turn_m":
            pe.wait_ge(m.max_ready, UNITS * t + KV * (i + 1))
            if i == 0:
                if begun(t):
                    pe.wait_ge(m.proj_used, t)
            else:
                pe.wait_ge(m.qmT_ready, 2 * t + 1)
            for r in range(REP):
                last = nc.tensor.transpose(k.bank[:, 7, r * P:(r + 1) * P],
                                           m.q[:, par, i, r].rearrange("p g s -> p (g s)"), k.ident[:])
            last.then_inc(m.qmT_full, 1)
        if what == "probs":
            pe.wait_ge(m.qmT_ready, 2 * t + qb + 1)
            if i < 2:
                if begun(UNITS * t + UNITS - 1 + i):
                    pe.wait_ge(m.max_ready, UNITS * t + UNITS - 1 + i)
            else:
                if begun(UNITS * t + i - 1):
                    pe.wait_ge(m.probs_ready, UNITS * t + i - 1)
            for kb in range(qb + 1):
                to = k.bank[:, pair + kb, :]
                if kb == qb:
                    nc.tensor.matmul(to, k.ident_b[:], m.mask_k[:].rearrange("p r n -> p (r n)"), start=True, stop=False,
                                     skip_group_check=True)
                last = nc.tensor.matmul(to, m.kT[rows_m, par, kb * P:(kb + 1) * P],
                                        m.qmT[rows_m, qb].rearrange("p r n -> p (r n)"), start=(kb != qb), stop=True,
                                        skip_group_check=True)
            last.then_inc(m.probs_full, 1)
        if what == "av":
            pe.wait_ge(m.probs_ready, UNITS * t + i + 1)
            if g == 0:
                if begun(t):
                    pe.wait_ge(m.att_ready, t)
            for r in range(REP):
                h = g * REP + r
                for kb in range(qb + 1):
                    last = nc.tensor.matmul(k.bank[:, 4 + qb, h * OW:(h + 1) * OW], m.probs[:, i % 2, kb, r, :],
                                            m.v[:, par, kb, g, :], start=(kb == 0), stop=(kb == qb))
            last.then_inc(m.probs_used, 1)
        if what == "turn_att":
            pe.wait_ge(m.att_ready, t + 1)
            if is_last(t, SEQS):
                if begun(t):
                    pe.wait_ge(m.attT_ready, t)
            else:
                pe.wait_ge(m.qT_ready, 2 * t + 4)
            for c in range(KD):
                for j in range(SEQ_TILES):
                    last = nc.tensor.transpose(k.bank[:, 6, (c * SEQ_TILES + j) * P:(c * SEQ_TILES + j + 1) * P],
                                               m.att[:, j, c * P:(c + 1) * P], k.ident[:])
            last.then_inc(m.attT_full, 1)
        if what == "proj":
            pe.wait_ge(m.attT_ready, t + 1)
            if is_last(t, SEQS):
                pe.wait_ge(m.qmT_ready, 2 * t + 2)
            else:
                pe.wait_ge(m.kT_ready, t + 2)
            for j in range(SEQ_TILES):
                for c in range(KD):
                    last = nc.tensor.matmul(k.bank[:, 7, j * D:(j + 1) * D], m.attT[:, c, j * P:(j + 1) * P],
                                            m.w_o[:, c, :], start=(c == 0), stop=(c == KD - 1))
            last.then_inc(m.proj_full, 1)

    pe.wait_ge(m.loaded, m.LOADS)
    pe.wait_ge(m.tables, 4)
    go_through(m, pe, step)


def attention_scalar(k, m, act):
    nc = k.nc

    def step(what, t, par, i):
        qb = i // KV
        if what == "turn_x":
            act.wait_ge(m.xT_full, t + 1)
            if begun(2 * t):
                act.wait_ge(m.qkv_full, 2 * t)
            nc.scalar.copy(m.xT[:].rearrange("p c t -> p (c t)"), k.bank[:, 6, :]).then_inc(m.xT_ready, 1)
        if what == "turn_q":
            act.wait_ge(m.qT_full, 2 * t + i + 1)
            if begun(UNITS * (t - 1)):
                act.wait_ge(m.scores_full, UNITS * (t - 1))
            nc.scalar.copy(m.qT[:, par, i].rearrange("p r n -> p (r n)"), k.bank[:, 7 - i, :]).then_inc(m.qT_ready, 1)
        if what == "turn_k":
            act.wait_ge(m.kT_full, t + 1)
            if begun(UNITS * (t - 1)):
                act.wait_ge(m.probs_full, UNITS * (t - 1))
            nc.scalar.copy(m.kT[:, par, :], k.bank[:, 7, 0:S]).then_inc(m.kT_ready, 1)
        if what == "turn_m":
            act.wait_ge(m.qmT_full, 2 * t + i + 1)
            if begun(UNITS * t):
                act.wait_ge(m.probs_full, UNITS * t)
            nc.scalar.copy(m.qmT[:, i].rearrange("p r n -> p (r n)"), k.bank[:, 7, :]).then_inc(m.qmT_ready, 1)
        if what == "probs":
            n = UNITS * t + i
            act.wait_ge(m.probs_full, n + 1)
            if begun(n - 1):
                act.wait_ge(m.probs_used, n - 1)
            nc.scalar.activation(m.probs[:, i % 2, 0:qb + 1].rearrange("p b r n -> p (b r n)"),
                                 k.bank[:, 2 * (i % 2):2 * (i % 2) + qb + 1, :].rearrange("p b n -> p (b n)"),
                                 ACT.Exp, scale=SCALE).then_inc(m.probs_ready, 1)
        if what == "turn_att":
            act.wait_ge(m.attT_full, t + 1)
            if begun(t):
                act.wait_ge(m.proj_full, t)
            nc.scalar.copy(m.attT[:].rearrange("p c t -> p (c t)"), k.bank[:, 6, :]).then_inc(m.attT_ready, 1)

    go_through(m, act, step)


def attention_vector(k, m, dve):
    nc = k.nc
    v = nc.vector
    chain = Chain(dve, m.dve_step)
    link = chain.link

    def step(what, t, par, i):
        qb, g = divmod(i, KV)
        if what == "norm":
            for j in range(SEQ_TILES):
                last = v.bn_stats(m.stat[:, j, :], cols(k.x, SEQ_TILES * t + j))
            link(last)
            own_wait(k, dve)
            for j in range(SEQ_TILES):
                last = v.bn_aggr(m.mv[:, j, :], m.stat[:, j, :])
            link(last)
            v.tensor_scalar(m.mv[:, :, 1], m.mv[:, :, 1], EPS, None, ALU.add).then_inc(m.var_ready, 1)
            dve.wait_ge(m.rstd_ready, t + 1)
            if begun(t):
                dve.wait_ge(m.xT_full, t)
            for j in range(SEQ_TILES):
                last = v.tensor_scalar(m.xn[:, j, :], cols(k.x, SEQ_TILES * t + j), m.mv[:, j, 0:1], m.rstd[:, j:j + 1],
                                       ALU.subtract, ALU.mult)
            last.then_inc(m.xn_ready, 1)
        if what == "rope":
            dve.wait_ge(m.qkv_full, 2 * t + i + 1)
            v.tensor_tensor(m.qkv[:, i, :], k.bank[:, 6, 0:NQKV], m.b_qkv[:], ALU.add).then_inc(m.qkv_read, 1)
            dve.wait_ge(m.qkv_read, 2 * t + i + 1)
            N = NQK // HD
            qk = m.qkv[:, i, 0:NQK]
            pairs = qk.rearrange("p (h f two) -> p h f two", h=N, two=2)
            rot_b = m.rot_b[:].rearrange("p (h f two) -> p h f two", h=N, two=2)
            v.tensor_tensor(m.rot_a[:].rearrange("p (h f) -> p h f", h=N), qk.rearrange("p (h f) -> p h f", h=N),
                            m.cos[:, i:i + 1, :].to_broadcast([P, N, HD]), ALU.mult)
            v.tensor_tensor(rot_b[:, :, :, 0], pairs[:, :, :, 1],
                            m.sin[:, i, 0:1, :].to_broadcast([P, N, HD // 2]), ALU.mult)
            link(v.tensor_tensor(rot_b[:, :, :, 1], pairs[:, :, :, 0],
                                 m.sin[:, i, 1:2, :].to_broadcast([P, N, HD // 2]), ALU.mult))
            if begun(2 * (t - 1)):
                dve.wait_ge(m.qmT_full, 2 * (t - 1))
            if begun(t):
                dve.wait_ge(m.kT_full, t)
            if begun(UNITS * (t - 1)):
                dve.wait_ge(m.probs_used, UNITS * (t - 1))
            for g in range(KV):
                sl = slice(g * REP * HD, (g + 1) * REP * HD)
                v.tensor_tensor(m.q[:, par, i, :, g, 0:HD], m.rot_a[:, sl].rearrange("p (r f) -> p r f", r=REP),
                                m.rot_b[:, sl].rearrange("p (r f) -> p r f", r=REP), ALU.add)
            v.tensor_tensor(m.kk[:, i, :, 0:HD], m.rot_a[:, NQ:NQK].rearrange("p (g f) -> p g f", g=KV),
                            m.rot_b[:, NQ:NQK].rearrange("p (g f) -> p g f", g=KV), ALU.add)
            v.tensor_copy(m.v[:, par, i, :, 0:HD], m.qkv[:, i, NQK:NQKV].rearrange("p (g f) -> p g f", g=KV))\
                .then_inc(m.rope_ready, 1)
        if what == "scores":
            dve.wait_ge(m.scores_full, UNITS * t + i + 1)
            pair = 2 * (i % 2)
            v.tensor_reduce(m.q[:, par, qb, :, g, HD],
                            k.bank[:, pair:pair + qb + 1, :].rearrange("p b (r n) -> p (b r) n", n=(qb + 1) * P),
                            AX.X, ALU.max, negate=True).then_inc(m.max_ready, 1)
        if what == "att":
            dve.wait_ge(m.probs_used, UNITS * (t + 1))
            outs = [k.bank[:, 4 + j, 0:HEADS * OW].rearrange("p (h w) -> p h w", w=OW) for j in range(SEQ_TILES)]
            for j in range(SEQ_TILES):
                last = v.reciprocal(m.rden[:, j, :], outs[j][:, :, HD])
            link(last)
            if begun(t):
                dve.wait_ge(m.attT_full, t)
            for j in range(SEQ_TILES):
                last = v.tensor_tensor(m.att[:, j, :].rearrange("p (h f) -> p h f", h=HEADS), outs[j][:, :, 0:HD],
                                       m.rden[:, j, :].unsqueeze(2).to_broadcast([P, HEADS, HD]), ALU.mult)
            last.then_inc(m.att_ready, 1)
        if what == "post":
            dve.wait_ge(m.proj_full, t + 1)
            v.tensor_tensor(m.y[:], k.bank[:, 7, :].rearrange("p (j d) -> p j d", j=SEQ_TILES),
                            m.b_o[:].unsqueeze(1).to_broadcast([P, SEQ_TILES, D]), ALU.add).then_inc(m.proj_used, 1)
            dve.wait_ge(m.proj_used, t + 1)
            for j in range(SEQ_TILES):
                last = v.bn_stats(m.pstat[:, j, :], m.y[:, j, :])
            link(last)
            own_wait(k, dve)
            for j in range(SEQ_TILES):
                last = v.bn_aggr(m.pmv[:, j, :], m.pstat[:, j, :])
            link(last)
            v.tensor_scalar(m.pmv[:, :, 1], m.pmv[:, :, 1], EPS, None, ALU.add).then_inc(m.post_var, 1)
            dve.wait_ge(m.post_rstd, t + 1)
            for j in range(SEQ_TILES):
                last = v.tensor_scalar(m.z[:, j, :], m.y[:, j, :], m.pmv[:, j, 0:1], m.prstd[:, j:j + 1],
                                       ALU.subtract, ALU.mult)
            link(last)
            x = cols(k.x, t, SEQ_TILES * D)
            v.tensor_tensor(x, x, m.z[:].rearrange("p j d -> p (j d)"), ALU.add).then_inc(m.x_done, 1)

    v.memset(m.q[:, :, :, :, :, HD:SLOT], 0.0)
    v.memset(m.kk[:, :, :, HD:SLOT], 0.0)
    link(v.memset(m.v[:, :, :, :, HD:OW], 1.0))
    link(v.memset(m.kk[:, :, :, HD:HD + 1], 1.0))
    dve.wait_ge(m.loaded, m.LOADS)
    go_through(m, dve, step, chain, 2 * (2 + 2 * 1 + 1 + 3))
    dve.wait_ge(m.x_done, m.finished)


def attention_pool(k, m, pool):
    g = k.nc.gpsimd
    g.memset(m.mask_q[:], 0.0)
    g.memset(m.mask_k[:], 0.0).then_inc(m.tables_step, 1)
    pool.wait_ge(m.tables_step, 1)
    g.affine_select(out=m.mask_q[:], in_=m.mask_q[:], compare_op=ALU.is_ge, fill=MASKED, base=0,
                    pattern=[[0, REP], [-1, P]], channel_multiplier=1).then_inc(m.tables, 2)
    g.affine_select(out=m.mask_k[:], in_=m.mask_k[:], compare_op=ALU.is_ge, fill=MASKED, base=0,
                    pattern=[[0, REP], [1, P]], channel_multiplier=-1).then_inc(m.tables, 2)

    def step(what, t, par, i):
        if what == "norm":
            pool.wait_ge(m.var_ready, t + 1)
            g.tensor_tensor(m.rstd[:], m.mv[:, :, 1], k.minus_half[:, 0:SEQ_TILES], ALU.pow).then_inc(m.rstd_ready, 1)
        if what == "post":
            pool.wait_ge(m.post_var, t + 1)
            g.tensor_tensor(m.prstd[:], m.pmv[:, :, 1], k.minus_half[:, 0:SEQ_TILES], ALU.pow).then_inc(m.post_rstd, 1)

    go_through(m, pool, step)


INNER = 512
STATE = 16
SH = 8
SHD = INNER // SH
TAPS = 4
FT = INNER // P
C_ROW = 32
BC = C_ROW + STATE
SEG = S + P
PARTS = 3
DOWN = 2.0 ** -20


class Ssm:

    def __init__(self, k, a):
        self.k, self.a = k, a
        self.finished = SEQS
        self.turns = (SEQS - 4) // 2
        self.loaded = k.sem("ssm_loaded")
        self.tables = k.sem("ssm_tables")
        self.tables_step = k.sem("ssm_tables_step")
        self.var_ready = k.sem("ssm_var_ready")
        self.rstd_ready = k.sem("ssm_rstd_ready")
        self.xn_ready = k.sem("ssm_xn_ready")
        self.xT_full = k.sem("ssm_xT_full")
        self.xT_ready = k.sem("ssm_xT_ready")
        self.feat_full = k.sem("ssm_feat_full")
        self.feat_ready = k.sem("ssm_feat_ready")
        self.gate_full = k.sem("ssm_gate_full")
        self.dAT_full = k.sem("ssm_dAT_full")
        self.xtok_full = k.sem("ssm_xtok_full")
        self.y2T_full = k.sem("ssm_y2T_full")
        self.out_full = k.sem("ssm_out_full")
        self.out_read = k.sem("ssm_out_read")
        self.dt_read = k.sem("ssm_dt_read")
        self.conv_ready = k.sem("ssm_conv_ready")
        self.silu_ready = k.sem("ssm_silu_ready")
        self.bc_ready = k.sem("ssm_bc_ready")
        self.gate_ready = k.sem("ssm_gate_ready")
        self.xtok_ready = k.sem("ssm_xtok_ready")
        self.xdt_ready = k.sem("ssm_xdt_ready")
        self.xd_ready = k.sem("ssm_xd_ready")
        self.min_ready = k.sem("ssm_min_ready")
        self.e_ready = k.sem("ssm_e_ready")
        self.w_ready = k.sem("ssm_w_ready")
        self.ln_ready = k.sem("ssm_ln_ready")
        self.da_ready = k.sem("ssm_da_ready")
        self.decay_ready = k.sem("ssm_decay_ready")
        self.parts_ready = k.sem("ssm_parts_ready")
        self.dAT_ready = k.sem("ssm_dAT_ready")
        self.dab_full = k.sem("ssm_dab_full")
        self.scan_done = k.sem("ssm_scan_done")
        self.g_full = k.sem("ssm_g_full")
        self.weight_done = k.sem("ssm_weight_done")
        self.y_full = k.sem("ssm_y_full")
        self.y_read = k.sem("ssm_y_read")
        self.yg_ready = k.sem("ssm_yg_ready")
        self.square_ready = k.sem("ssm_square_ready")
        self.rms_ready = k.sem("ssm_rms_ready")
        self.y2_ready = k.sem("ssm_y2_ready")
        self.y2T_ready = k.sem("ssm_y2T_ready")
        self.post_var = k.sem("ssm_post_var")
        self.post_rstd = k.sem("ssm_post_rstd")
        self.x_done = k.sem("ssm_x_done")
        self.dve_step = k.sem("ssm_dve_step")
        self.ms_ready = k.sem("ssm_ms_ready")
        self.log_ready = k.sem("ssm_log_ready")

    def weights(self, sb):
        self.w_x = sb("w_x", [P, KD, INNER])
        self.w_bc = sb("w_bc", [P, KD, BC])
        self.w_g = sb("w_g", [P, KD, INNER])
        self.w_dt = sb("w_dt", [P, KD, SH])
        self.w_out = sb("w_out", [P, FT, D])
        self.taps = sb("taps", [P, FT, TAPS + 1])
        self.taps_bc = sb("taps_bc", [BC, TAPS + 1])
        self.a_log = sb("a_log", [P, SH])
        self.skip = sb("skip", [P, INNER])
        self.dt_bias = sb("dt_bias", [P, SH])
        self.norm_w = sb("norm_w", [P, INNER])
        self.sel = sb("sel", [PARTS * SH, SH, P], BF16)

    def load(self, sp):
        a = self.a
        for dst, src in ((self.w_x, a["w_x"].rearrange("c p n -> p c n")), (self.w_bc, a["w_bc"].rearrange("c p n -> p c n")),
                         (self.w_g, a["w_g"].rearrange("c p n -> p c n")), (self.w_dt, a["w_dt"].rearrange("c p n -> p c n")),
                         (self.w_out, a["w_out"].rearrange("c p n -> p c n")), (self.taps, a["taps"]),
                         (self.taps_bc, a["taps_bc"]), (self.a_log, a["a_log"]), (self.skip, a["skip"]),
                         (self.dt_bias, a["dt_bias"]), (self.norm_w, a["norm_w"])):
            sp.dma_start(dst[:], src).then_inc(self.loaded, 16)

    LOADS = 11 * 16

    def buffers(self, sb):
        self.neg_a = sb("neg_a", [P, SH])
        self.a_lim = sb("a_lim", [P, SH])
        self.pos_a = sb("pos_a", [P, SH])
        self.delta = sb("delta", [P, S])
        self.stat = sb("ssm_stat", [P, SEQ_TILES, 6])
        self.mv = sb("ssm_mv", [P, SEQ_TILES, 2])
        self.rstd = sb("ssm_rstd", [P, SEQ_TILES])
        self.pstat = sb("ssm_pstat", [P, SEQ_TILES, 6])
        self.pmv = sb("ssm_pmv", [P, SEQ_TILES, 2])
        self.prstd = sb("ssm_prstd", [P, SEQ_TILES])
        self.xn = sb("ssm_xn", [P, SEQ_TILES, D])
        self.xT = sb("ssm_xT", [P, KD, S])
        self.feat = sb("feat", [P, FT, TAPS - 1 + S])
        self.feat_bc = sb("feat_bc", [BC, TAPS - 1 + S])
        self.conv = sb("conv", [P, FT, S])
        self.conv_bc = sb("conv_bc", [BC, S])
        self.bT = sb("bT", [STATE, 2, S])
        self.cT = sb("cT", [STATE, 2, S])
        self.gate = sb("gate", [P, 2, SEQ_TILES, INNER])
        self.xtok = sb("xtok", [P, SEQ_TILES, INNER])
        self.xdt = sb("xdt", [P, 2, SEQ_TILES, INNER])
        self.xd = sb("xd", [P, 2, SEQ_TILES, INNER])
        self.s_u = sb("s_u", [P, SEQ_TILES, SH])
        self.s_mn = sb("s_mn", [P, SEQ_TILES, SH])
        self.s_e = sb("s_e", [P, SEQ_TILES, SH])
        self.s_w = sb("s_w", [P, SEQ_TILES, SH])
        self.s_ln = sb("s_ln", [P, SEQ_TILES, SH])
        self.s_eq = sb("s_eq", [P, SEQ_TILES, SH])
        self.s_num = sb("s_num", [P, SEQ_TILES, SH])
        self.s_den = sb("s_den", [P, SEQ_TILES, SH])
        self.s_dt = sb("s_dt", [P, SEQ_TILES, SH])
        self.s_da = sb("s_da", [P, SEQ_TILES, SH])
        self.s_decay = sb("s_decay", [P, SEQ_TILES, SH])
        self.s_rest = sb("s_rest", [P, SEQ_TILES, SH])
        self.parts = sb("parts", [P, SEQ_TILES, PARTS, SH], BF16)
        self.dAT = sb("dAT", [PARTS * SH, 2, S], BF16)
        self.m = sb("m", [P, SH, SEG])
        self.yg = sb("yg", [P, SEQ_TILES, INNER])
        self.square = sb("square", [P, SEQ_TILES, INNER], BF16)
        self.sum2 = sb("sum2", [P, SEQ_TILES])
        self.ms = sb("ms", [P, SEQ_TILES])
        self.rms = sb("rms", [P, SEQ_TILES])
        self.y2T = sb("y2T", [P, SEQ_TILES, FT, P])
        self.z = sb("ssm_z", [P, SEQ_TILES, D])

    def order(self, t, par, first, last):
        n, npar = t + 1, 1 - par

        def here(what, i=0):
            return what, t, par, i

        def ahead(*steps):
            return [] if last else [(what, n, npar, i) for what, i in steps]

        yield here("dab", 0)
        yield here("dab", 1)
        yield here("gmat")
        yield here("dab", 2)
        yield from ahead(("norm", 0))
        yield here("weight", 0)
        yield here("ymm", 0)
        yield from ahead(("turn_x", 0), ("feat", 0), ("feat", 1), ("bcdt", 0))
        yield here("dab", 3)
        yield from ahead(("dt", 0), ("gate", 0), ("gate", 1))
        yield here("weight", 1)
        yield here("ymm", 1)
        yield from ahead(("conv", 0), ("conv", 1))
        yield here("gating")
        yield from ahead(("conv", 2), ("conv", 3))
        yield here("scale")
        yield here("turn_y", 0)
        yield here("turn_y", 1)
        yield from ahead(("turn_dA", 0), ("silu", 0), ("turn_c", 0), ("turn_c", 1))
        yield here("out")
        yield from ahead(("xdt", 0))
        yield here("post")

    def head(self):
        for what, i in (("norm", 0), ("turn_x", 0), ("feat", 0), ("feat", 1), ("bcdt", 0), ("dt", 0), ("gate", 0),
                        ("gate", 1), ("conv", 0), ("conv", 1), ("conv", 2), ("conv", 3), ("turn_dA", 0), ("silu", 0),
                        ("turn_c", 0), ("turn_c", 1), ("xdt", 0)):
            yield what, 0, 0, i
        yield from self.order(0, 0, True, False)
        yield from self.order(1, 1, False, False)

    def pair(self, it):
        yield from self.order(2 * it + 2, 0, False, False)
        yield from self.order(2 * it + 3, 1, False, False)

    def rest(self):
        yield from self.order(SEQS - 2, 0, False, False)
        yield from self.order(SEQS - 1, 1, False, True)


def ssm_layout(i):
    w = i["L1_attn_W_in"]
    o = 2 * INNER
    w_bc = np.zeros((D, BC), w.dtype)
    w_bc[:, 0:STATE] = w[:, o:o + STATE]
    w_bc[:, C_ROW:BC] = w[:, o + STATE:o + 2 * STATE]
    taps = np.concatenate([i["L1_attn_conv_w"], i["L1_attn_conv_b"][:, None]], axis=1)
    taps_bc = np.zeros((BC, TAPS + 1), taps.dtype)
    taps_bc[0:STATE] = taps[INNER:INNER + STATE]
    taps_bc[C_ROW:BC] = taps[INNER + STATE:]

    def rows(v):
        return np.broadcast_to(v, (P, v.shape[0]))

    return {
        "w_x": w[:, INNER:o].reshape(KD, P, INNER), "w_bc": w_bc.reshape(KD, P, BC),
        "w_g": w[:, 0:INNER].reshape(KD, P, INNER), "w_dt": w[:, o + 2 * STATE:].reshape(KD, P, SH),
        "w_out": i["L1_attn_W_out"].reshape(FT, P, D),
        "taps": taps[0:INNER].reshape(FT, P, TAPS + 1).transpose(1, 0, 2), "taps_bc": taps_bc,
        "a_log": rows(i["L1_attn_A_log"]), "skip": rows(np.repeat(i["L1_attn_D_skip"], SHD)),
        "dt_bias": rows(i["L1_attn_dt_bias"]), "norm_w": rows(i["L1_attn_norm_w"]),
    }


DECAY_BANK, Y_BANK, G_BANK = 0, 2, 4
BANK_OF = {("turn_x", 0): 5, ("feat", 0): 6, ("feat", 1): 7, ("bcdt", 0): 5, ("gate", 0): 6, ("gate", 1): 7,
           ("turn_y", 0): 5, ("turn_y", 1): 6, ("turn_dA", 0): 7, ("turn_c", 0): 5, ("turn_c", 1): 6, ("out", 0): 7}


def ssm_tensor(k, m, pe):
    nc = k.nc
    mm, turn = nc.tensor.matmul, nc.tensor.transpose

    def step(what, t, par, i):
        if (what, i) in BANK_OF:
            to = k.bank[:, BANK_OF[what, i], :]
        if what == "turn_x":
            pe.wait_ge(m.xn_ready, t + 1)
            if begun(2 * t - 1):
                pe.wait_ge(m.xtok_ready, 2 * t - 1)
            for c in range(KD):
                for j in range(SEQ_TILES):
                    last = turn(to[:, (c * SEQ_TILES + j) * P:(c * SEQ_TILES + j + 1) * P],
                                m.xn[:, j, c * P:(c + 1) * P], k.ident[:])
            last.then_inc(m.xT_full, 1)
        if what == "feat":
            pe.wait_ge(m.xT_ready, t + 1)
            if i == 0:
                if begun(2 * t):
                    pe.wait_ge(m.xtok_ready, 2 * t)
            else:
                if begun(t - 1):
                    pe.wait_ge(m.out_read, t - 1)
            for f in (0, 1):
                for c in range(KD):
                    last = mm(to[:, f * S:(f + 1) * S], m.w_x[:, c, (2 * i + f) * P:(2 * i + f + 1) * P], m.xT[:, c, :],
                              start=(c == 0), stop=(c == KD - 1))
            last.then_inc(m.feat_full, 1)
        if what == "bcdt":
            pe.wait_ge(m.xT_ready, t + 1)
            for c in range(KD):
                mm(to[0:BC, 0:S], m.w_bc[:, c, :], m.xT[:, c, :], start=(c == 0), stop=(c == KD - 1))
            for j in range(SEQ_TILES):
                for c in range(KD):
                    last = mm(to[:, S + j * SH:S + (j + 1) * SH], m.xT[:, c, j * P:(j + 1) * P], m.w_dt[:, c, :],
                              start=(c == 0), stop=(c == KD - 1))
            last.then_inc(m.feat_full, 1)
        if what == "gate":
            pe.wait_ge(m.feat_ready, 3 * t + i + 1)
            for c in range(KD):
                last = mm(to, m.xT[:, c, i * P:(i + 1) * P], m.w_g[:, c, :], start=(c == 0), stop=(c == KD - 1))
            last.then_inc(m.gate_full, 1)
        if what == "turn_dA":
            pe.wait_ge(m.parts_ready, t + 1)
            pe.wait_ge(m.gate_ready, 2 * t + 2)
            to = to.bitcast(BF16)
            for j in range(SEQ_TILES):
                last = turn(to[0:PARTS * SH, j * P:(j + 1) * P], m.parts[:, j].rearrange("p a h -> p (a h)"), k.ident_b[:])
            last.then_inc(m.dAT_full, 1)
        if what == "turn_c":
            pe.wait_ge(m.silu_ready, t + 1)
            if begun(2 * t - 1 + i):
                pe.wait_ge(m.y2T_ready, 2 * t - 1 + i)
            for f in range(FT):
                last = turn(to[:, f * P:(f + 1) * P], m.conv[:, f, i * P:(i + 1) * P], k.ident[:])
            last.then_inc(m.xtok_full, 1)
        if what == "turn_y":
            pe.wait_ge(m.y2_ready, 2 * t + i + 1)
            if is_last(t, SEQS):
                pe.wait_ge(m.xtok_ready, 2 * t + i + 1)
            elif i == 0:
                pe.wait_ge(m.feat_ready, 3 * t + 6)
                pe.wait_ge(m.dt_read, t + 2)
            else:
                pe.wait_ge(m.gate_ready, 2 * t + 3)
            for f in range(FT):
                last = turn(to[:, f * P:(f + 1) * P], m.yg[:, i, f * P:(f + 1) * P], k.ident[:])
            last.then_inc(m.y2T_full, 1)
        if what == "out":
            pe.wait_ge(m.y2T_ready, 2 * t + 2)
            if is_last(t, SEQS):
                if begun(t):
                    pe.wait_ge(m.out_read, t)
            else:
                pe.wait_ge(m.dAT_ready, t + 2)
            for j in range(SEQ_TILES):
                for f in range(FT):
                    last = mm(to[:, j * D:(j + 1) * D], m.y2T[:, j, f, :], m.w_out[:, f, :],
                              start=(f == 0), stop=(f == FT - 1))
            last.then_inc(m.out_full, 1)
        if what == "dab":
            n = 4 * t + i
            pe.wait_ge(m.dAT_ready, t + 1)
            if begun(n - 1):
                pe.wait_ge(m.scan_done, n - 1)
            for h in (0, 1):
                last = mm(k.bank[:, DECAY_BANK + i % 2, h * S:(h + 1) * S], m.sel[:, 2 * i + h, :], m.dAT[:, par, :],
                          start=True, stop=True)
            last.then_inc(m.dab_full, 1)
        if what == "gmat":
            pe.wait_ge(m.bc_ready, t + 1)
            if begun(2 * t):
                pe.wait_ge(m.weight_done, 2 * t)
            mm(k.bank[:, G_BANK, 0:S], m.bT[:, par, 0:P], m.cT[:, par, :], start=True, stop=True)
            mm(k.bank[:, G_BANK, S:SEG], m.bT[:, par, P:S], m.cT[:, par, P:S], start=True, stop=True).then_inc(m.g_full, 1)
        if what == "ymm":
            pe.wait_ge(m.weight_done, 2 * t + i + 1)
            pe.wait_ge(m.xdt_ready, t + 1)
            if i == 0:
                if begun(t):
                    pe.wait_ge(m.y_read, t)
            for h in range(4 * i, 4 * i + 4):
                hc = slice(h * SHD, (h + 1) * SHD)
                mm(k.bank[:, Y_BANK, hc], m.m[:, h, 0:P], m.xdt[:, par, 0, hc], start=True, stop=True)
                mm(k.bank[:, Y_BANK + 1, hc], m.m[:, h, P:S], m.xdt[:, par, 0, hc], start=True, stop=False)
                last = mm(k.bank[:, Y_BANK + 1, hc], m.m[:, h, S:SEG], m.xdt[:, par, 1, hc], start=False, stop=True)
            last.then_inc(m.y_full, 1)

    pe.wait_ge(m.loaded, m.LOADS)
    pe.wait_ge(m.tables_step, 1 + PARTS)
    go_through(m, pe, step)


def ssm_scalar(k, m, act):
    nc = k.nc
    copy, activation = nc.scalar.copy, nc.scalar.activation
    act.wait_ge(m.loaded, m.LOADS)
    act.wait_ge(m.log_ready, 1)
    activation(m.pos_a[:], m.a_lim[:], ACT.Exp).then_inc(m.tables, 1)

    def step(what, t, par, i):
        if (what, i) in BANK_OF:
            at = k.bank[:, BANK_OF[what, i], :]
        if what == "turn_x":
            act.wait_ge(m.xT_full, t + 1)
            if begun(2 * t):
                act.wait_ge(m.gate_full, 2 * t)
            copy(m.xT[:].rearrange("p c t -> p (c t)"), at).then_inc(m.xT_ready, 1)
        if what == "feat":
            act.wait_ge(m.feat_full, 3 * t + i + 1)
            if begun(t):
                act.wait_ge(m.conv_ready, t)
            copy(m.feat[:, 2 * i:2 * i + 2, TAPS - 1:], at.rearrange("p (f t) -> p f t", f=2)).then_inc(m.feat_ready, 1)
        if what == "bcdt":
            act.wait_ge(m.feat_full, 3 * t + 3)
            if begun(t):
                act.wait_ge(m.conv_ready, t)
            copy(m.feat_bc[:, TAPS - 1:], at[0:BC, 0:S]).then_inc(m.feat_ready, 1)
        if what == "dt":
            act.wait_ge(m.min_ready, t + 1)
            activation(m.s_e[:], m.s_mn[:], ACT.Exp).then_inc(m.e_ready, 1)
            act.wait_ge(m.w_ready, t + 1)
            activation(m.s_ln[:], m.s_w[:], ACT.Ln).then_inc(m.ln_ready, 1)
            act.wait_ge(m.da_ready, t + 1)
            activation(m.s_decay[:], m.s_da[:], ACT.Exp).then_inc(m.decay_ready, 1)
        if what == "gate":
            act.wait_ge(m.gate_full, 2 * t + i + 1)
            if begun(t - 1):
                act.wait_ge(m.yg_ready, t - 1)
            activation(m.gate[:, par, i, :], at, ACT.Silu).then_inc(m.gate_ready, 1)
        if what == "turn_dA":
            act.wait_ge(m.dAT_full, t + 1)
            if begun(4 * (t - 1)):
                act.wait_ge(m.dab_full, 4 * (t - 1))
            copy(m.dAT[:, par, :], at.bitcast(BF16)[0:PARTS * SH, 0:S]).then_inc(m.dAT_ready, 1)
        if what == "silu":
            act.wait_ge(m.conv_ready, t + 1)
            if begun(t - 1):
                act.wait_ge(m.g_full, t - 1)
            activation(m.bT[:, par, :], m.conv_bc[0:STATE, :], ACT.Silu)
            activation(m.cT[:, par, :], m.conv_bc[C_ROW:BC, :], ACT.Silu).then_inc(m.bc_ready, 1)
            whole = m.conv[:].rearrange("p f t -> p (f t)")
            activation(whole, whole, ACT.Silu).then_inc(m.silu_ready, 1)
        if what == "turn_c":
            act.wait_ge(m.xtok_full, 2 * t + i + 1)
            if begun(t):
                act.wait_ge(m.xdt_ready, t)
            if begun(t):
                act.wait_ge(m.xd_ready, t)
            copy(m.xtok[:, i, :], at).then_inc(m.xtok_ready, 1)
        if what == "gating":
            act.wait_ge(m.yg_ready, t + 1)
            for j in range(SEQ_TILES):
                last = activation(m.square[:, j, :], m.yg[:, j, :], ACT.Square, accum_out=m.sum2[:, j:j + 1])
            last.then_inc(m.square_ready, 1)
        if what == "turn_y":
            act.wait_ge(m.y2T_full, 2 * t + i + 1)
            if begun(t):
                act.wait_ge(m.out_full, t)
            copy(m.y2T[:, i].rearrange("p f t -> p (f t)"), at).then_inc(m.y2T_ready, 1)

    go_through(m, act, step)


def ssm_vector(k, m, dve):
    nc = k.nc
    v = nc.vector
    tt, ts, stt = v.tensor_tensor, v.tensor_scalar, v.scalar_tensor_tensor
    chain = Chain(dve, m.dve_step)
    link = chain.link

    def step(what, t, par, i):
        if what == "norm":
            for j in range(SEQ_TILES):
                last = v.bn_stats(m.stat[:, j, :], cols(k.x, SEQ_TILES * t + j))
            link(last)
            own_wait(k, dve)
            for j in range(SEQ_TILES):
                last = v.bn_aggr(m.mv[:, j, :], m.stat[:, j, :])
            link(last)
            ts(m.mv[:, :, 1], m.mv[:, :, 1], EPS, None, ALU.add).then_inc(m.var_ready, 1)
            dve.wait_ge(m.rstd_ready, t + 1)
            if begun(t):
                dve.wait_ge(m.xT_full, t)
            for j in range(SEQ_TILES):
                last = ts(m.xn[:, j, :], cols(k.x, SEQ_TILES * t + j), m.mv[:, j, 0:1], m.rstd[:, j:j + 1],
                          ALU.subtract, ALU.mult)
            last.then_inc(m.xn_ready, 1)
        if what == "dt":
            def rows(a):
                return a[:].unsqueeze(1).to_broadcast([P, SEQ_TILES, SH])
            dve.wait_ge(m.feat_ready, 3 * t + 3)
            raw = k.bank[:, BANK_OF["bcdt", 0], S:S + SEQ_TILES * SH].rearrange("p (j h) -> p j h", j=SEQ_TILES)
            tt(m.s_u[:], raw, rows(m.dt_bias), ALU.add).then_inc(m.dt_read, 1)
            dve.wait_ge(m.dt_read, t + 1)
            stt(m.s_mn[:], m.s_u[:], -1.0, m.s_u[:], ALU.mult, ALU.min).then_inc(m.min_ready, 1)
            dve.wait_ge(m.e_ready, t + 1)
            ts(m.s_w[:], m.s_e[:], 1.0, None, ALU.add).then_inc(m.w_ready, 1)
            dve.wait_ge(m.w_ready, t + 1)
            link(ts(m.s_den[:], m.s_w[:], -1.0, None, ALU.add))
            link(ts(m.s_eq[:], m.s_den[:], 0.0, None, ALU.is_equal))
            link(tt(m.s_den[:], m.s_den[:], m.s_eq[:], ALU.add))
            link(v.reciprocal(m.s_rest[:], m.s_den[:]))
            link(tt(m.s_rest[:], m.s_rest[:], m.s_e[:], ALU.mult))
            dve.wait_ge(m.ln_ready, t + 1)
            link(tt(m.s_num[:], m.s_ln[:], m.s_eq[:], ALU.add))
            link(tt(m.s_num[:], m.s_num[:], m.s_rest[:], ALU.mult))
            link(stt(m.s_dt[:], m.s_u[:], 0.0, m.s_num[:], ALU.max, ALU.add))
            link(stt(m.s_da[:], m.s_dt[:], DOWN, rows(m.neg_a), ALU.mult, ALU.mult))
            ts(m.s_da[:], m.s_da[:], -200.0 * DOWN, 1.0 / DOWN, ALU.max, ALU.mult).then_inc(m.da_ready, 1)
            dve.wait_ge(m.decay_ready, t + 1)
            if begun(t):
                dve.wait_ge(m.dAT_full, t)
            link(v.tensor_copy(m.parts[:, :, 0, :], m.s_decay[:]))
            link(tt(m.s_rest[:], m.s_decay[:], m.parts[:, :, 0, :], ALU.subtract))
            link(v.tensor_copy(m.parts[:, :, 1, :], m.s_rest[:]))
            tt(m.parts[:, :, 2, :], m.s_rest[:], m.parts[:, :, 1, :], ALU.subtract).then_inc(m.parts_ready, 1)
        if what == "conv":
            if i == 0:
                dve.wait_ge(m.feat_ready, 3 * t + 3)
                if begun(2 * t):
                    dve.wait_ge(m.xtok_full, 2 * t)
                if begun(t):
                    dve.wait_ge(m.bc_ready, t)
            for f in range(FT + 1):
                src, dst, taps = (m.feat[:, f], m.conv[:, f], m.taps[:, f]) if f < FT else (m.feat_bc[:], m.conv_bc[:], m.taps_bc[:])
                if i == 0:
                    last = ts(dst, src[:, i:i + S], taps[:, i:i + 1], taps[:, TAPS:TAPS + 1], ALU.mult, ALU.add)
                else:
                    last = stt(dst, src[:, i:i + S], taps[:, i:i + 1], dst, ALU.mult, ALU.add)
            if i == TAPS - 1:
                last.then_inc(m.conv_ready, 1)
            else:
                link(last)
        if what == "xdt":
            dve.wait_ge(m.xtok_ready, 2 * t + 2)
            if begun(2 * (t - 1)):
                dve.wait_ge(m.y_full, 2 * (t - 1))
            for j in range(SEQ_TILES):
                last = tt(m.xdt[:, par, j, :].rearrange("p (h f) -> p h f", h=SH),
                          m.xtok[:, j, :].rearrange("p (h f) -> p h f", h=SH),
                          m.s_dt[:, j, :].unsqueeze(2).to_broadcast([P, SH, SHD]), ALU.mult)
            last.then_inc(m.xdt_ready, 1)
        if what == "dab":
            dve.wait_ge(m.dab_full, 4 * t + i + 1)
            if begun(2 * t):
                dve.wait_ge(m.y_full, 2 * t)
            for h in (0, 1):
                base = k.bank[:, DECAY_BANK + i % 2, h * S:(h + 1) * S]
                to = m.m[:, 2 * i + h, :]
                v.tensor_tensor_scan(to[:, 0:S], base, m.delta[:], 0.0, ALU.mult, ALU.add)
                last = v.tensor_tensor_scan(to[:, S:SEG], base[:, P:S], m.delta[:, 0:P], 0.0, ALU.mult, ALU.add)
            last.then_inc(m.scan_done, 1)
        if what == "weight":
            dve.wait_ge(m.g_full, t + 1)
            dve.wait_ge(m.scan_done, 4 * t + 2 * i + 2)
            part = m.m[:, 4 * i:4 * i + 4, :]
            tt(part, part, k.bank[:, G_BANK, 0:SEG].unsqueeze(1).to_broadcast([P, 4, SEG]), ALU.mult)\
                .then_inc(m.weight_done, 1)
        if what == "gating":
            dve.wait_ge(m.y_full, 2 * t + 2)
            dve.wait_ge(m.xd_ready, t + 1)
            if begun(2 * t):
                dve.wait_ge(m.y2T_full, 2 * t)
            tt(m.yg[:], k.bank[:, Y_BANK:Y_BANK + SEQ_TILES, :], m.xd[:, par], ALU.add).then_inc(m.y_read, 1)
            dve.wait_ge(m.y_read, t + 1)
            dve.wait_ge(m.gate_ready, 2 * t + 2)
            tt(m.yg[:], m.yg[:], m.gate[:, par], ALU.mult).then_inc(m.yg_ready, 1)
        if what == "scale":
            dve.wait_ge(m.square_ready, t + 1)
            ts(m.ms[:], m.sum2[:], 1.0 / INNER, EPS, ALU.mult, ALU.add).then_inc(m.ms_ready, 1)
            dve.wait_ge(m.rms_ready, t + 1)
            for j in range(SEQ_TILES):
                stt(m.yg[:, j, :], m.yg[:, j, :], m.rms[:, j:j + 1], m.norm_w[:], ALU.mult, ALU.mult)\
                    .then_inc(m.y2_ready, 1)
        if what == "post":
            dve.wait_ge(m.out_full, t + 1)
            y = k.bank[:, BANK_OF["out", 0], :].rearrange("p (j d) -> p j d", j=SEQ_TILES)
            for j in range(SEQ_TILES):
                last = v.bn_stats(m.pstat[:, j, :], y[:, j, :])
            link(last)
            own_wait(k, dve)
            for j in range(SEQ_TILES):
                last = v.bn_aggr(m.pmv[:, j, :], m.pstat[:, j, :])
            link(last)
            ts(m.pmv[:, :, 1], m.pmv[:, :, 1], EPS, None, ALU.add).then_inc(m.post_var, 1)
            dve.wait_ge(m.post_rstd, t + 1)
            for j in range(SEQ_TILES):
                last = ts(m.z[:, j, :], y[:, j, :], m.pmv[:, j, 0:1], m.prstd[:, j:j + 1], ALU.subtract, ALU.mult)
            last.then_inc(m.out_read, 1)
            dve.wait_ge(m.out_read, t + 1)
            x = cols(k.x, t, SEQ_TILES * D)
            tt(x, x, m.z[:].rearrange("p j d -> p (j d)"), ALU.add).then_inc(m.x_done, 1)

    v.memset(m.feat[:, :, 0:TAPS - 1], 0.0)
    link(v.memset(m.feat_bc[:, 0:TAPS - 1], 0.0))
    dve.wait_ge(m.loaded, m.LOADS)
    ts(m.a_lim[:], m.a_log[:], 88.0, None, ALU.min).then_inc(m.log_ready, 1)
    dve.wait_ge(m.tables, 2)
    link(ts(m.neg_a[:], m.pos_a[:], -1.0, None, ALU.mult))
    go_through(m, dve, step, chain, 2 * (2 + 9 + 3 + 3 + 2))
    dve.wait_ge(m.x_done, m.finished)


def ssm_pool(k, m, pool):
    g = k.nc.gpsimd
    g.memset(m.delta[:], 0.0)
    g.memset(m.sel[:], 0.0).then_inc(m.tables_step, 1)
    pool.wait_ge(m.tables_step, 1)
    for part in range(PARTS):
        g.affine_select(out=m.sel[:], in_=m.sel[:], compare_op=ALU.not_equal, fill=1.0, base=-part * SH,
                        pattern=[[-1, SH], [0, P]], channel_multiplier=1).then_inc(m.tables_step, 1)
        pool.wait_ge(m.tables_step, 2 + part)
    g.affine_select(out=m.delta[:], in_=m.delta[:], compare_op=ALU.not_equal, fill=1.0, base=0,
                    pattern=[[-1, S]], channel_multiplier=1).then_inc(m.tables, 1)
    pool.wait_ge(m.loaded, m.LOADS)

    def step(what, t, par, i):
        if what == "norm":
            pool.wait_ge(m.var_ready, t + 1)
            g.tensor_tensor(m.rstd[:], m.mv[:, :, 1], k.minus_half[:, 0:SEQ_TILES], ALU.pow).then_inc(m.rstd_ready, 1)
        if what == "post":
            pool.wait_ge(m.post_var, t + 1)
            g.tensor_tensor(m.prstd[:], m.pmv[:, :, 1], k.minus_half[:, 0:SEQ_TILES], ALU.pow).then_inc(m.post_rstd, 1)
        if what == "xdt":
            pool.wait_ge(m.xtok_ready, 2 * t + 2)
            if begun(t - 1):
                pool.wait_ge(m.y_read, t - 1)
            for j in range(SEQ_TILES):
                last = g.tensor_tensor(m.xd[:, par, j, :], m.xtok[:, j, :], m.skip[:], ALU.mult)
            last.then_inc(m.xd_ready, 1)
        if what == "scale":
            pool.wait_ge(m.ms_ready, t + 1)
            g.tensor_tensor(m.rms[:], m.ms[:], k.minus_half[:, 0:SEQ_TILES], ALU.pow).then_inc(m.rms_ready, 1)

    go_through(m, pool, step)


class Kernel:

    def __init__(self, nc, ctx):
        self.nc, self.ctx = nc, ctx

    def sem(self, name):
        return self.ctx.enter_context(self.nc.semaphore(name))

    def sb(self, name, shape, dtype=F32):
        return self.ctx.enter_context(self.nc.sbuf_tensor(name, shape, dtype))


def program(nc, a, out):
    with ExitStack() as ctx:
        k = Kernel(nc, ctx)
        sem, sb = k.sem, k.sb
        k.bank = ctx.enter_context(nc.psum_tensor("bank", [P, 8, BANK], F32))
        k.x = sb("x", [P, TILES * D])
        k.spare = sb("spare", [P, 1])
        k.ident = sb("ident", [P, P])
        k.ident_b = sb("ident_b", [P, P], BF16)
        k.minus_half = sb("minus_half", [P, 4])
        k.expert_no = sb("expert_no", [P, E])
        gate0 = sb("gate0", [P, KD, E])
        gate1 = sb("gate1", [P, KD, E])
        up_w = sb("up_w", [P, KD, (E + 2) * 2 * 176])
        down_w = sb("down_w", [P, 25, D])

        x_loaded = sem("x_loaded")
        gates_loaded, moe0_loaded, moe1_loaded = sem("gates_loaded"), sem("moe0_loaded"), sem("moe1_loaded")
        consts = k.consts = sem("consts")
        consts_step = sem("consts_step")
        stored = sem("stored")

        first = Moe(k, "moe0", 176, 1, 2, True, None, up_w, down_w, gate0, [(moe0_loaded, 64), (gates_loaded, 32)])
        second = Moe(k, "moe1", 128, 2, 8, False, 2.5, up_w, down_w, gate1, [(moe1_loaded, 64), (gates_loaded, 32)])
        layers = [Attention(k, a), first, Ssm(k, a), second]
        for layer in layers:
            if not isinstance(layer, Moe):
                layer.weights(sb)
        for layer in layers:
            with ExitStack() as scratch:
                layer.buffers(lambda name, shape, dtype=F32: scratch.enter_context(nc.sbuf_tensor(name, shape, dtype)))

        def walk(eng, **parts):
            before = None
            for layer in layers:
                if before is not None:
                    eng.wait_ge(before.x_done, before.finished)
                parts[type(layer).__name__](k, layer, eng)
                before = layer

        block = ctx.enter_context(nc.Block())

        @block.sync
        def _(sp):
            for c in range(0, TILES, 8):
                sp.dma_start(k.x[:, c * D:(c + 8) * D].rearrange("p (t d) -> p t d", d=D),
                             a["x"][c:c + 8].rearrange("t p d -> p t d")).then_inc(x_loaded, 16)
            for layer in layers:
                if not isinstance(layer, Moe):
                    layer.load(sp)
            sp.dma_start(gate0[:], a["gate0"].rearrange("c p e -> p c e")).then_inc(gates_loaded, 16)
            sp.dma_start(gate1[:], a["gate1"].rearrange("c p e -> p c e")).then_inc(gates_loaded, 16)

            def load_moe(m, up, down, done):
                W = m.units * 2 * m.unit_w
                for c in range(KD):
                    sp.dma_start(up_w[:, c, 0:W], a[up][c]).then_inc(done, 16)
                half = m.chunks // 2
                for lo, hi in ((0, half), (half, m.chunks)):
                    sp.dma_start(down_w[:, lo:hi, :], a[down][lo:hi].rearrange("c p d -> p c d")).then_inc(done, 16)

            if first in layers:
                load_moe(first, "up0", "down0", moe0_loaded)
            if second in layers:
                if first in layers:
                    sp.wait_ge(first.x_done, first.finished)
                load_moe(second, "up1", "down1", moe1_loaded)
            pair = 2
            per_pair = layers[-1].finished * pair // TILES
            with sp.Fori(0, TILES // pair) as it:
                sp.wait_ge(layers[-1].x_done, per_pair * it + per_pair)
                sp.dma_start(out[bass.ds(pair * it, pair)].rearrange("t p d -> p t d"),
                             k.x[:, bass.ds(it * pair * D, pair * D)].rearrange("p (t d) -> p t d", d=D)).then_inc(stored, 16)
            sp.wait_ge(stored, 16 * TILES // pair)

        @block.gpsimd
        def _(pool):
            nc.gpsimd.memset(k.ident[:], 0.0).then_inc(consts_step, 1)
            nc.gpsimd.memset(k.minus_half[:], -0.5).then_inc(consts, 1)
            nc.gpsimd.iota(k.expert_no[:], [[1, E]], base=0, channel_multiplier=0,
                           allow_small_or_imprecise_dtypes=True).then_inc(consts, 1)
            pool.wait_ge(consts_step, 1)
            nc.gpsimd.affine_select(out=k.ident[:], in_=k.ident[:], compare_op=ALU.not_equal, fill=1.0, base=0,
                                    pattern=[[-1, P]], channel_multiplier=1).then_inc(consts, 1)
            pool.wait_ge(consts, 3)
            nc.gpsimd.tensor_copy(k.ident_b[:], k.ident[:]).then_inc(consts, 1)
            walk(pool, Moe=moe_pool, Attention=attention_pool, Ssm=ssm_pool)

        @block.scalar
        def _(act):
            walk(act, Moe=moe_scalar, Attention=attention_scalar, Ssm=ssm_scalar)

        @block.vector
        def _(dve):
            dve.wait_ge(consts, 4)
            dve.wait_ge(x_loaded, 16 * TILES // 8)
            walk(dve, Moe=moe_vector, Attention=attention_vector, Ssm=ssm_vector)

        @block.tensor
        def _(pe):
            pe.wait_ge(consts, 4)
            walk(pe, Moe=moe_tensor, Attention=attention_tensor, Ssm=ssm_tensor)


def expert_columns(first, second, per_unit):
    n, d, inter = first.shape
    both = np.stack([first, second]).reshape(2, n // per_unit, per_unit, d, inter)
    return np.ascontiguousarray(both.transpose(3, 1, 0, 2, 4)).reshape(KD, P, n * 2 * inter)


def padded_rows(rows):
    n = rows.shape[0]
    full = np.zeros((-(-n // P) * P, rows.shape[1]), rows.dtype)
    full[:n] = rows
    return full.reshape(-1, P, rows.shape[1])


def layout(i):
    c = np.ascontiguousarray
    arrays = {"x": i["L0_attn_x"].reshape(TILES, P, D)}
    arrays["gate0"] = c(i["L0_ffn_gate_w"].T).reshape(KD, P, E)
    arrays["gate1"] = c(i["L1_ffn_gate_w"].T).reshape(KD, P, E)

    def with_shared(routed, shared):
        return np.concatenate([routed, shared])

    sw1, sw3 = (i[n].reshape(2, 176, D).transpose(0, 2, 1) for n in ("L0_ffn_sw1", "L0_ffn_sw3"))
    arrays["up0"] = expert_columns(with_shared(i["L0_ffn_w1"].transpose(0, 2, 1), sw1),
                                   with_shared(i["L0_ffn_w3"].transpose(0, 2, 1), sw3), 1)
    arrays["down0"] = padded_rows(np.concatenate([i["L0_ffn_w2"].transpose(0, 2, 1).reshape(-1, D), i["L0_ffn_sw2"].T]))
    swg, swu = (i[n].reshape(D, 2, P).transpose(1, 0, 2) for n in ("L1_ffn_sWg", "L1_ffn_sWu"))
    arrays["up1"] = expert_columns(with_shared(i["L1_ffn_Wg"], swg), with_shared(i["L1_ffn_Wu"], swu), 2)
    arrays["down1"] = padded_rows(np.concatenate([i["L1_ffn_Wd"].reshape(-1, D), i["L1_ffn_sWd"]]))
    arrays.update(attention_layout(i))
    arrays.update(ssm_layout(i))
    return {n: c(v) for n, v in arrays.items()}


def kernel(**inputs):
    import concourse.bacc as bacc
    from concourse.bass_utils import run_bass_kernel_spmd

    arrays = layout({n: np.asarray(v) for n, v in inputs.items()})
    nc = bacc.Bacc("TRN2", target_bir_lowering=False, num_devices=1)
    handles = {n: nc.dram_tensor("in_" + n, v.shape, mybir.dt.from_np(v.dtype), kind="ExternalInput").ap()
               for n, v in arrays.items()}
    out = nc.dram_tensor("out", (TILES, P, D), F32, kind="ExternalOutput").ap()
    program(nc, handles, out)
    done = run_bass_kernel_spmd(nc, [{"in_" + n: v for n, v in arrays.items()}], core_ids=[0])
    return done.results[0]["out"].reshape(B, S, D)
```

```python
from contextlib import ExitStack

import numpy as np

import concourse.bass as bass
from concourse import mybir

F32 = mybir.dt.float32
BF16 = mybir.dt.bfloat16
U32 = mybir.dt.uint32
I32 = mybir.dt.int32
ALU = mybir.AluOpType
ACT = mybir.ActivationFunctionType
AX = mybir.AxisListType

P = 128
B, S, D = 16, 256, 256
TILES = B * S // P
SEQ_TILES = S // P
KD = D // P
E = 16
EPS = 1e-5
BANK = 512


class Chain:

    def __init__(self, eng, sem):
        self.eng, self.sem, self.count, self.turns = eng, sem, 0, 0

    def link(self, ins):
        ins.then_inc(self.sem, 1)
        self.count += 1
        self.eng.wait_ge(self.sem, self.count + self.turns)


def own_wait(k, eng):
    k.nc.vector.memset(k.spare[:], 0.0)


def begun(count):
    return not isinstance(count, int) or count > 0


def cols(tile, t, width=D):
    return tile[:, bass.ds(t * width, width)]


def go_through(layer, eng, step, chain=None, links=0):
    for s in layer.head():
        step(*s)
    before = chain.count if chain else 0
    with eng.Fori(0, layer.turns) as it:
        if chain:
            chain.turns = it * links
        for s in layer.pair(it):
            step(*s)
    if chain:
        assert chain.count - before == links, chain.count - before
        chain.turns, chain.count = 0, before + layer.turns * links
    for s in layer.rest():
        step(*s)


class Moe:

    turns = (TILES - 4) // 2

    def __init__(self, k, name, inter, per_unit, scale, w_up, w_down, w_gate, loads):
        self.k, self.name, self.inter, self.per_unit, self.scale = k, name, inter, per_unit, scale
        self.w_up, self.w_down, self.w_gate, self.loads = w_up, w_down, w_gate, loads
        self.finished = TILES
        self.units = (E + 2) // per_unit
        self.unit_w = inter * per_unit
        self.total = inter * (E + 2)
        self.chunks = -(-self.total // P)
        self.groups = -(-self.chunks // 4)
        self.last_unit = [(min((g + 1) * 4 * P, self.total) - 1) // self.unit_w for g in range(self.groups)]
        self.xn_ready = k.sem(name + "_xn_ready")
        self.xT_full = k.sem(name + "_xT_full")
        self.xT_ready = k.sem(name + "_xT_ready")
        self.var_ready = k.sem(name + "_var_ready")
        self.rstd_ready = k.sem(name + "_rstd_ready")
        self.logits_full = k.sem(name + "_logits_full")
        self.exp_ready = k.sem(name + "_exp_ready")
        self.up_full = k.sem(name + "_up_full")
        self.silu_ready = k.sem(name + "_silu_ready")
        self.h_ready = k.sem(name + "_h_ready")
        self.hT_full = k.sem(name + "_hT_full")
        self.hT_ready = k.sem(name + "_hT_ready")
        self.down_done = k.sem(name + "_down_done")
        self.post_var = k.sem(name + "_post_var")
        self.post_rstd = k.sem(name + "_post_rstd")
        self.y_used = k.sem(name + "_y_used")
        self.x_done = k.sem(name + "_x_done")
        self.dve_step = k.sem(name + "_dve_step")

    def buffers(self, sb):
        n = self.name
        self.h = sb(n + "_h", [P, 2, self.chunks * P])
        self.hT = sb(n + "_hT", [P, 2, 4, P])
        self.silu = sb(n + "_silu", [P, 3, self.unit_w])
        self.xn = sb(n + "_xn", [P, D])
        self.xT = sb(n + "_xT", [P, 2, KD, P])
        self.comb = sb(n + "_comb", [P, 2, E + 2])
        self.stat = sb(n + "_stat", [P, 6])
        self.mv = sb(n + "_mv", [P, 2])
        self.rstd = sb(n + "_rstd", [P, 1])
        self.pstat = sb(n + "_pstat", [P, 6])
        self.pmv = sb(n + "_pmv", [P, 2])
        self.prstd = sb(n + "_prstd", [P, 1])
        self.z = sb(n + "_z", [P, D])
        self.exp = sb(n + "_exp", [P, E])
        self.score = sb(n + "_score", [P, E])
        self.den = sb(n + "_den", [P, 1])
        self.rden = sb(n + "_rden", [P, 1])
        self.top = sb(n + "_top", [P, 8])
        self.part = sb(n + "_part", [P, E])

    def pieces(self, g):
        return [(c, min(P, self.total - c * P)) for c in range(4 * g, min(4 * g + 4, self.chunks))]

    def tile(self, t, par, first, last):
        for u in range(self.units):
            yield "up", t, par, u
            if not last and u in (3, 5, 6, 7):
                yield {3: "norm", 5: "turn_x", 6: "logits", 7: "route"}[u], t + 1, 1 - par, 0
            for g, unit in enumerate(self.last_unit):
                for what, at in (("down", unit + 3), ("turn", unit + 2)):
                    if at == u:
                        yield what, t, par, g
                    if at == u + self.units and not first:
                        yield what, t - 1, 1 - par, g
            if u == 5 and not first:
                yield "post", t - 1, 1 - par, 0

    def head(self):
        yield from ((what, 0, 0, 0) for what in ("norm", "turn_x", "logits", "route"))
        yield from self.tile(0, 0, True, False)
        yield from self.tile(1, 1, False, False)

    def pair(self, it):
        yield from self.tile(2 * it + 2, 0, False, False)
        yield from self.tile(2 * it + 3, 1, False, False)

    def rest(self):
        t = TILES - 1
        yield from self.tile(t - 1, 0, False, False)
        yield from self.tile(t, 1, False, True)
        for at in range(self.units, self.units + 4):
            for g, unit in enumerate(self.last_unit):
                if unit + 3 == at:
                    yield "down", t, 1, g
                if unit + 2 == at:
                    yield "turn", t, 1, g
        yield "post", t, 1, 0


def moe_tensor(k, m, pe):
    U, G = m.units, m.groups
    nc = k.nc

    def step(what, t, par, i):
        n, g = t * U + i, t * G + i
        if what == "turn_x":
            pe.wait_ge(m.xn_ready, t + 1)
            if begun(t):
                pe.wait_ge(m.exp_ready, t)
            for c in range(KD):
                last = nc.tensor.transpose(k.bank[:, 7, c * P:(c + 1) * P], m.xn[:, c * P:(c + 1) * P], k.ident[:])
            last.then_inc(m.xT_full, 1)
        if what == "logits":
            pe.wait_ge(m.xT_ready, t + 1)
            for c in range(KD):
                last = nc.tensor.matmul(k.bank[:, 7, D:D + E], m.xT[:, par, c, :], m.w_gate[:, c, :],
                                        start=(c == 0), stop=(c == KD - 1))
            last.then_inc(m.logits_full, 1)
        if what == "up":
            pe.wait_ge(m.xT_ready, t + 1)
            if begun(n - 2):
                pe.wait_ge(m.h_ready, n - 2)
            W = 2 * m.unit_w
            for c in range(KD):
                last = nc.tensor.matmul(k.bank[:, i % 3, 0:W], m.xT[:, par, c, :], m.w_up[:, c, i * W:(i + 1) * W],
                                        start=(c == 0), stop=(c == KD - 1))
            last.then_inc(m.up_full, 1)
        if what == "turn":
            bank = 3 + (par * G + i) % 2
            pe.wait_ge(m.h_ready, t * U + m.last_unit[i] + 1)
            if begun(g - 1):
                pe.wait_ge(m.hT_ready, g - 1)
            for j, (c, w) in enumerate(m.pieces(i)):
                last = nc.tensor.transpose(k.bank[0:w, bank, j * P:(j + 1) * P], m.h[:, par, c * P:c * P + w], k.ident[:])
            last.then_inc(m.hT_full, 1)
        if what == "down":
            pe.wait_ge(m.hT_ready, g + 1)
            if i == 0:
                if begun(t - 1):
                    pe.wait_ge(m.y_used, t - 1)
            for j, (c, w) in enumerate(m.pieces(i)):
                last = nc.tensor.matmul(k.bank[:, 5 + par, 0:D], m.hT[0:w, (par * G + i) % 2, j, :],
                                        m.w_down[0:w, c, :], start=(c == 0), stop=(c == m.chunks - 1))
            last.then_inc(m.down_done, 1)

    for sem, count in m.loads:
        pe.wait_ge(sem, count)
    go_through(m, pe, step)


def moe_scalar(k, m, act):
    U, G = m.units, m.groups
    nc = k.nc

    def step(what, t, par, i):
        n, g = t * U + i, t * G + i
        if what == "turn_x":
            act.wait_ge(m.xT_full, t + 1)
            if begun((t - 1) * U):
                act.wait_ge(m.up_full, (t - 1) * U)
            nc.scalar.copy(m.xT[:, par, :, :].rearrange("p c t -> p (c t)"), k.bank[:, 7, 0:D]).then_inc(m.xT_ready, 1)
        if what == "route":
            act.wait_ge(m.logits_full, t + 1)
            nc.scalar.activation(m.exp[:], k.bank[:, 7, D:D + E], ACT.Exp, scale=-1.0).then_inc(m.exp_ready, 1)
        if what == "up":
            act.wait_ge(m.up_full, n + 1)
            if begun(n - 2):
                act.wait_ge(m.h_ready, n - 2)
            nc.scalar.activation(m.silu[:, i % 3, :], k.bank[:, i % 3, 0:m.unit_w], ACT.Silu).then_inc(m.silu_ready, 1)
        if what == "turn":
            act.wait_ge(m.hT_full, g + 1)
            if begun(g - 1):
                act.wait_ge(m.down_done, g - 1)
            w = max(w for _, w in m.pieces(i))
            full = len(m.pieces(i)) * P
            nc.scalar.copy(m.hT[0:w, (par * G + i) % 2, :, :].rearrange("p c t -> p (c t)")[:, 0:full],
                           k.bank[0:w, 3 + (par * G + i) % 2, 0:full]).then_inc(m.hT_ready, 1)

    go_through(m, act, step)


def moe_vector(k, m, dve):
    U, G = m.units, m.groups
    nc = k.nc
    chain = Chain(dve, m.dve_step)
    link = chain.link
    chain.link(nc.vector.memset(m.comb[:, :, E:E + 2], 1.0))

    def route(t, par):
        score, comb = m.score, m.comb[:, par, 0:E]
        dve.wait_ge(m.exp_ready, t + 1)
        link(nc.vector.tensor_scalar(m.part[:], m.exp[:], 1.0, None, ALU.add))
        link(nc.vector.reciprocal(score[:], m.part[:]))
        own_wait(k, dve)
        link(nc.vector.max(m.top[:], score[:]))
        own_wait(k, dve)
        link(nc.vector.match_replace(m.part[:], m.top[:], score[:], 0.0))
        link(nc.vector.reduce_sum(m.den[:], m.top[:], AX.X))
        link(nc.vector.tensor_scalar(m.den[:], m.den[:], 1e-6, None, ALU.add))
        link(nc.vector.reciprocal(m.rden[:], m.den[:]))
        link(nc.vector.tensor_tensor(comb, score[:], m.part[:], ALU.subtract))
        link(nc.vector.tensor_scalar(comb, comb, m.rden[:], m.scale, ALU.mult, ALU.mult))

    def step(what, t, par, i):
        n = t * U + i
        if what == "norm":
            x = cols(k.x, t)
            link(nc.vector.bn_stats(m.stat[:], x))
            own_wait(k, dve)
            link(nc.vector.bn_aggr(m.mv[:], m.stat[:]))
            nc.vector.tensor_scalar(m.mv[:, 1:2], m.mv[:, 1:2], EPS, None, ALU.add).then_inc(m.var_ready, 1)
            dve.wait_ge(m.rstd_ready, t + 1)
            if begun(t):
                dve.wait_ge(m.xT_full, t)
            nc.vector.tensor_scalar(m.xn[:], x, m.mv[:, 0:1], m.rstd[:], ALU.subtract, ALU.mult).then_inc(m.xn_ready, 1)
        if what == "route":
            route(t, par)
        if what == "up":
            dve.wait_ge(m.silu_ready, n + 1)
            if i == 0:
                if begun((t - 1) * G):
                    dve.wait_ge(m.hT_full, (t - 1) * G)
            for e in range(m.per_unit):
                a, b = e * m.inter, m.unit_w + e * m.inter
                ex = i * m.per_unit + e
                last = nc.vector.scalar_tensor_tensor(
                    m.h[:, par, ex * m.inter:(ex + 1) * m.inter], m.silu[:, i % 3, a:a + m.inter],
                    m.comb[:, par, ex:ex + 1], k.bank[:, i % 3, b:b + m.inter], ALU.mult, ALU.mult)
            last.then_inc(m.h_ready, 1)
        if what == "post":
            y = k.bank[:, 5 + par, 0:D]
            dve.wait_ge(m.down_done, (t + 1) * G)
            link(nc.vector.bn_stats(m.pstat[:], y))
            own_wait(k, dve)
            link(nc.vector.bn_aggr(m.pmv[:], m.pstat[:]))
            nc.vector.tensor_scalar(m.pmv[:, 1:2], m.pmv[:, 1:2], EPS, None, ALU.add).then_inc(m.post_var, 1)
            dve.wait_ge(m.post_rstd, t + 1)
            nc.vector.tensor_scalar(m.z[:], y, m.pmv[:, 0:1], m.prstd[:], ALU.subtract, ALU.mult).then_inc(m.y_used, 1)
            dve.wait_ge(m.y_used, t + 1)
            x = cols(k.x, t)
            nc.vector.tensor_tensor(x, x, m.z[:], ALU.add).then_inc(m.x_done, 1)

    links = 2 * (2 + 2 + 9)
    go_through(m, dve, step, chain, links)
    dve.wait_ge(m.x_done, TILES)


def moe_pool(k, m, pool):
    def step(what, t, par, i):
        if what == "norm":
            pool.wait_ge(m.var_ready, t + 1)
            k.nc.gpsimd.tensor_tensor(m.rstd[:], m.mv[:, 1:2], k.minus_half[:, 0:1], ALU.pow).then_inc(m.rstd_ready, 1)
        if what == "post":
            pool.wait_ge(m.post_var, t + 1)
            k.nc.gpsimd.tensor_tensor(m.prstd[:], m.pmv[:, 1:2], k.minus_half[:, 0:1], ALU.pow).then_inc(m.post_rstd, 1)

    go_through(m, pool, step)




SLOTS = 80
RESULTS = 4
GATHERS = 4
ROW = D + 1
ZERO_FILLS = 10
assert SLOTS >= (2 * TILES * P + E * (P - 1)) // P


class Steps:

    def __init__(self, count, tile, lead, trail, each=2):
        self.count, self.tile, self.lead, self.trail, self.each = count, tile, lead, trail, each
        self.turns = (count - 4) // each
        assert self.turns * each == count - 4

    def head(self):
        yield from ((what, 0, 0) for what in self.lead)
        yield from self.tile(0, 0, True, False)
        yield from self.tile(1, 1, False, False)

    def pair(self, it):
        yield "turn_begins", None, None
        for j in range(self.each):
            yield from self.tile(self.each * it + 2 + j, j % 2, False, False)

    def rest(self):
        yield "turn_begins", None, None
        yield from self.tile(self.count - 2, 0, False, False)
        yield from self.tile(self.count - 1, 1, False, True)
        yield from ((what, self.count - 1, 1) for what in self.trail)


def router_tile(t, par, first, last):
    if not last:
        yield "norm", t + 1, 1 - par
        yield "turn_x", t + 1, 1 - par
    yield "logits", t, par


def shared_tile(t, par, first, last):
    if not last:
        yield "norm", t + 1, 1 - par
    yield "up0", t, par
    if not first:
        yield "turn", t - 1, 1 - par
    yield "up1", t, par
    if not last:
        yield "turn_x", t + 1, 1 - par
        yield "scatter", t + 1, 1 - par
    if not first:
        yield "down", t - 1, 1 - par


def block_tile(b, par, first, last):
    yield "up", b, par
    if not last:
        yield "turn_x", b + 1, 1 - par
        yield "fetch", b + 2, par
    if not first:
        yield "down", b - 1, 1 - par
    yield "turn", b, par


class SparseMoe:

    def __init__(self, k, inter, w_up, w_down, w_gate, loads, sorted_in, results):
        self.k, self.inter, self.w_up, self.w_down, self.w_gate, self.loads = k, inter, w_up, w_down, w_gate, loads
        self.sorted_in, self.results = sorted_in, results
        self.half = inter // 2
        self.shared_chunks = -(-2 * inter // P)
        self.finished = TILES // 2
        self.router = Steps(TILES, router_tile, ("norm", "turn_x"), ())
        self.shared = Steps(TILES, shared_tile, ("norm", "turn_x", "scatter"), ("turn", "down"))
        self.blocks = Steps(SLOTS, block_tile, ("fetch0", "fetch1", "turn_x"), ("down",), 4)
        self.zeroed = k.sem("moe0_zeroed")
        self.var_ready = k.sem("moe0_var_ready")
        self.rstd_ready = k.sem("moe0_rstd_ready")
        self.xn_ready = k.sem("moe0_xn_ready")
        self.xT_full = k.sem("moe0_xT_full")
        self.xT_ready = k.sem("moe0_xT_ready")
        self.logits_full = k.sem("moe0_logits_full")
        self.shift_ready = k.sem("moe0_shift_ready")
        self.exp_ready = k.sem("moe0_exp_ready")
        self.both_ready = k.sem("moe0_both_ready")
        self.ranks_full = k.sem("moe0_ranks_full")
        self.pos_ready = k.sem("moe0_pos_ready")
        self.table_ready = k.sem("moe0_table_ready")
        self.up_full = k.sem("moe0_up_full")
        self.silu_ready = k.sem("moe0_silu_ready")
        self.h_ready = k.sem("moe0_h_ready")
        self.hT_full = k.sem("moe0_hT_full")
        self.hT_ready = k.sem("moe0_hT_ready")
        self.y_full = k.sem("moe0_y_full")
        self.y_read = k.sem("moe0_y_read")
        self.place_ready = k.sem("moe0_place_ready")
        self.bup_full = k.sem("moe0_bup_full")
        self.bsilu_ready = k.sem("moe0_bsilu_ready")
        self.bh_ready = k.sem("moe0_bh_ready")
        self.by_ready = k.sem("moe0_by_ready")
        self.part_ready = k.sem("moe0_part_ready")
        self.gather_used = k.sem("moe0_gather_used")
        self.ystats_done = k.sem("moe0_ystats_done")
        self.z_ready = k.sem("moe0_z_ready")
        self.x_done = k.sem("moe0_x_done")
        self.dve_step = k.sem("moe0_dve_step")
        self.scattered = [k.sem(f"moe0_scattered{i}") for i in range(2)]
        self.fetched = [k.sem(f"moe0_fetched{i}") for i in range(2)]
        self.kept = [k.sem(f"moe0_kept{i}") for i in range(RESULTS)]
        self.gathered = [k.sem(f"moe0_gathered{i}") for i in range(GATHERS)]
        self.carried = k.sem("moe0_carried")
        self.ids_read = k.sem("moe0_ids_read")

    def buffers(self, sb):
        inter = self.inter
        self.stat = self.k.next_stat
        self.mean = sb("moe0_mean", [P, TILES])
        self.var = sb("moe0_var", [P, TILES])
        self.rstd = sb("moe0_rstd", [P, TILES])
        self.diff = sb("moe0_diff", [P, TILES])
        self.top = sb("moe0_top", [P, TILES])
        self.den = sb("moe0_den", [P, TILES])
        self.weight = sb("moe0_weight", [P, 2 * TILES])
        self.both = sb("moe0_both", [P, E * TILES], BF16)
        self.ends = sb("moe0_ends", [P, E + 1])
        self.need = sb("moe0_need", [P, E])
        self.need_i = sb("moe0_need_i", [P, E], I32)
        self.slot_ends = sb("moe0_slot_ends", [P, E + 1])
        self.base = sb("moe0_base", [P, E])
        self.places_f = sb("moe0_places_f", [P, TILES, 2])
        self.places = sb("moe0_places", [P, TILES * 2], U32)
        self.table_f = sb("moe0_table_f", [1, SLOTS])
        self.table = sb("moe0_table", [1, SLOTS], I32)
        self.place = sb("moe0_place", [P, GATHERS * 2], U32)
        self.xn = sb("moe0_xn", [P, 2, 2, ROW])
        self.xT = sb("moe0_xT", [P, 2, KD, P])
        self.silu = sb("moe0_silu", [P, 2, inter])
        self.h = sb("moe0_h", [P, 2, 2 * inter])
        self.hT = sb("moe0_hT", [P, 2, self.shared_chunks, P])
        self.rows = sb("moe0_rows", [P, 2, ROW])
        self.home = sb("moe0_home", [P, RESULTS], U32)
        self.result = sb("moe0_result", [P, RESULTS, D])
        self.got = sb("moe0_got", [P, GATHERS * 2 * D])
        self.y = sb("moe0_y", [P, TILES * D])
        tables = [self.y[:, i * TILES * E:(i + 1) * TILES * E] for i in range(6)]
        self.score, self.mark, *self.one = [x.rearrange("p (t e) -> p t e", e=E) for x in tables[:4]]
        self.ones_row, self.count = tables[4:]
        self.past = self.got[0:1, 0:SLOTS * E].rearrange("p (s e) -> p s e", e=E)


def sparse_tensor(k, m, pe):
    nc, inter = k.nc, m.inter
    for sem, count in m.loads:
        pe.wait_ge(sem, count)

    def turn(to, rows, done):
        for c in range(KD):
            last = nc.tensor.transpose(to[:, c * P:(c + 1) * P], rows[:, c * P:(c + 1) * P], k.ident[:])
        last.then_inc(done, 1)

    def router(what, t, par):
        if what == "turn_x":
            pe.wait_ge(m.xn_ready, t + 1)
            if begun(t - 1):
                pe.wait_ge(m.xT_ready, t - 1)
            turn(k.bank[:, par, :], m.xn[:, par, 0, :], m.xT_full)
        if what == "logits":
            pe.wait_ge(m.xT_ready, t + 1)
            for c in range(KD):
                last = nc.tensor.matmul(cols(k.bank[:, 7, :], t, E), m.xT[:, par, c, :], m.w_gate[:, c, :],
                                        start=(c == 0), stop=(c == KD - 1))
            last.then_inc(m.logits_full, 1)

    go_through(m.router, pe, router)

    pe.wait_ge(m.both_ready, 1)
    nc.tensor.matmul(k.bank[:, 4, :], k.before[:], m.both[:], start=True, stop=True)
    nc.tensor.matmul(k.bank[:, 5, :], k.all_ones[:], m.both[:], start=True, stop=True).then_inc(m.ranks_full, 1)
    pe.wait_ge(m.pos_ready, 1)

    def shared(what, t, par):
        if what == "turn_x":
            pe.wait_ge(m.xn_ready, TILES + t + 1)
            if begun(t - 1):
                pe.wait_ge(m.xT_ready, TILES + t - 1)
            turn(k.bank[:, par, :], m.xn[:, par, 0, :], m.xT_full)
        if what in ("up0", "up1"):
            i = int(what[2])
            pe.wait_ge(m.xT_ready, TILES + t + 1)
            if begun(2 * t + i - 1):
                pe.wait_ge(m.h_ready, 2 * t + i - 1)
            lo = (E + i) * 2 * inter
            for c in range(KD):
                last = nc.tensor.matmul(k.bank[:, 2 + i, 0:2 * inter], m.xT[:, par, c, :],
                                        m.w_up[:, c, lo:lo + 2 * inter], start=(c == 0), stop=(c == KD - 1))
            last.then_inc(m.up_full, 1)
        if what == "turn":
            pe.wait_ge(m.h_ready, 2 * t + 2)
            if begun(t - 1):
                pe.wait_ge(m.hT_ready, t - 1)
            for c in range(m.shared_chunks):
                w = min(P, 2 * inter - c * P)
                last = nc.tensor.transpose(k.bank[0:w, 4 + par, c * P:(c + 1) * P], m.h[:, par, c * P:c * P + w],
                                           k.ident[:])
            last.then_inc(m.hT_full, 1)
        if what == "down":
            pe.wait_ge(m.hT_ready, t + 1)
            if begun(t - 1):
                pe.wait_ge(m.y_read, t - 1)
            for c in range(m.shared_chunks):
                w = min(P, 2 * inter - c * P)
                last = nc.tensor.matmul(k.bank[:, 6 + par, 0:D], m.hT[0:w, par, c, :], m.w_down[0:w, 2 * E + c, :],
                                        start=(c == 0), stop=(c == m.shared_chunks - 1))
            last.then_inc(m.y_full, 1)

    go_through(m.shared, pe, shared)

    pe.wait_ge(m.y_read, TILES)
    pe.wait_ge(m.table_ready, 1)

    experts = [None]

    def load_expert(b):
        experts.append(pe.value_load(m.table[0:1, bass.ds(b, 1)], min_val=0, max_val=E - 1))

    done = [0]

    def block(what, b, par):
        if what == "turn_begins":
            experts.clear()
            done[0] = 0
        if what == "turn_x":
            pe.wait_ge(m.fetched[par], (b - par) * 8 + 16)
            if begun(b - 1):
                pe.wait_ge(m.xT_ready, 2 * TILES + b - 1)
            turn(k.bank[:, par, :], m.rows[:, par, :], m.xT_full)
        if what == "up":
            if not experts:
                load_expert(b - 1)
            if done[0] == 0:
                load_expert(b)
            done[0] += 1
            expert = experts[done[0]]
            pe.wait_ge(m.xT_ready, 2 * TILES + b + 1)
            if begun(b - 1):
                pe.wait_ge(m.bh_ready, b - 1)
            for c in range(KD):
                last = nc.tensor.matmul(k.bank[:, 2 + par, 0:2 * inter], m.xT[:, par, c, :],
                                        cols(m.w_up[:, c, :], expert, 2 * inter), start=(c == 0), stop=(c == KD - 1))
            last.then_inc(m.bup_full, 1)
            if done[0] < (2 if isinstance(b, int) else m.blocks.each):
                load_expert(b + 1)
        if what == "turn":
            pe.wait_ge(m.bh_ready, b + 1)
            if begun(b - 1):
                pe.wait_ge(m.hT_ready, TILES + b - 1)
            for c in range(2):
                last = nc.tensor.transpose(k.bank[0:m.half, 4 + par, c * P:(c + 1) * P],
                                           m.h[:, par, c * m.half:(c + 1) * m.half], k.ident[:])
            last.then_inc(m.hT_full, 1)
        if what == "down":
            expert = experts[done[0] if isinstance(b, int) and b == SLOTS - 1 else done[0] - 1]
            pe.wait_ge(m.hT_ready, TILES + b + 1)
            if begun(b - 1):
                pe.wait_ge(m.by_ready, b - 1)
            w_down = m.w_down[:].rearrange("p c d -> p (c d)")
            for c in range(2):
                last = nc.tensor.matmul(k.bank[:, 6 + par, 0:D], m.hT[0:m.half, par, c, :],
                                        w_down[0:m.half, bass.ds(expert * 2 * D + c * D, D)],
                                        start=(c == 0), stop=(c == 1))
            last.then_inc(m.y_full, 1)

    go_through(m.blocks, pe, block)


def sparse_scalar(k, m, act):
    nc, inter = k.nc, m.inter

    def router(what, t, par):
        if what == "turn_x":
            act.wait_ge(m.xT_full, t + 1)
            if begun(t - 1):
                act.wait_ge(m.logits_full, t - 1)
            nc.scalar.copy(m.xT[:, par, :, :].rearrange("p c t -> p (c t)"), k.bank[:, par, 0:D]).then_inc(m.xT_ready, 1)

    go_through(m.router, act, router)
    act.wait_ge(m.shift_ready, 1)
    nc.scalar.activation(m.score, m.score, ACT.Exp).then_inc(m.exp_ready, 1)

    def shared(what, t, par):
        if what == "turn_x":
            act.wait_ge(m.xT_full, TILES + t + 1)
            if begun(t - 1):
                act.wait_ge(m.up_full, 2 * t - 2)
            nc.scalar.copy(m.xT[:, par, :, :].rearrange("p c t -> p (c t)"), k.bank[:, par, 0:D]).then_inc(m.xT_ready, 1)
        if what in ("up0", "up1"):
            i = int(what[2])
            act.wait_ge(m.up_full, 2 * t + i + 1)
            if begun(2 * t + i - 1):
                act.wait_ge(m.h_ready, 2 * t + i - 1)
            nc.scalar.activation(m.silu[:, i, :], k.bank[:, 2 + i, 0:inter], ACT.Silu).then_inc(m.silu_ready, 1)
        if what == "turn":
            act.wait_ge(m.hT_full, t + 1)
            if begun(t - 1):
                act.wait_ge(m.y_full, t - 1)
            c, w = m.shared_chunks - 1, 2 * inter - (m.shared_chunks - 1) * P
            nc.scalar.copy(m.hT[:, par, 0:c, :].rearrange("p c t -> p (c t)"), k.bank[:, 4 + par, 0:c * P])
            nc.scalar.copy(m.hT[0:w, par, c, :], k.bank[0:w, 4 + par, c * P:(c + 1) * P]).then_inc(m.hT_ready, 1)
        if what == "down":
            act.wait_ge(m.y_full, t + 1)
            nc.scalar.copy(cols(m.y, t), k.bank[:, 6 + par, 0:D]).then_inc(m.y_read, 1)

    go_through(m.shared, act, shared)

    def block(what, b, par):
        if what == "turn_x":
            act.wait_ge(m.xT_full, 2 * TILES + b + 1)
            if begun(b - 1):
                act.wait_ge(m.bup_full, b - 1)
            nc.scalar.copy(m.xT[:, par, :, :].rearrange("p c t -> p (c t)"), k.bank[:, par, 0:D]).then_inc(m.xT_ready, 1)
        if what == "up":
            act.wait_ge(m.bup_full, b + 1)
            if begun(b - 1):
                act.wait_ge(m.bh_ready, b - 1)
            nc.scalar.activation(m.silu[:, par, :], k.bank[:, 2 + par, 0:inter], ACT.Silu).then_inc(m.bsilu_ready, 1)
        if what == "turn":
            act.wait_ge(m.hT_full, TILES + b + 1)
            if begun(b - 1):
                act.wait_ge(m.y_full, TILES + b - 1)
            nc.scalar.copy(m.hT[0:m.half, par, 0:2, :].rearrange("p c t -> p (c t)"),
                           k.bank[0:m.half, 4 + par, 0:2 * P]).then_inc(m.hT_ready, 1)

    go_through(m.blocks, act, block)

    act.wait_ge(m.shift_ready, 2)
    with act.Fori(0, TILES // 2) as it:
        for j in range(2):
            t = 2 * it + j
            nc.scalar.activation(cols(m.y, t), cols(m.y, t), ACT.Identity, bias=cols(m.diff, t, 1),
                                 scale=cols(m.rstd, t, 1)).then_inc(m.z_ready, 1)


def moments(k, m, link, done):
    v = k.nc.vector
    stat = m.stat[:].rearrange("p (t s) -> p t s", s=6)
    n = D // 2
    link(v.tensor_tensor(m.diff[:], stat[:, :, 1], stat[:, :, 4], ALU.subtract))
    link(v.scalar_tensor_tensor(m.diff[:], m.diff[:], float(n * n / D), m.diff[:], ALU.mult, ALU.mult))
    link(v.tensor_tensor(m.var[:], stat[:, :, 2], stat[:, :, 5], ALU.add))
    link(v.tensor_tensor(m.var[:], m.var[:], m.diff[:], ALU.add))
    link(v.tensor_tensor(m.mean[:], stat[:, :, 1], stat[:, :, 4], ALU.add))
    link(v.tensor_scalar(m.mean[:], m.mean[:], 0.5, None, ALU.mult))
    v.tensor_scalar(m.var[:], m.var[:], 1.0 / D, EPS, ALU.mult, ALU.add).then_inc(done, 1)


def sparse_vector(k, m, dve):
    nc, v, inter = k.nc, k.nc.vector, m.inter
    chain = Chain(dve, m.dve_step)
    link = chain.link

    dve.wait_ge(k.next_stats, SEQS)
    moments(k, m, link, m.var_ready)
    dve.wait_ge(m.rstd_ready, 1)

    def normalise(t, par, j=0):
        return v.tensor_scalar(m.xn[:, par, j, 0:D], cols(k.x, t), cols(m.mean, t, 1), cols(m.rstd, t, 1),
                               ALU.subtract, ALU.mult)

    def router(what, t, par):
        if what == "norm":
            if begun(t - 1):
                dve.wait_ge(m.xT_full, t - 1)
            normalise(t, par).then_inc(m.xn_ready, 1)

    go_through(m.router, dve, router)

    dve.wait_ge(m.logits_full, TILES)
    per_tile = lambda x: x.unsqueeze(2).to_broadcast([P, TILES, E])
    per_expert = lambda x: x.unsqueeze(1).to_broadcast([P, TILES, E])
    logits = k.bank[:, 7, :].rearrange("p (t e) -> p t e", e=E)
    link(v.tensor_reduce(m.top[:], logits, AX.X, ALU.max))
    v.tensor_tensor(m.score, logits, per_tile(m.top[:]), ALU.subtract).then_inc(m.shift_ready, 1)
    dve.wait_ge(m.exp_ready, 1)
    link(v.tensor_reduce(m.den[:], m.score, AX.X, ALU.add))
    link(v.reciprocal(m.den[:], m.den[:]))
    link(v.tensor_tensor(m.score, m.score, per_tile(m.den[:]), ALU.mult))
    for j in range(2):
        weight = m.weight[:, j * TILES:(j + 1) * TILES]
        link(v.tensor_reduce(weight, m.score, AX.X, ALU.max))
        link(v.tensor_tensor(m.mark, m.score, per_tile(weight), ALU.is_equal))
        link(v.tensor_tensor(m.mark, m.mark, per_expert(k.expert_rank[:]), ALU.mult))
        link(v.tensor_reduce(m.top[:], m.mark, AX.X, ALU.max))
        link(v.tensor_tensor(m.one[j], per_expert(k.expert_rank[:]), per_tile(m.top[:]), ALU.is_equal))
        if j == 0:
            link(v.scalar_tensor_tensor(m.score, m.one[0], -2.0, m.score, ALU.mult, ALU.add))
    by_expert = lambda x: x.rearrange("p (e t) -> p t e", e=E)
    v.tensor_tensor(by_expert(m.both[:]), m.one[0], m.one[1], ALU.add).then_inc(m.both_ready, 1)

    dve.wait_ge(m.ranks_full, 1)
    link(v.memset(m.ones_row, 1.0))
    link(v.memset(m.ends[:], 0.0))
    link(v.memset(m.slot_ends[:], 0.0))
    link(v.tensor_tensor_scan(m.count, m.ones_row, k.bank[:, 5, :], 0.0, ALU.mult, ALU.add))
    link(v.tensor_copy(m.ends[:, 1:E + 1], m.count.rearrange("p (e t) -> p e t", e=E)[:, :, TILES - 1]))
    link(v.tensor_tensor(m.need[:], m.ends[:, 1:E + 1], m.ends[:, 0:E], ALU.subtract))
    link(v.tensor_scalar(m.need[:], m.need[:], float(P - 1), None, ALU.add))
    link(v.tensor_copy(m.need_i[:], m.need[:]))
    link(v.tensor_scalar(m.need_i[:], m.need_i[:], P.bit_length() - 1, None, ALU.arith_shift_right))
    link(v.tensor_copy(m.need[:], m.need_i[:]))
    link(v.tensor_tensor_scan(m.slot_ends[:, 1:E + 1], m.ones_row[:, 0:E], m.need[:], 0.0, ALU.mult, ALU.add))
    link(v.scalar_tensor_tensor(m.base[:], m.slot_ends[:, 0:E], float(P), m.ends[:, 0:E], ALU.mult, ALU.subtract))
    link(v.tensor_tensor(m.count, m.count, k.bank[:, 5, :], ALU.subtract))
    link(v.tensor_tensor(m.count, m.count, k.bank[:, 4, :], ALU.add))
    count = m.count.rearrange("p (e t) -> p e t", e=E)
    link(v.tensor_tensor(count, count, m.base[:].unsqueeze(2).to_broadcast([P, E, TILES]), ALU.add))
    for j in range(2):
        link(v.tensor_tensor(m.mark, m.one[j], by_expert(m.count), ALU.mult))
        link(v.tensor_reduce(m.places_f[:, :, j], m.mark, AX.X, ALU.add))
    v.tensor_copy(m.places[:], m.places_f[:].rearrange("p t j -> p (t j)")).then_inc(m.pos_ready, 1)

    def shared(what, t, par):
        if what == "norm":
            if begun(t - 1):
                dve.wait_ge(m.xT_full, TILES + t - 1)
                dve.wait_ge(m.scattered[par], (t - par) * 16)
            normalise(t, par)
            normalise(t, par, 1)
            v.tensor_copy(m.xn[:, par, :, D].bitcast(U32), cols(k.pair_no, t, 2)).then_inc(m.xn_ready, 1)
        if what in ("up0", "up1"):
            i = int(what[2])
            dve.wait_ge(m.silu_ready, 2 * t + i + 1)
            if i == 0:
                if begun(t - 1):
                    dve.wait_ge(m.hT_full, t - 1)
            v.tensor_tensor(m.h[:, par, i * inter:(i + 1) * inter], m.silu[:, i, :],
                            k.bank[:, 2 + i, inter:2 * inter], ALU.mult).then_inc(m.h_ready, 1)

    go_through(m.shared, dve, shared)

    ends = m.slot_ends[0:1, 1:E + 1].unsqueeze(1).to_broadcast([1, SLOTS, E])
    link(v.tensor_tensor(m.past, ends, k.slot_no[0:1, :].unsqueeze(2).to_broadcast([1, SLOTS, E]), ALU.is_le))
    link(v.tensor_reduce(m.table_f[:], m.past, AX.X, ALU.add))
    link(v.tensor_scalar(m.table_f[:], m.table_f[:], float(E - 1), None, ALU.min))
    v.tensor_copy(m.table[:], m.table_f[:]).then_inc(m.table_ready, 1)

    seen = [0]

    def block(what, b, par):
        if what == "up":
            r = seen[0] % RESULTS
            seen[0] += 1
            dve.wait_ge(m.bsilu_ready, b + 1)
            if begun(b - 1):
                dve.wait_ge(m.hT_full, TILES + b - 1)
            v.tensor_tensor(m.h[:, par, 0:inter], m.silu[:, par, :], k.bank[:, 2 + par, inter:2 * inter],
                            ALU.mult).then_inc(m.bh_ready, 1)
            if begun(b - RESULTS + 1):
                dve.wait_ge(m.kept[r], (b - r) * 4)
            v.tensor_copy(m.home[:, r:r + 1], m.rows[:, par, D:ROW].bitcast(U32)).then_inc(m.ids_read, 1)
        if what == "down":
            dve.wait_ge(m.y_full, TILES + b + 1)
            r = (seen[0] - (1 if isinstance(b, int) and b == SLOTS - 1 else 2)) % RESULTS
            v.tensor_copy(m.result[:, r, :], k.bank[:, 6 + par, 0:D]).then_inc(m.by_ready, 1)

    go_through(m.blocks, dve, block)

    dve.wait_ge(m.y_read, TILES)

    def combine(turn):
        tiles = [(GATHERS * turn + q, m.got[:, 2 * q * D:(2 * q + 1) * D], m.got[:, (2 * q + 1) * D:(2 * q + 2) * D])
                 for q in range(GATHERS)]
        for q, (t, first, _) in enumerate(tiles):
            dve.wait_ge(m.gathered[q], 16 * turn + 16)
            v.scalar_tensor_tensor(cols(m.y, t), first, cols(m.weight, t, 1), cols(m.y, t),
                                   ALU.mult, ALU.add).then_inc(m.part_ready, 1)
        for t, _, second in tiles:
            dve.wait_ge(m.part_ready, t + 1)
            v.scalar_tensor_tensor(cols(m.y, t), second, cols(m.weight, t + TILES, 1), cols(m.y, t),
                                   ALU.mult, ALU.add).then_inc(m.gather_used, 1)
        for t, _, _ in tiles:
            dve.wait_ge(m.gather_used, t + 1)
            v.bn_stats(cols(m.stat, t, 6), cols(m.y, t)).then_inc(m.ystats_done, 1)

    with dve.Fori(0, TILES // GATHERS) as turn:
        combine(turn)
    dve.wait_ge(m.ystats_done, TILES)
    moments(k, m, link, m.var_ready)
    dve.wait_ge(m.rstd_ready, 2)
    v.scalar_tensor_tensor(m.diff[:], m.mean[:], -1.0, m.rstd[:], ALU.mult, ALU.mult).then_inc(m.shift_ready, 1)
    with dve.Fori(0, TILES // 2) as it:
        dve.wait_ge(m.z_ready, 2 * it + 2)
        v.tensor_tensor(cols(k.x, it, 2 * D), cols(k.x, it, 2 * D), cols(m.y, it, 2 * D), ALU.add).then_inc(m.x_done, 1)
    dve.wait_ge(m.x_done, m.finished)


def sparse_pool(k, m, pool):
    nc, g = k.nc, k.nc.gpsimd
    pool.wait_ge(m.var_ready, 1)
    g.tensor_tensor(m.rstd[:], m.var[:], k.minus_half[:], ALU.pow).then_inc(m.rstd_ready, 1)
    pool.wait_ge(m.pos_ready, 1)
    pool.wait_ge(m.zeroed, 2 * 16 * ZERO_FILLS)

    def shared(what, t, par):
        if what == "scatter":
            pool.wait_ge(m.xn_ready, TILES + t + 1)
            g.tensor_copy(m.place[:, 2 * par:2 * par + 2], cols(m.places, t, 2)).then_inc(m.place_ready, 1)
            pool.wait_ge(m.place_ready, t + 1)
            g.tensor_tensor(k.pool_spare[:, 0:1], k.minus_half[:, 0:1], k.minus_half[:, 0:1], ALU.add)
            for j in range(2):
                at = bass.IndirectOffsetOnAxis(m.place[:, 2 * par + j:2 * par + j + 1], 0)
                g.indirect_dma_start(m.sorted_in, at, m.xn[:, par, j, :], None).then_inc(m.scattered[par], 16)

    go_through(m.shared, pool, shared)

    sent = [0]

    def block(what, b, par):
        if what == "down":
            r = sent[0] % RESULTS
            sent[0] += 1
            pool.wait_ge(m.by_ready, b + 1)
            if begun(b):
                pool.wait_ge(m.carried, b)
            g.tensor_tensor(k.pool_spare[:, 1:2], k.minus_half[:, 0:1], k.minus_half[:, 0:1], ALU.add).then_inc(m.carried, 1)
            g.indirect_dma_start(m.results, bass.IndirectOffsetOnAxis(m.home[:, r:r + 1], 0), m.result[:, r, :],
                                 None).then_inc(m.kept[r], 16)

    go_through(m.blocks, pool, block)
    pool.wait_ge(m.var_ready, 2)
    g.tensor_tensor(m.rstd[:], m.var[:], k.minus_half[:], ALU.pow).then_inc(m.rstd_ready, 1)


def sparse_sync(k, m, sp):
    for par in range(2):
        sp.wait_ge(m.scattered[par], 16 * TILES)
    sorted_in = m.sorted_in.rearrange("(s p) d -> s p d", p=P)
    results = m.results[0:2 * TILES * P].rearrange("(t p j) d -> t p (j d)", p=P, j=2)

    def block(what, b, par):
        if what in ("fetch0", "fetch1"):
            i = int(what[5])
            sp.dma_start(m.rows[:, i, :], sorted_in[i]).then_inc(m.fetched[i], 16)
        if what == "fetch" and not (isinstance(b, int) and b >= SLOTS):
            sp.wait_ge(m.ids_read, b - 1)
            sp.dma_start(m.rows[:, par, :], sorted_in[bass.ds(b, 1)].rearrange("o p d -> p (o d)")).then_inc(m.fetched[par], 16)

    go_through(m.blocks, sp, block)
    for kept in m.kept:
        sp.wait_ge(kept, 16 * SLOTS // RESULTS)

    def fetch(turn, first):
        for q in range(GATHERS):
            t = GATHERS * turn + q
            if not first:
                sp.wait_ge(m.gather_used, t - GATHERS + 1)
            src = results[t] if first else results[bass.ds(t, 1)].rearrange("o p d -> p (o d)")
            sp.dma_start(m.got[:, 2 * q * D:2 * (q + 1) * D], src).then_inc(m.gathered[q], 16)

    fetch(0, True)
    with sp.Fori(1, TILES // GATHERS) as turn:
        fetch(turn, False)
HEADS, KV = 16, 4
HD = D // HEADS
REP = HEADS // KV
SLOT = 32
NQ = HEADS * HD
NKV = KV * HD
NQK = NQ + NKV
NQKV = NQ + 2 * NKV
SCALE = float(HD) ** -0.5
MASKED = -1e30
OW = SLOT


class Attention:

    def __init__(self, k, a):
        self.k, self.a = k, a
        self.loaded = k.sem("attn_loaded")
        self.tables = k.sem("attn_tables")
        self.tables_step = k.sem("attn_tables_step")
        self.var_ready = k.sem("attn_var_ready")
        self.rstd_ready = k.sem("attn_rstd_ready")
        self.xn_ready = k.sem("attn_xn_ready")
        self.xT_full = k.sem("attn_xT_full")
        self.xT_ready = k.sem("attn_xT_ready")
        self.qkv_full = k.sem("attn_qkv_full")
        self.qkv_read = k.sem("attn_qkv_read")
        self.rope_ready = k.sem("attn_rope_ready")
        self.qT_full = k.sem("attn_qT_full")
        self.qT_ready = k.sem("attn_qT_ready")
        self.kT_full = k.sem("attn_kT_full")
        self.kT_ready = k.sem("attn_kT_ready")
        self.scores_full = k.sem("attn_scores_full")
        self.max_ready = k.sem("attn_max_ready")
        self.qm_ready = k.sem("attn_qm_ready")
        self.qmT_full = k.sem("attn_qmT_full")
        self.qmT_ready = k.sem("attn_qmT_ready")
        self.probs_full = k.sem("attn_probs_full")
        self.probs_ready = k.sem("attn_probs_ready")
        self.probs_used = k.sem("attn_probs_used")
        self.av_copied = k.sem("attn_av_copied")
        self.av_turned = k.sem("attn_av_turned")
        self.att_ready = k.sem("attn_att_ready")
        self.attT_full = k.sem("attn_attT_full")
        self.attT_ready = k.sem("attn_attT_ready")
        self.proj_full = k.sem("attn_proj_full")
        self.post_var = k.sem("attn_post_var")
        self.post_rstd = k.sem("attn_post_rstd")
        self.proj_used = k.sem("attn_proj_used")
        self.x_done = k.sem("attn_x_done")
        self.dve_step = k.sem("attn_dve_step")

    def weights(self, sb):
        self.w_qkv = sb("w_qkv", [P, KD, NQKV])
        self.b_qkv = sb("b_qkv", [P, NQKV])
        self.w_o = sb("w_o", [P, KD, D])
        self.b_o = sb("b_o", [P, D])
        self.cos = sb("cos", [P, SEQ_TILES, HD])
        self.sin = sb("sin", [P, SEQ_TILES, 2, HD // 2])

    def buffers(self, sb):
        self.mask_q = sb("mask_q", [P, REP, P], BF16)
        self.mask_k = sb("mask_k", [P, REP, P], BF16)
        self.stat = sb("attn_stat", [P, SEQ_TILES, 6])
        self.mv = sb("attn_mv", [P, SEQ_TILES, 2])
        self.rstd = sb("attn_rstd", [P, SEQ_TILES])
        self.pstat = sb("attn_pstat", [P, SEQ_TILES, 6])
        self.pmv = sb("attn_pmv", [P, SEQ_TILES, 2])
        self.prstd = sb("attn_prstd", [P, SEQ_TILES])
        self.xn = sb("attn_xn", [P, SEQ_TILES, D])
        self.xT = sb("attn_xT", [P, KD, S])
        self.qkv = sb("attn_qkv", [P, SEQ_TILES, NQKV])
        self.rot_a = sb("rot_a", [P, NQK])
        self.rot_b = sb("rot_b", [P, NQK])
        self.q = sb("q_slots", [P, 2, SEQ_TILES, REP, KV, SLOT])
        self.kk = sb("k_slots", [P, SEQ_TILES, KV, SLOT])
        self.v = sb("v_slots", [P, 2, SEQ_TILES, KV, OW])
        self.qT = sb("qT", [P, 2, SEQ_TILES, REP, P])
        self.kT = sb("kT", [P, 2, KV, S])
        self.qmT = sb("qmT", [P, SEQ_TILES, REP, P])
        self.probs = sb("probs", [P, 2, SEQ_TILES, REP, P])
        self.rden = sb("rden", [P, SEQ_TILES, HEADS])
        self.avT = sb("avT", [P, SEQ_TILES, REP, P])
        self.att = sb("att", [P, SEQ_TILES, D])
        self.attT = sb("attT", [P, KD, S])
        self.y = sb("attn_y", [P, SEQ_TILES, D])

    def load(self, sp):
        a = self.a
        for dst, src in ((self.w_qkv[:], a["w_qkv"].rearrange("c p n -> p c n")), (self.b_qkv[:], a["b_qkv"]),
                         (self.w_o[:], a["w_o"].rearrange("c p n -> p c n")), (self.b_o[:], a["b_o"]),
                         (self.cos[:], a["cos"]), (self.sin[:], a["sin"])):
            sp.dma_start(dst, src).then_inc(self.loaded, 16)

    LOADS = 6 * 16


def attention_layout(i):
    def rows(v):
        return np.broadcast_to(v, (P, v.shape[0]))

    w = np.concatenate([i["L0_attn_Wq"], i["L0_attn_Wk"], i["L0_attn_Wv"]]).T
    b = np.concatenate([i["L0_attn_bq"], i["L0_attn_bk"], i["L0_attn_bv"]])
    inv = (np.float32(1.0) / np.float32(10000.0) ** (np.arange(0, HD, 2, dtype=np.float32) / np.float32(HD)))
    freqs = np.arange(S, dtype=np.float32)[:, None] * inv.astype(np.float32)[None, :]
    cos = np.repeat(np.cos(freqs), 2, axis=-1).reshape(SEQ_TILES, P, HD).transpose(1, 0, 2)
    sin = np.sin(freqs).reshape(SEQ_TILES, P, HD // 2).transpose(1, 0, 2)
    return {
        "w_qkv": w.reshape(KD, P, NQKV), "b_qkv": rows(b),
        "w_o": i["L0_attn_Wo"].T.reshape(KD, P, D), "b_o": rows(i["L0_attn_bo"]),
        "cos": cos.astype(np.float32), "sin": np.stack([-sin, sin], axis=2).astype(np.float32),
    }


SEQS = B
PAIR = 2
UNITS = 3 * KV // PAIR


def unit(i):
    turn, pair = divmod(i, KV // PAIR)
    return min(turn, 1), max(turn - 1, 0), range(pair * PAIR, (pair + 1) * PAIR)


ORDER = (
    (0, "scores", 0), (0, "scores", 1), (0, "scores", 2), (0, "turn_m", 0), (-1, "att", 0), (-1, "turn_av", 1),
    (0, "scores", 3), (0, "scores", 4), (-1, "turn_att", 0), (1, "norm", 0), (0, "scores", 5), (-1, "proj", 0),
    (0, "probs", 0), (-1, "post", 0), (1, "turn_x", 0), (0, "probs", 1), (0, "turn_m", 1), (1, "qkv", 0),
    (0, "av", 0), (0, "probs", 2), (1, "rope", 0), (0, "av", 1), (0, "copy_av", 0), (0, "probs", 3), (1, "qkv", 1),
    (0, "av", 2), (0, "av", 3), (0, "probs", 4), (0, "turn_av", 0), (1, "rope", 1), (1, "turn_q", 0), (0, "probs", 5),
    (1, "turn_k", 0), (1, "turn_q", 1), (0, "av", 4), (0, "av", 5), (0, "copy_av", 1),
)


def attention_order(t, par, first, last):
    for ahead, what, i in ORDER:
        if not (ahead == -1 and first or ahead == 1 and last):
            yield what, t + ahead, (par + ahead) % 2, i


def attention_head(self):
    for what, i in (("norm", 0), ("turn_x", 0), ("qkv", 0), ("rope", 0), ("qkv", 1), ("rope", 1),
                    ("turn_q", 0), ("turn_q", 1), ("turn_k", 0)):
        yield what, 0, 0, i
    yield from attention_order(0, 0, True, False)
    yield from attention_order(1, 1, False, False)


def attention_pair(self, it):
    yield from attention_order(2 * it + 2, 0, False, False)
    yield from attention_order(2 * it + 3, 1, False, False)


def attention_rest(self):
    yield from attention_order(SEQS - 2, 0, False, False)
    yield from attention_order(SEQS - 1, 1, False, True)
    for what, i in (("turn_av", 1), ("att", 0), ("turn_att", 0), ("proj", 0), ("post", 0)):
        yield what, SEQS - 1, 1, i


Attention.head, Attention.pair, Attention.rest = attention_head, attention_pair, attention_rest
Attention.turns = (SEQS - 4) // 2
Attention.finished = SEQS


def is_last(t, n):
    return isinstance(t, int) and t == n - 1


def attention_tensor(k, m, pe):
    nc = k.nc

    def step(what, t, par, i):
        qb, half, heads = unit(i)
        if what == "turn_x":
            pe.wait_ge(m.xn_ready, t + 1)
            if begun(t - 1):
                pe.wait_ge(m.attT_ready, t - 1)
            for c in range(KD):
                for j in range(SEQ_TILES):
                    last = nc.tensor.transpose(k.bank[:, 6, (c * SEQ_TILES + j) * P:(c * SEQ_TILES + j + 1) * P],
                                               m.xn[:, j, c * P:(c + 1) * P], k.ident[:])
            last.then_inc(m.xT_full, 1)
        if what == "qkv":
            pe.wait_ge(m.xT_ready, t + 1)
            if begun(2 * t + i):
                pe.wait_ge(m.qkv_read, 2 * t + i)
            for c in range(KD):
                last = nc.tensor.matmul(k.bank[:, 6, 0:NQKV], m.xT[:, c, i * P:(i + 1) * P], m.w_qkv[:, c, :],
                                        start=(c == 0), stop=(c == KD - 1))
            last.then_inc(m.qkv_full, 1)
        if what == "turn_q":
            pe.wait_ge(m.rope_ready, 2 * t + i + 1)
            if i == 0:
                if begun(2 * t):
                    pe.wait_ge(m.qmT_ready, 2 * t)
            else:
                pe.wait_ge(m.qkv_read, 2 * t + 2)
            for r in range(REP):
                last = nc.tensor.transpose(k.bank[:, 7 - i, r * P:(r + 1) * P],
                                           m.q[:, par, i, r].rearrange("p g s -> p (g s)"), k.ident[:])
            last.then_inc(m.qT_full, 1)
        if what == "turn_k":
            pe.wait_ge(m.rope_ready, 2 * t + 2)
            pe.wait_ge(m.qT_ready, 2 * t + 1)
            for j in range(SEQ_TILES):
                last = nc.tensor.transpose(k.bank[:, 7, j * P:(j + 1) * P],
                                           m.kk[:, j].rearrange("p g s -> p (g s)"), k.ident[:])
            last.then_inc(m.kT_full, 1)
        if what == "scores":
            pe.wait_ge(m.qT_ready, 2 * t + qb + 1)
            pe.wait_ge(m.kT_ready, t + 1)
            if i < 2:
                if begun(UNITS * t + i - 1):
                    pe.wait_ge(m.probs_ready, UNITS * t + i - 1)
            else:
                if begun(UNITS * t + i - 1):
                    pe.wait_ge(m.max_ready, UNITS * t + i - 1)
            keys, per = (qb + 1) * P, REP // (qb + 1)
            to = [k.bank[:, g, :].rearrange("p (r n) -> p r n", r=per) for g in heads]
            for x in to:
                nc.tensor.matmul(x[:, :, keys - P:keys], k.ident_b[:], m.mask_q[:, 0:per, :], start=True, stop=False,
                                 skip_group_check=True)
            for r in range(per):
                for g, x in zip(heads, to):
                    last = nc.tensor.matmul(x[:, r, :], m.qT[:, par, qb, half * per + r, :],
                                            m.kT[:, par, g, 0:keys], start=False, stop=(r == per - 1),
                                            skip_group_check=True)
            last.then_inc(m.scores_full, 1)
        if what == "turn_m":
            pe.wait_ge(m.max_ready, UNITS * t + (UNITS if i else KV // PAIR))
            if i == 0:
                pe.wait_ge(m.kT_ready, t + 1)
            else:
                pe.wait_ge(m.qmT_ready, 2 * t + 1)
            for r in range(REP):
                last = nc.tensor.transpose(k.bank[:, 7, r * P:(r + 1) * P],
                                           m.q[:, par, i, r].rearrange("p g s -> p (g s)"), k.ident[:])
            last.then_inc(m.qmT_full, 1)
        if what == "probs":
            pe.wait_ge(m.qmT_ready, 2 * t + qb + 1)
            if i < 2:
                if begun(UNITS * t + UNITS - 1 + i):
                    pe.wait_ge(m.max_ready, UNITS * t + UNITS - 1 + i)
            else:
                if begun(UNITS * t + i - 1):
                    pe.wait_ge(m.probs_ready, UNITS * t + i - 1)
            masked = half == qb
            for g in heads:
                if masked:
                    nc.tensor.matmul(k.bank[:, g, :], k.ident_b[:], m.mask_k[:].rearrange("p r n -> p (r n)"),
                                     start=True, stop=False, skip_group_check=True)
            for g in heads:
                last = nc.tensor.matmul(k.bank[:, g, :], m.kT[:, par, g, half * P:(half + 1) * P],
                                        m.qmT[:, qb].rearrange("p r n -> p (r n)"), start=not masked, stop=True,
                                        skip_group_check=True)
            last.then_inc(m.probs_full, 1)
        if what == "av":
            pe.wait_ge(m.probs_ready, UNITS * t + i + 1)
            if i == 0:
                if begun(t):
                    pe.wait_ge(m.proj_used, t)
            for g in heads:
                last = nc.tensor.matmul(k.bank[OW * g:OW * (g + 1), 4 + qb, :], m.v[:, par, half, g, :],
                                        m.probs[:, i % 2, g % PAIR].rearrange("p r n -> p (r n)"),
                                        start=(half == 0), stop=(half == qb), skip_group_check=True)
            last.then_inc(m.probs_used, 1)
        if what == "turn_av":
            pe.wait_ge(m.av_copied, 2 * t + i + 1)
            for r in range(REP):
                last = nc.tensor.transpose(k.bank[:, 4 + i, r * P:(r + 1) * P], m.avT[:, i, r, :], k.ident[:])
            last.then_inc(m.av_turned, 1)
        if what == "turn_att":
            pe.wait_ge(m.att_ready, t + 1)
            if is_last(t, SEQS):
                if begun(t):
                    pe.wait_ge(m.attT_ready, t)
            else:
                pe.wait_ge(m.qT_ready, 2 * t + 4)
            for c in range(KD):
                for j in range(SEQ_TILES):
                    last = nc.tensor.transpose(k.bank[:, 6, (c * SEQ_TILES + j) * P:(c * SEQ_TILES + j + 1) * P],
                                               m.att[:, j, c * P:(c + 1) * P], k.ident[:])
            last.then_inc(m.attT_full, 1)
        if what == "proj":
            pe.wait_ge(m.attT_ready, t + 1)
            for j in range(SEQ_TILES):
                for c in range(KD):
                    last = nc.tensor.matmul(k.bank[:, 4, j * D:(j + 1) * D], m.attT[:, c, j * P:(j + 1) * P],
                                            m.w_o[:, c, :], start=(c == 0), stop=(c == KD - 1))
            last.then_inc(m.proj_full, 1)

    pe.wait_ge(m.loaded, m.LOADS)
    pe.wait_ge(m.tables, 5)
    go_through(m, pe, step)


def attention_scalar(k, m, act):
    nc = k.nc
    act.wait_ge(m.tables, 5)

    def step(what, t, par, i):
        if what == "turn_x":
            act.wait_ge(m.xT_full, t + 1)
            if begun(2 * t):
                act.wait_ge(m.qkv_full, 2 * t)
            nc.scalar.copy(m.xT[:].rearrange("p c t -> p (c t)"), k.bank[:, 6, :]).then_inc(m.xT_ready, 1)
        if what == "turn_q":
            act.wait_ge(m.qT_full, 2 * t + i + 1)
            if begun(UNITS * (t - 1)):
                act.wait_ge(m.scores_full, UNITS * (t - 1))
            nc.scalar.copy(m.qT[:, par, i].rearrange("p r n -> p (r n)"), k.bank[:, 7 - i, :]).then_inc(m.qT_ready, 1)
        if what == "turn_k":
            act.wait_ge(m.kT_full, t + 1)
            if begun(UNITS * (t - 1)):
                act.wait_ge(m.probs_full, UNITS * (t - 1))
            for g in range(KV):
                rows = slice(SLOT * g, SLOT * (g + 1))
                last = nc.scalar.copy(m.kT[rows, par, g, :], k.bank[rows, 7, 0:S])
            last.then_inc(m.kT_ready, 1)
        if what == "turn_m":
            act.wait_ge(m.qmT_full, 2 * t + i + 1)
            if begun(UNITS * t):
                act.wait_ge(m.probs_full, UNITS * t)
            nc.scalar.copy(m.qmT[:, i].rearrange("p r n -> p (r n)"), k.bank[:, 7, :]).then_inc(m.qmT_ready, 1)
        if what == "probs":
            n = UNITS * t + i
            act.wait_ge(m.probs_full, n + 1)
            if begun(n - 1):
                act.wait_ge(m.probs_used, n - 1)
            heads = unit(i)[2]
            nc.scalar.activation(m.probs[:, i % 2].rearrange("p g r n -> p (g r n)"),
                                 k.bank[:, heads[0]:heads[0] + PAIR, :].rearrange("p b n -> p (b n)"),
                                 ACT.Exp, scale=SCALE).then_inc(m.probs_ready, 1)
        if what == "copy_av":
            act.wait_ge(m.probs_used, UNITS * t + (UNITS if i else KV // PAIR))
            if begun(2 * t + i - 1):
                act.wait_ge(m.av_turned, 2 * t + i - 1)
            nc.scalar.copy(m.avT[:, i].rearrange("p r n -> p (r n)"), k.bank[:, 4 + i, :]).then_inc(m.av_copied, 1)
        if what == "turn_att":
            act.wait_ge(m.attT_full, t + 1)
            if begun(t):
                act.wait_ge(m.proj_full, t)
            nc.scalar.copy(m.attT[:].rearrange("p c t -> p (c t)"), k.bank[:, 6, :]).then_inc(m.attT_ready, 1)

    go_through(m, act, step)


def attention_vector(k, m, dve):
    nc = k.nc
    v = nc.vector
    chain = Chain(dve, m.dve_step)
    link = chain.link

    def step(what, t, par, i):
        if what == "norm":
            if isinstance(t, int) and t == SEQS_FIRST:
                dve.wait_ge(k.x_loaded, 16 * REST_LOADS)
            for j in range(SEQ_TILES):
                last = v.bn_stats(m.stat[:, j, :], cols(k.x, SEQ_TILES * t + j))
            link(last)
            own_wait(k, dve)
            for j in range(SEQ_TILES):
                last = v.bn_aggr(m.mv[:, j, :], m.stat[:, j, :])
            link(last)
            v.tensor_scalar(m.mv[:, :, 1], m.mv[:, :, 1], EPS, None, ALU.add).then_inc(m.var_ready, 1)
            dve.wait_ge(m.rstd_ready, t + 1)
            if begun(t):
                dve.wait_ge(m.xT_full, t)
            for j in range(SEQ_TILES):
                last = v.tensor_scalar(m.xn[:, j, :], cols(k.x, SEQ_TILES * t + j), m.mv[:, j, 0:1], m.rstd[:, j:j + 1],
                                       ALU.subtract, ALU.mult)
            last.then_inc(m.xn_ready, 1)
        if what == "rope":
            dve.wait_ge(m.qkv_full, 2 * t + i + 1)
            v.tensor_tensor(m.qkv[:, i, :], k.bank[:, 6, 0:NQKV], m.b_qkv[:], ALU.add).then_inc(m.qkv_read, 1)
            dve.wait_ge(m.qkv_read, 2 * t + i + 1)
            N = NQK // HD
            qk = m.qkv[:, i, 0:NQK]
            pairs = qk.rearrange("p (h f two) -> p h f two", h=N, two=2)
            rot_b = m.rot_b[:].rearrange("p (h f two) -> p h f two", h=N, two=2)
            v.tensor_tensor(m.rot_a[:].rearrange("p (h f) -> p h f", h=N), qk.rearrange("p (h f) -> p h f", h=N),
                            m.cos[:, i:i + 1, :].to_broadcast([P, N, HD]), ALU.mult)
            v.tensor_tensor(rot_b[:, :, :, 0], pairs[:, :, :, 1],
                            m.sin[:, i, 0:1, :].to_broadcast([P, N, HD // 2]), ALU.mult)
            link(v.tensor_tensor(rot_b[:, :, :, 1], pairs[:, :, :, 0],
                                 m.sin[:, i, 1:2, :].to_broadcast([P, N, HD // 2]), ALU.mult))
            if begun(2 * (t - 1)):
                dve.wait_ge(m.qmT_full, 2 * (t - 1))
            if begun(t):
                dve.wait_ge(m.kT_full, t)
            if begun(UNITS * (t - 1)):
                dve.wait_ge(m.probs_used, UNITS * (t - 1))
            for g in range(KV):
                sl = slice(g * REP * HD, (g + 1) * REP * HD)
                v.tensor_tensor(m.q[:, par, i, :, g, 0:HD], m.rot_a[:, sl].rearrange("p (r f) -> p r f", r=REP),
                                m.rot_b[:, sl].rearrange("p (r f) -> p r f", r=REP), ALU.add)
            v.tensor_tensor(m.kk[:, i, :, 0:HD], m.rot_a[:, NQ:NQK].rearrange("p (g f) -> p g f", g=KV),
                            m.rot_b[:, NQ:NQK].rearrange("p (g f) -> p g f", g=KV), ALU.add)
            v.tensor_copy(m.v[:, par, i, :, 0:HD], m.qkv[:, i, NQK:NQKV].rearrange("p (g f) -> p g f", g=KV))\
                .then_inc(m.rope_ready, 1)
        if what == "scores":
            dve.wait_ge(m.scores_full, UNITS * t + i + 1)
            qb, half, heads = unit(i)
            per = REP // (qb + 1)
            v.tensor_reduce(m.q[:, par, qb, half * per:(half + 1) * per, heads[0]:heads[0] + PAIR, HD].rearrange("p r g -> p g r"),
                            k.bank[:, heads[0]:heads[0] + PAIR, :].rearrange("p g (r n) -> p g r n", r=per),
                            AX.X, ALU.max, negate=True).then_inc(m.max_ready, 1)
        if what == "att":
            dve.wait_ge(m.av_turned, 2 * (t + 1))
            outs = [k.bank[:, 4 + j, :].rearrange("p (r g w) -> p g r w", r=REP, g=KV) for j in range(SEQ_TILES)]
            for j in range(SEQ_TILES):
                last = v.reciprocal(m.rden[:, j, :].rearrange("p (g r) -> p g r", g=KV), outs[j][:, :, :, HD])
            link(last)
            if begun(t):
                dve.wait_ge(m.attT_full, t)
            for j in range(SEQ_TILES):
                for g in range(KV):
                    heads = slice(g * REP, (g + 1) * REP)
                    last = v.tensor_tensor(m.att[:, j, :].rearrange("p (h f) -> p h f", h=HEADS)[:, heads],
                                           outs[j][:, g, :, 0:HD],
                                           m.rden[:, j, heads].unsqueeze(2).to_broadcast([P, REP, HD]), ALU.mult)
            last.then_inc(m.att_ready, 1)
        if what == "post":
            dve.wait_ge(m.proj_full, t + 1)
            v.tensor_tensor(m.y[:], k.bank[:, 4, :].rearrange("p (j d) -> p j d", j=SEQ_TILES),
                            m.b_o[:].unsqueeze(1).to_broadcast([P, SEQ_TILES, D]), ALU.add).then_inc(m.proj_used, 1)
            dve.wait_ge(m.proj_used, t + 1)
            for j in range(SEQ_TILES):
                last = v.bn_stats(m.pstat[:, j, :], m.y[:, j, :])
            link(last)
            own_wait(k, dve)
            for j in range(SEQ_TILES):
                last = v.bn_aggr(m.pmv[:, j, :], m.pstat[:, j, :])
            link(last)
            v.tensor_scalar(m.pmv[:, :, 1], m.pmv[:, :, 1], EPS, None, ALU.add).then_inc(m.post_var, 1)
            dve.wait_ge(m.post_rstd, t + 1)
            for j in range(SEQ_TILES):
                last = v.tensor_scalar(m.y[:, j, :], m.y[:, j, :], m.pmv[:, j, 0:1], m.prstd[:, j:j + 1],
                                       ALU.subtract, ALU.mult)
            link(last)
            x = cols(k.x, t, SEQ_TILES * D)
            v.tensor_tensor(x, x, m.y[:].rearrange("p j d -> p (j d)"), ALU.add).then_inc(m.x_done, 1)
            dve.wait_ge(m.x_done, t + 1)
            for j in range(SEQ_TILES):
                last = v.bn_stats(cols(k.next_stat, SEQ_TILES * t + j, 6), cols(k.x, SEQ_TILES * t + j))
            last.then_inc(k.next_stats, 1)

    v.memset(m.q[:, :, :, :, :, HD:SLOT], 0.0)
    v.memset(m.kk[:, :, :, HD:SLOT], 0.0)
    link(v.memset(m.v[:, :, :, :, HD:OW], 1.0))
    link(v.memset(m.kk[:, :, :, HD:HD + 1], 1.0))
    dve.wait_ge(m.loaded, m.LOADS)
    go_through(m, dve, step, chain, 2 * (2 + 2 * 1 + 1 + 3))
    dve.wait_ge(m.x_done, m.finished)


def attention_pool(k, m, pool):
    g = k.nc.gpsimd
    g.memset(m.kT[:], 0.0).then_inc(m.tables, 1)
    g.memset(m.mask_q[:], 0.0)
    g.memset(m.mask_k[:], 0.0).then_inc(m.tables_step, 1)
    pool.wait_ge(m.tables_step, 1)
    g.affine_select(out=m.mask_q[:], in_=m.mask_q[:], compare_op=ALU.is_ge, fill=MASKED, base=0,
                    pattern=[[0, REP], [-1, P]], channel_multiplier=1).then_inc(m.tables, 2)
    g.affine_select(out=m.mask_k[:], in_=m.mask_k[:], compare_op=ALU.is_ge, fill=MASKED, base=0,
                    pattern=[[0, REP], [1, P]], channel_multiplier=-1).then_inc(m.tables, 2)

    def step(what, t, par, i):
        if what == "norm":
            pool.wait_ge(m.var_ready, t + 1)
            g.tensor_tensor(m.rstd[:], m.mv[:, :, 1], k.minus_half[:, 0:SEQ_TILES], ALU.pow).then_inc(m.rstd_ready, 1)
        if what == "post":
            pool.wait_ge(m.post_var, t + 1)
            g.tensor_tensor(m.prstd[:], m.pmv[:, :, 1], k.minus_half[:, 0:SEQ_TILES], ALU.pow).then_inc(m.post_rstd, 1)

    go_through(m, pool, step)


INNER = 512
STATE = 16
SH = 8
SHD = INNER // SH
TAPS = 4
FT = INNER // P
C_ROW = 32
BC = C_ROW + STATE
SEG = S + P
PARTS = 3
DOWN = 2.0 ** -20


class Ssm:

    def __init__(self, k, a):
        self.k, self.a = k, a
        self.finished = SEQS
        self.turns = (SEQS - 4) // 2
        self.loaded = k.sem("ssm_loaded")
        self.tables = k.sem("ssm_tables")
        self.tables_step = k.sem("ssm_tables_step")
        self.var_ready = k.sem("ssm_var_ready")
        self.rstd_ready = k.sem("ssm_rstd_ready")
        self.xn_ready = k.sem("ssm_xn_ready")
        self.xT_full = k.sem("ssm_xT_full")
        self.xT_ready = k.sem("ssm_xT_ready")
        self.feat_full = k.sem("ssm_feat_full")
        self.feat_ready = k.sem("ssm_feat_ready")
        self.gate_full = k.sem("ssm_gate_full")
        self.dAT_full = k.sem("ssm_dAT_full")
        self.xtok_full = k.sem("ssm_xtok_full")
        self.out_full = k.sem("ssm_out_full")
        self.out_read = k.sem("ssm_out_read")
        self.dt_read = k.sem("ssm_dt_read")
        self.tap_ready = k.sem("ssm_tap_ready")
        self.conv_ready = k.sem("ssm_conv_ready")
        self.silu_ready = k.sem("ssm_silu_ready")
        self.bc_ready = k.sem("ssm_bc_ready")
        self.gate_ready = k.sem("ssm_gate_ready")
        self.xtok_ready = k.sem("ssm_xtok_ready")
        self.xdt_ready = k.sem("ssm_xdt_ready")
        self.min_ready = k.sem("ssm_min_ready")
        self.e_ready = k.sem("ssm_e_ready")
        self.w_ready = k.sem("ssm_w_ready")
        self.ln_ready = k.sem("ssm_ln_ready")
        self.da_ready = k.sem("ssm_da_ready")
        self.decay_ready = k.sem("ssm_decay_ready")
        self.parts_ready = k.sem("ssm_parts_ready")
        self.dAT_ready = k.sem("ssm_dAT_ready")
        self.dab_full = k.sem("ssm_dab_full")
        self.scan_done = k.sem("ssm_scan_done")
        self.g_full = k.sem("ssm_g_full")
        self.weight_done = k.sem("ssm_weight_done")
        self.y_full = k.sem("ssm_y_full")
        self.y_read = k.sem("ssm_y_read")
        self.yg_ready = k.sem("ssm_yg_ready")
        self.w_out_ready = k.sem("ssm_w_out_ready")
        self.square_ready = k.sem("ssm_square_ready")
        self.post_var = k.sem("ssm_post_var")
        self.post_rstd = k.sem("ssm_post_rstd")
        self.x_done = k.sem("ssm_x_done")
        self.dve_step = k.sem("ssm_dve_step")
        self.log_ready = k.sem("ssm_log_ready")

    def weights(self, sb):
        self.w_x = sb("w_x", [P, KD, INNER])
        self.w_bc = sb("w_bc", [P, KD, BC])
        self.w_g = sb("w_g", [P, KD, INNER])
        self.w_dt = sb("w_dt", [P, KD, SH])
        self.w_out = sb("w_out", [P, FT, D])
        self.taps = sb("taps", [P, FT, TAPS + 1])
        self.taps_bc = sb("taps_bc", [BC, TAPS + 1])
        self.a_log = sb("a_log", [P, SH])
        self.skip = sb("skip", [P, FT])
        self.dt_bias = sb("dt_bias", [P, SH])
        self.norm_w = sb("norm_w", [P, FT])
        self.sel = sb("sel", [PARTS * SH, SH, P], BF16)

    def load(self, sp):
        a = self.a
        for dst, src in ((self.w_x, a["w_x"].rearrange("c p n -> p c n")), (self.w_bc, a["w_bc"].rearrange("c p n -> p c n")),
                         (self.w_g, a["w_g"].rearrange("c p n -> p c n")), (self.w_dt, a["w_dt"].rearrange("c p n -> p c n")),
                         (self.w_out, a["w_out"].rearrange("c p n -> p c n")), (self.taps, a["taps"]),
                         (self.taps_bc, a["taps_bc"]), (self.a_log, a["a_log"]), (self.skip, a["skip"]),
                         (self.dt_bias, a["dt_bias"]), (self.norm_w, a["norm_w"])):
            sp.dma_start(dst[:], src).then_inc(self.loaded, 16)

    LOADS = 11 * 16

    def buffers(self, sb):
        self.neg_a = sb("neg_a", [P, SH])
        self.a_lim = sb("a_lim", [P, SH])
        self.pos_a = sb("pos_a", [P, SH])
        self.delta = sb("delta", [P, S])
        self.stat = sb("ssm_stat", [P, SEQ_TILES, 6])
        self.mv = sb("ssm_mv", [P, SEQ_TILES, 2])
        self.rstd = sb("ssm_rstd", [P, SEQ_TILES])
        self.pstat = sb("ssm_pstat", [P, SEQ_TILES, 6])
        self.pmv = sb("ssm_pmv", [P, SEQ_TILES, 2])
        self.prstd = sb("ssm_prstd", [P, SEQ_TILES])
        self.xn = sb("ssm_xn", [P, SEQ_TILES, D])
        self.xT = sb("ssm_xT", [P, KD, S])
        self.feat = sb("feat", [P, FT, TAPS - 1 + S])
        self.feat_bc = sb("feat_bc", [BC, TAPS - 1 + S])
        self.conv = sb("conv", [P, 2, FT, S])
        self.conv_bc = sb("conv_bc", [BC, S])
        self.bT = sb("bT", [STATE, 2, S])
        self.cT = sb("cT", [STATE, 2, S])
        self.gate = sb("gate", [P, 2, FT, S])
        self.xdt = sb("xdt", [P, 2, SEQ_TILES, INNER])
        self.s_u = sb("s_u", [P, SEQ_TILES, SH])
        self.s_mn = sb("s_mn", [P, SEQ_TILES, SH])
        self.s_e = sb("s_e", [P, SEQ_TILES, SH])
        self.s_w = sb("s_w", [P, SEQ_TILES, SH])
        self.s_ln = sb("s_ln", [P, SEQ_TILES, SH])
        self.s_eq = sb("s_eq", [P, SEQ_TILES, SH])
        self.s_num = sb("s_num", [P, SEQ_TILES, SH])
        self.s_den = sb("s_den", [P, SEQ_TILES, SH])
        self.s_dt = sb("s_dt", [P, SEQ_TILES, SH])
        self.s_da = sb("s_da", [P, SEQ_TILES, SH])
        self.s_decay = sb("s_decay", [P, SEQ_TILES, SH])
        self.s_rest = sb("s_rest", [P, SEQ_TILES, SH])
        self.parts = sb("parts", [P, SEQ_TILES, PARTS, SH], BF16)
        self.dAT = sb("dAT", [PARTS * SH, 2, S], BF16)
        self.m = sb("m", [P, SH, SEG])
        n = SEQ_TILES * INNER // D
        room = [self.k.down_w[:, E + 2 + i * n:E + 2 + (i + 1) * n, :] for i in range(3)]
        self.xtok = room[0].rearrange("p (s c) d -> p s (c d)", s=SEQ_TILES)
        self.yg, self.square = room[1:]
        self.one = sb("one", [P, 1])
        self.ms = sb("ms", [P, SEQ_TILES])
        self.z = sb("ssm_z", [P, SEQ_TILES, D])

    ORDER = (
        (0, "dab", 0), (0, "gmat", 0), (0, "dab", 1), (0, "xdt", 0), (1, "feat", 0), (0, "dab", 2), (1, "feat", 1),
        (1, "bcdt", 0), (0, "weight", 0), (0, "dab", 3), (0, "ymm", 0), (0, "weight", 1), (0, "ymm", 1), (1, "dt", 0),
        (1, "conv", 0), (1, "dt", 1), (1, "gate", 0), (0, "gating", 0), (0, "gating", 1), (0, "out", 0), (1, "dt", 2),
        (1, "gate", 1), (1, "conv", 2), (1, "conv", 1), (1, "dt", 3), (1, "turn_dA", 0), (1, "conv", 3),
        (1, "silu", 0), (2, "norm", 0), (0, "post", 0), (2, "norm", 1), (1, "turn_c", 0), (1, "turn_c", 1),
        (2, "turn_x", 0), (0, "post", 1),
    )

    def order(self, t, par, first, last):
        for ahead, what, i in self.ORDER:
            if not (ahead and last or ahead == 2 and isinstance(t, int) and t + 2 >= SEQS):
                yield what, t + ahead, (par + ahead) % 2, i

    def head(self):
        for what, i in (("norm", 0), ("norm", 1), ("turn_x", 0), ("feat", 0), ("feat", 1), ("bcdt", 0), ("gate", 0),
                        ("gate", 1), ("dt", 0), ("conv", 0), ("dt", 1), ("conv", 1), ("dt", 2), ("conv", 2), ("dt", 3),
                        ("turn_dA", 0), ("conv", 3), ("silu", 0), ("turn_c", 0), ("turn_c", 1)):
            yield what, 0, 0, i
        for what, i in (("norm", 0), ("norm", 1), ("turn_x", 0)):
            yield what, 1, 1, i
        yield from self.order(0, 0, True, False)
        yield from self.order(1, 1, False, False)

    def pair(self, it):
        yield from self.order(2 * it + 2, 0, False, False)
        yield from self.order(2 * it + 3, 1, False, False)

    def rest(self):
        yield from self.order(SEQS - 2, 0, False, False)
        yield from self.order(SEQS - 1, 1, False, True)


def ssm_layout(i):
    w = i["L1_attn_W_in"]
    o = 2 * INNER
    w_bc = np.zeros((D, BC), w.dtype)
    w_bc[:, 0:STATE] = w[:, o:o + STATE]
    w_bc[:, C_ROW:BC] = w[:, o + STATE:o + 2 * STATE]
    taps = np.concatenate([i["L1_attn_conv_w"], i["L1_attn_conv_b"][:, None]], axis=1)
    taps_bc = np.zeros((BC, TAPS + 1), taps.dtype)
    taps_bc[0:STATE] = taps[INNER:INNER + STATE]
    taps_bc[C_ROW:BC] = taps[INNER + STATE:]

    def rows(v):
        return np.broadcast_to(v, (P, v.shape[0]))

    return {
        "w_x": w[:, INNER:o].reshape(KD, P, INNER), "w_bc": w_bc.reshape(KD, P, BC),
        "w_g": w[:, 0:INNER].reshape(KD, P, INNER), "w_dt": w[:, o + 2 * STATE:].reshape(KD, P, SH),
        "w_out": i["L1_attn_W_out"].reshape(FT, P, D),
        "taps": taps[0:INNER].reshape(FT, P, TAPS + 1).transpose(1, 0, 2), "taps_bc": taps_bc,
        "a_log": rows(i["L1_attn_A_log"]), "skip": np.repeat(i["L1_attn_D_skip"], SHD).reshape(FT, P).T,
        "dt_bias": rows(i["L1_attn_dt_bias"]), "norm_w": i["L1_attn_norm_w"].reshape(FT, P).T,
    }


DECAY_BANK, Y_BANK, G_BANK = 0, 2, 4
BANK_OF = {("turn_x", 0): 5, ("feat", 0): 6, ("feat", 1): 7, ("bcdt", 0): 5, ("gate", 0): 6, ("gate", 1): 7,
           ("turn_dA", 0): 5, ("turn_c", 0): 6, ("turn_c", 1): 7}
OUT_BANK, SUM_BANK = Y_BANK, Y_BANK + 1


def ssm_tensor(k, m, pe):
    nc = k.nc
    mm, turn = nc.tensor.matmul, nc.tensor.transpose

    def step(what, t, par, i):
        if (what, i) in BANK_OF:
            to = k.bank[:, BANK_OF[what, i], :]
        if what == "turn_x":
            pe.wait_ge(m.xn_ready, t + 1)
            if begun(t):
                pe.wait_ge(m.dAT_ready, t)
            for c in range(KD):
                for j in range(SEQ_TILES):
                    last = turn(to[:, (c * SEQ_TILES + j) * P:(c * SEQ_TILES + j + 1) * P],
                                m.xn[:, j, c * P:(c + 1) * P], k.ident[:])
            last.then_inc(m.xT_full, 1)
        if what == "feat":
            pe.wait_ge(m.xT_ready, t + 1)
            if begun(2 * t - 1 + i):
                pe.wait_ge(m.xtok_ready, 2 * t - 1 + i)
            for f in (0, 1):
                for c in range(KD):
                    last = mm(to[:, f * S:(f + 1) * S], m.w_x[:, c, (2 * i + f) * P:(2 * i + f + 1) * P], m.xT[:, c, :],
                              start=(c == 0), stop=(c == KD - 1))
            last.then_inc(m.feat_full, 1)
        if what == "bcdt":
            pe.wait_ge(m.xT_ready, t + 1)
            for c in range(KD):
                mm(to[0:BC, 0:S], m.w_bc[:, c, :], m.xT[:, c, :], start=(c == 0), stop=(c == KD - 1))
            for j in range(SEQ_TILES):
                for c in range(KD):
                    last = mm(to[:, S + j * SH:S + (j + 1) * SH], m.xT[:, c, j * P:(j + 1) * P], m.w_dt[:, c, :],
                              start=(c == 0), stop=(c == KD - 1))
            last.then_inc(m.feat_full, 1)
        if what == "gate":
            pe.wait_ge(m.feat_ready, 3 * t + i + 1)
            for f in (0, 1):
                for c in range(KD):
                    last = mm(to[:, f * S:(f + 1) * S], m.w_g[:, c, (2 * i + f) * P:(2 * i + f + 1) * P], m.xT[:, c, :],
                              start=(c == 0), stop=(c == KD - 1))
            last.then_inc(m.gate_full, 1)
        if what == "turn_dA":
            pe.wait_ge(m.parts_ready, t + 1)
            pe.wait_ge(m.feat_ready, 3 * t + 3)
            to = to.bitcast(BF16)
            for j in range(SEQ_TILES):
                last = turn(to[0:PARTS * SH, j * P:(j + 1) * P], m.parts[:, j].rearrange("p a h -> p (a h)"), k.ident_b[:])
            last.then_inc(m.dAT_full, 1)
        if what == "turn_c":
            pe.wait_ge(m.silu_ready, t + 1)
            pe.wait_ge(m.gate_ready, 2 * t + i + 1)
            for f in range(FT):
                last = turn(to[:, f * P:(f + 1) * P], m.conv[:, par, f, i * P:(i + 1) * P], k.ident[:])
            last.then_inc(m.xtok_full, 1)
        if what == "out":
            pe.wait_ge(m.yg_ready, 2 * t + 2)
            for j in range(SEQ_TILES):
                for f in range(FT):
                    mm(k.bank[:, OUT_BANK, j * D:(j + 1) * D], m.yg[:, f, j * P:(j + 1) * P], m.w_out[:, f, :],
                       start=(f == 0), stop=(f == FT - 1))
            pe.wait_ge(m.square_ready, 2 * t + 2)
            for j in range(SEQ_TILES):
                for f in range(FT):
                    last = mm(k.bank[:, SUM_BANK, j:j + 1], m.square[:, f, j * P:(j + 1) * P], m.one[:],
                              start=(f == 0), stop=(f == FT - 1))
            last.then_inc(m.out_full, 1)
        if what == "dab":
            n = 4 * t + i
            pe.wait_ge(m.dAT_ready, t + 1)
            if begun(n - 1):
                pe.wait_ge(m.scan_done, n - 1)
            for h in (0, 1):
                last = mm(k.bank[:, DECAY_BANK + i % 2, h * S:(h + 1) * S], m.sel[:, 2 * i + h, :], m.dAT[:, par, :],
                          start=True, stop=True)
            last.then_inc(m.dab_full, 1)
        if what == "gmat":
            pe.wait_ge(m.bc_ready, t + 1)
            if begun(2 * t):
                pe.wait_ge(m.weight_done, 2 * t)
            mm(k.bank[:, G_BANK, 0:S], m.bT[:, par, 0:P], m.cT[:, par, :], start=True, stop=True)
            mm(k.bank[:, G_BANK, S:SEG], m.bT[:, par, P:S], m.cT[:, par, P:S], start=True, stop=True).then_inc(m.g_full, 1)
        if what == "ymm":
            pe.wait_ge(m.weight_done, 2 * t + i + 1)
            pe.wait_ge(m.xdt_ready, t + 1)
            if begun(t):
                pe.wait_ge(m.out_read, t)
            for pair in (2 * i, 2 * i + 1):
                to = [(h, k.bank[(h % 2) * SHD:(h % 2 + 1) * SHD, Y_BANK + i, (pair % 2) * S:(pair % 2 + 1) * S])
                      for h in (2 * pair, 2 * pair + 1)]
                for h, y in to:
                    mm(y, m.xdt[:, par, 0, h * SHD:(h + 1) * SHD], m.m[:, h, 0:S], start=True, stop=False,
                       skip_group_check=True)
                for h, y in to:
                    last = mm(y[:, P:S], m.xdt[:, par, 1, h * SHD:(h + 1) * SHD], m.m[:, h, S:SEG], start=False, stop=True,
                              skip_group_check=True)
            last.then_inc(m.y_full, 1)

    pe.wait_ge(m.loaded, m.LOADS)
    pe.wait_ge(m.tables_step, 2 + PARTS)
    pe.wait_ge(m.w_out_ready, 1)
    go_through(m, pe, step)


def ssm_scalar(k, m, act):
    nc = k.nc
    copy, activation = nc.scalar.copy, nc.scalar.activation
    act.wait_ge(m.loaded, m.LOADS)
    act.wait_ge(m.log_ready, 1)
    activation(m.pos_a[:], m.a_lim[:], ACT.Exp).then_inc(m.tables, 1)

    def step(what, t, par, i):
        if (what, i) in BANK_OF:
            at = k.bank[:, BANK_OF[what, i], :]
        if what == "turn_x":
            act.wait_ge(m.xT_full, t + 1)
            if begun(2 * t):
                act.wait_ge(m.gate_full, 2 * t)
            copy(m.xT[:].rearrange("p c t -> p (c t)"), at).then_inc(m.xT_ready, 1)
        if what == "feat":
            act.wait_ge(m.feat_full, 3 * t + i + 1)
            if begun(t):
                act.wait_ge(m.conv_ready, t)
            copy(m.feat[:, 2 * i:2 * i + 2, TAPS - 1:], at.rearrange("p (f t) -> p f t", f=2)).then_inc(m.feat_ready, 1)
        if what == "bcdt":
            act.wait_ge(m.feat_full, 3 * t + 3)
            if begun(t):
                act.wait_ge(m.conv_ready, t)
            copy(m.feat_bc[:, TAPS - 1:], at[0:BC, 0:S]).then_inc(m.feat_ready, 1)
        if what == "dt" and i == 0:
            act.wait_ge(m.min_ready, t + 1)
            activation(m.s_e[:], m.s_mn[:], ACT.Exp).then_inc(m.e_ready, 1)
        if what == "dt" and i == 1:
            act.wait_ge(m.w_ready, t + 1)
            activation(m.s_ln[:], m.s_w[:], ACT.Ln).then_inc(m.ln_ready, 1)
        if what == "dt" and i == 2:
            act.wait_ge(m.da_ready, t + 1)
            activation(m.s_decay[:], m.s_da[:], ACT.Exp).then_inc(m.decay_ready, 1)
        if what == "gate":
            act.wait_ge(m.gate_full, 2 * t + i + 1)
            if begun(2 * (t - 1)):
                act.wait_ge(m.yg_ready, 2 * (t - 1))
            activation(m.gate[:, par, 2 * i:2 * i + 2, :].rearrange("p f t -> p (f t)"), at, ACT.Silu).then_inc(m.gate_ready, 1)
        if what == "turn_dA":
            act.wait_ge(m.dAT_full, t + 1)
            if begun(4 * (t - 1)):
                act.wait_ge(m.dab_full, 4 * (t - 1))
            copy(m.dAT[:, par, :], at.bitcast(BF16)[0:PARTS * SH, 0:S]).then_inc(m.dAT_ready, 1)
        if what == "conv" and i == 0:
            act.wait_ge(m.feat_ready, 3 * t + 3)
            if begun(2 * (t - 1)):
                act.wait_ge(m.xtok_full, 2 * (t - 1))
                act.wait_ge(m.y_read, 2 * (t - 1))
            for f in range(FT + 1):
                src, dst, taps = (m.feat[:, f], m.conv[:, par, f], m.taps[:, f]) if f < FT else (m.feat_bc[:], m.conv_bc[:], m.taps_bc[:])
                last = activation(dst, src[:, 0:S], ACT.Identity, bias=taps[:, TAPS:TAPS + 1], scale=taps[:, 0:1])
            last.then_inc(m.tap_ready, 1)
        if what == "silu":
            act.wait_ge(m.conv_ready, t + 1)
            if begun(t - 1):
                act.wait_ge(m.g_full, t - 1)
            activation(m.bT[:, par, :], m.conv_bc[0:STATE, :], ACT.Silu)
            activation(m.cT[:, par, :], m.conv_bc[C_ROW:BC, :], ACT.Silu).then_inc(m.bc_ready, 1)
            whole = m.conv[:, par].rearrange("p f t -> p (f t)")
            activation(whole, whole, ACT.Silu).then_inc(m.silu_ready, 1)
        if what == "turn_c":
            act.wait_ge(m.xtok_full, 2 * t + i + 1)
            if begun(t):
                act.wait_ge(m.xdt_ready, t)
            copy(m.xtok[:, i, :], at).then_inc(m.xtok_ready, 1)
        if what == "gating":
            act.wait_ge(m.yg_ready, 2 * t + i + 1)
            if begun(t):
                act.wait_ge(m.out_full, t)
            activation(m.square[:, 2 * i:2 * i + 2, :], m.yg[:, 2 * i:2 * i + 2, :], ACT.Square).then_inc(m.square_ready, 1)

    go_through(m, act, step)


def ssm_vector(k, m, dve):
    nc = k.nc
    v = nc.vector
    tt, ts, stt = v.tensor_tensor, v.tensor_scalar, v.scalar_tensor_tensor
    chain = Chain(dve, m.dve_step)
    link = chain.link

    def rows(a):
        return a[:].unsqueeze(1).to_broadcast([P, SEQ_TILES, SH])

    def step(what, t, par, i):
        if what == "norm" and i == 0:
            for j in range(SEQ_TILES):
                last = v.bn_stats(m.stat[:, j, :], cols(k.x, SEQ_TILES * t + j))
            link(last)
            own_wait(k, dve)
            for j in range(SEQ_TILES):
                last = v.bn_aggr(m.mv[:, j, :], m.stat[:, j, :])
            link(last)
            ts(m.mv[:, :, 1], m.mv[:, :, 1], EPS, None, ALU.add).then_inc(m.var_ready, 1)
        if what == "norm" and i == 1:
            dve.wait_ge(m.rstd_ready, t + 1)
            if begun(t):
                dve.wait_ge(m.xT_full, t)
            for j in range(SEQ_TILES):
                last = ts(m.xn[:, j, :], cols(k.x, SEQ_TILES * t + j), m.mv[:, j, 0:1], m.rstd[:, j:j + 1],
                          ALU.subtract, ALU.mult)
            last.then_inc(m.xn_ready, 1)
        if what == "dt" and i == 0:
            dve.wait_ge(m.feat_ready, 3 * t + 3)
            raw = k.bank[:, BANK_OF["bcdt", 0], S:S + SEQ_TILES * SH].rearrange("p (j h) -> p j h", j=SEQ_TILES)
            tt(m.s_u[:], raw, rows(m.dt_bias), ALU.add).then_inc(m.dt_read, 1)
            dve.wait_ge(m.dt_read, t + 1)
            stt(m.s_mn[:], m.s_u[:], -1.0, m.s_u[:], ALU.mult, ALU.min).then_inc(m.min_ready, 1)
        if what == "dt" and i == 1:
            dve.wait_ge(m.e_ready, t + 1)
            ts(m.s_w[:], m.s_e[:], 1.0, None, ALU.add).then_inc(m.w_ready, 1)
            dve.wait_ge(m.w_ready, t + 1)
            link(ts(m.s_den[:], m.s_w[:], -1.0, None, ALU.add))
            link(ts(m.s_eq[:], m.s_den[:], 0.0, None, ALU.is_equal))
            link(tt(m.s_den[:], m.s_den[:], m.s_eq[:], ALU.add))
            link(v.reciprocal(m.s_rest[:], m.s_den[:]))
            link(tt(m.s_rest[:], m.s_rest[:], m.s_e[:], ALU.mult))
        if what == "dt" and i == 2:
            dve.wait_ge(m.ln_ready, t + 1)
            link(tt(m.s_num[:], m.s_ln[:], m.s_eq[:], ALU.add))
            link(tt(m.s_num[:], m.s_num[:], m.s_rest[:], ALU.mult))
            link(stt(m.s_dt[:], m.s_u[:], 0.0, m.s_num[:], ALU.max, ALU.add))
            link(stt(m.s_da[:], m.s_dt[:], DOWN, rows(m.neg_a), ALU.mult, ALU.mult))
            ts(m.s_da[:], m.s_da[:], -200.0 * DOWN, 1.0 / DOWN, ALU.max, ALU.mult).then_inc(m.da_ready, 1)
        if what == "dt" and i == 3:
            dve.wait_ge(m.decay_ready, t + 1)
            if begun(t):
                dve.wait_ge(m.dAT_full, t)
            link(v.tensor_copy(m.parts[:, :, 0, :], m.s_decay[:]))
            link(tt(m.s_rest[:], m.s_decay[:], m.parts[:, :, 0, :], ALU.subtract))
            link(v.tensor_copy(m.parts[:, :, 1, :], m.s_rest[:]))
            tt(m.parts[:, :, 2, :], m.s_rest[:], m.parts[:, :, 1, :], ALU.subtract).then_inc(m.parts_ready, 1)
        if what == "conv" and i > 0:
            dve.wait_ge(m.tap_ready, t + 1)
            for f in range(FT + 1):
                src, dst, taps = (m.feat[:, f], m.conv[:, par, f], m.taps[:, f]) if f < FT else (m.feat_bc[:], m.conv_bc[:], m.taps_bc[:])
                last = stt(dst, src[:, i:i + S], taps[:, i:i + 1], dst, ALU.mult, ALU.add)
            if i == TAPS - 1:
                last.then_inc(m.conv_ready, 1)
            else:
                link(last)
        if what == "xdt":
            dve.wait_ge(m.xtok_ready, 2 * t + 2)
            if begun(2 * (t - 1)):
                dve.wait_ge(m.y_full, 2 * (t - 1))
            for j in range(SEQ_TILES):
                last = tt(m.xdt[:, par, j, :].rearrange("p (h f) -> p h f", h=SH),
                          m.xtok[:, j, :].rearrange("p (h f) -> p h f", h=SH),
                          m.s_dt[:, j, :].unsqueeze(2).to_broadcast([P, SH, SHD]), ALU.mult)
            last.then_inc(m.xdt_ready, 1)
        if what == "dab":
            dve.wait_ge(m.dab_full, 4 * t + i + 1)
            if begun(2 * t):
                dve.wait_ge(m.y_full, 2 * t)
            for h in (0, 1):
                base = k.bank[:, DECAY_BANK + i % 2, h * S:(h + 1) * S]
                to = m.m[:, 2 * i + h, :]
                v.tensor_tensor_scan(to[:, 0:S], base, m.delta[:], 0.0, ALU.mult, ALU.add)
                last = v.tensor_tensor_scan(to[:, S:SEG], base[:, P:S], m.delta[:, 0:P], 0.0, ALU.mult, ALU.add)
            last.then_inc(m.scan_done, 1)
        if what == "weight":
            dve.wait_ge(m.g_full, t + 1)
            dve.wait_ge(m.scan_done, 4 * t + 2 * i + 2)
            part = m.m[:, 4 * i:4 * i + 4, :]
            tt(part, part, k.bank[:, G_BANK, 0:SEG].unsqueeze(1).to_broadcast([P, 4, SEG]), ALU.mult)\
                .then_inc(m.weight_done, 1)
        if what == "gating":
            pair = slice(2 * i, 2 * i + 2)
            dve.wait_ge(m.y_full, 2 * t + i + 1)
            dve.wait_ge(m.silu_ready, t + 1)
            if begun(t):
                dve.wait_ge(m.out_full, t)
            for f in (2 * i, 2 * i + 1):
                last = stt(m.yg[:, f, :], m.conv[:, par, f, :], m.skip[:, f:f + 1],
                           k.bank[:, Y_BANK + i, (f % 2) * S:(f % 2 + 1) * S], ALU.mult, ALU.add)
            last.then_inc(m.y_read, 1)
            dve.wait_ge(m.y_read, 2 * t + i + 1)
            dve.wait_ge(m.gate_ready, 2 * t + i + 1)
            tt(m.yg[:, pair, :], m.yg[:, pair, :], m.gate[:, par, pair, :], ALU.mult).then_inc(m.yg_ready, 1)
        y = k.bank[:, OUT_BANK, :].rearrange("p (j d) -> p j d", j=SEQ_TILES)
        if what == "post" and i == 0:
            dve.wait_ge(m.out_full, t + 1)
            link(ts(m.ms[:], k.bank[:, SUM_BANK, 0:SEQ_TILES], 1.0 / INNER, EPS, ALU.mult, ALU.add))
            for j in range(SEQ_TILES):
                last = v.bn_stats(m.pstat[:, j, :], y[:, j, :])
            link(last)
            own_wait(k, dve)
            for j in range(SEQ_TILES):
                last = v.bn_aggr(m.pmv[:, j, :], m.pstat[:, j, :])
            link(last)
            stt(m.pmv[:, :, 1], m.ms[:], EPS, m.pmv[:, :, 1], ALU.mult, ALU.add).then_inc(m.post_var, 1)
        if what == "post" and i == 1:
            dve.wait_ge(m.post_rstd, t + 1)
            for j in range(SEQ_TILES):
                last = ts(m.z[:, j, :], y[:, j, :], m.pmv[:, j, 0:1], m.prstd[:, j:j + 1], ALU.subtract, ALU.mult)
            last.then_inc(m.out_read, 1)
            dve.wait_ge(m.out_read, t + 1)
            x = cols(k.x, t, SEQ_TILES * D)
            tt(x, x, m.z[:].rearrange("p j d -> p (j d)"), ALU.add).then_inc(m.x_done, 1)

    v.memset(m.feat[:, :, 0:TAPS - 1], 0.0)
    link(v.memset(m.feat_bc[:, 0:TAPS - 1], 0.0))
    dve.wait_ge(m.loaded, m.LOADS)
    for f in range(FT):
        last = ts(m.w_out[:, f, :], m.w_out[:, f, :], m.norm_w[:, f:f + 1], None, ALU.mult)
    last.then_inc(m.w_out_ready, 1)
    ts(m.a_lim[:], m.a_log[:], 88.0, None, ALU.min).then_inc(m.log_ready, 1)
    dve.wait_ge(m.tables, 2)
    link(ts(m.neg_a[:], m.pos_a[:], -1.0, None, ALU.mult))
    go_through(m, dve, step, chain, 2 * (2 + 9 + 3 + 2 + 3))
    dve.wait_ge(m.x_done, m.finished)


def ssm_pool(k, m, pool):
    g = k.nc.gpsimd
    g.memset(m.delta[:], 0.0)
    g.memset(m.one[:], 1.0).then_inc(m.tables_step, 1)
    g.memset(m.sel[:], 0.0).then_inc(m.tables_step, 1)
    pool.wait_ge(m.tables_step, 2)
    for part in range(PARTS):
        g.affine_select(out=m.sel[:], in_=m.sel[:], compare_op=ALU.not_equal, fill=1.0, base=-part * SH,
                        pattern=[[-1, SH], [0, P]], channel_multiplier=1).then_inc(m.tables_step, 1)
        pool.wait_ge(m.tables_step, 3 + part)
    g.affine_select(out=m.delta[:], in_=m.delta[:], compare_op=ALU.not_equal, fill=1.0, base=0,
                    pattern=[[-1, S]], channel_multiplier=1).then_inc(m.tables, 1)
    pool.wait_ge(m.loaded, m.LOADS)

    def step(what, t, par, i):
        if what == "norm" and i == 0:
            pool.wait_ge(m.var_ready, t + 1)
            g.tensor_tensor(m.rstd[:], m.mv[:, :, 1], k.minus_half[:, 0:SEQ_TILES], ALU.pow).then_inc(m.rstd_ready, 1)
        if what == "post" and i == 0:
            pool.wait_ge(m.post_var, t + 1)
            g.tensor_tensor(m.prstd[:], m.pmv[:, :, 1], k.minus_half[:, 0:SEQ_TILES], ALU.pow).then_inc(m.post_rstd, 1)

    go_through(m, pool, step)


SEQS_FIRST, REST_LOADS = 2, 4
CONSTS = 10


class Kernel:

    def __init__(self, nc, ctx):
        self.nc, self.ctx = nc, ctx

    def sem(self, name):
        return self.ctx.enter_context(self.nc.semaphore(name))

    def sb(self, name, shape, dtype=F32):
        return self.ctx.enter_context(self.nc.sbuf_tensor(name, shape, dtype))


def program(nc, a, out):
    with ExitStack() as ctx:
        k = Kernel(nc, ctx)
        sem, sb = k.sem, k.sb
        k.bank = ctx.enter_context(nc.psum_tensor("bank", [P, 8, BANK], F32))
        k.x = sb("x", [P, TILES * D])
        k.spare = sb("spare", [P, 1])
        k.pool_spare = sb("pool_spare", [P, 2])
        k.ident = sb("ident", [P, P])
        k.ident_b = sb("ident_b", [P, P], BF16)
        k.minus_half = sb("minus_half", [P, TILES])
        k.expert_rank = sb("expert_rank", [P, E])
        k.slot_no = sb("slot_no", [1, SLOTS])
        k.before = sb("before", [P, P], BF16)
        k.all_ones = sb("all_ones", [P, P], BF16)
        k.zero = sb("zero", [P, D])
        k.pair_no = sb("pair_no", [P, 2 * TILES], U32)
        k.filler_no = sb("filler_no", [P, SLOTS], U32)
        gate0 = sb("gate0", [P, KD, E])
        gate1 = sb("gate1", [P, KD, E])
        up_w = sb("up_w", [P, KD, (E + 2) * 2 * 176])
        down_w = k.down_w = sb("down_w", [P, 2 * E + 3, D])
        sorted_in = nc.dram_tensor("sorted_in", (SLOTS * P, ROW), F32, kind="Internal").ap()
        results = nc.dram_tensor("results", (2 * TILES * P + SLOTS * P, D), F32, kind="Internal").ap()

        k.next_stat = sb("next_stat", [P, TILES * 6])
        k.next_stats = sem("next_stats")
        x_first, k.x_loaded = sem("x_first"), sem("x_loaded")
        gates_loaded, moe0_loaded, moe1_loaded = sem("gates_loaded"), sem("moe0_loaded"), sem("moe1_loaded")
        consts = k.consts = sem("consts")
        consts_step = sem("consts_step")
        stored = sem("stored")

        first = SparseMoe(k, 176, up_w, down_w, gate0, [(moe0_loaded, 64), (gates_loaded, 32)], sorted_in, results)
        second = Moe(k, "moe1", 128, 2, 2.5, up_w, down_w, gate1, [(moe1_loaded, 64), (gates_loaded, 32)])
        layers = [Attention(k, a), first, Ssm(k, a), second]
        for layer in layers:
            if not isinstance(layer, (Moe, SparseMoe)):
                layer.weights(sb)
        for layer in layers:
            with ExitStack() as scratch:
                layer.buffers(lambda name, shape, dtype=F32: scratch.enter_context(nc.sbuf_tensor(name, shape, dtype)))

        def walk(eng, **parts):
            before = None
            for layer in layers:
                if before is not None:
                    eng.wait_ge(before.x_done, before.finished)
                parts[type(layer).__name__](k, layer, eng)
                before = layer

        block = ctx.enter_context(nc.Block())

        @block.sync
        def _(sp):
            def load_x(lo, hi, done):
                sp.dma_start(k.x[:, lo * D:hi * D].rearrange("p (t d) -> p t d", d=D),
                             a["x"][lo:hi].rearrange("t p d -> p t d")).then_inc(done, 16)

            first_tiles = SEQS_FIRST * SEQ_TILES
            load_x(0, first_tiles, x_first)
            for n, layer in enumerate(x for x in layers if not isinstance(x, (Moe, SparseMoe))):
                layer.load(sp)
                if n == 0:
                    step = (TILES - first_tiles) // REST_LOADS
                    for c in range(REST_LOADS):
                        load_x(first_tiles + c * step, first_tiles + (c + 1) * step, k.x_loaded)
            sp.dma_start(gate0[:], a["gate0"].rearrange("c p e -> p c e")).then_inc(gates_loaded, 16)
            sp.dma_start(gate1[:], a["gate1"].rearrange("c p e -> p c e")).then_inc(gates_loaded, 16)

            def load_moe(up, down, done):
                W, chunks = a[up].shape[2], a[down].shape[0]
                for c in range(KD):
                    sp.dma_start(up_w[:, c, 0:W], a[up][c]).then_inc(done, 16)
                half = chunks // 2
                for lo, hi in ((0, half), (half, chunks)):
                    sp.dma_start(down_w[:, lo:hi, :], a[down][lo:hi].rearrange("c p d -> p c d")).then_inc(done, 16)

            if first in layers:
                load_moe("up0", "down0", moe0_loaded)
                sp.wait_ge(consts, CONSTS)
                n = SLOTS // ZERO_FILLS
                for i in range(ZERO_FILLS):
                    to = sorted_in[i * n * P:(i + 1) * n * P].rearrange("(n p) d -> p n d", p=P)
                    sp.dma_start(to[:, :, 0:D], k.zero[:].unsqueeze(1).to_broadcast([P, n, D])).then_inc(first.zeroed, 16)
                    sp.dma_start(to[:, :, D:ROW].bitcast(U32), k.filler_no[:, i * n:(i + 1) * n].unsqueeze(2),\
                                 allow_slow_non_contiguous=True)\
                        .then_inc(first.zeroed, 16)
                sparse_sync(k, first, sp)
            if second in layers:
                if first in layers:
                    sp.wait_ge(first.x_done, first.finished)
                load_moe("up1", "down1", moe1_loaded)
            pair = 2
            per_pair = layers[-1].finished * pair // TILES
            with sp.Fori(0, TILES // pair) as it:
                sp.wait_ge(layers[-1].x_done, per_pair * it + per_pair)
                sp.dma_start(out[bass.ds(pair * it, pair)].rearrange("t p d -> p t d"),
                             k.x[:, bass.ds(it * pair * D, pair * D)].rearrange("p (t d) -> p t d", d=D)).then_inc(stored, 16)
            sp.wait_ge(stored, 16 * TILES // pair)

        @block.gpsimd
        def _(pool):
            nc.gpsimd.memset(k.ident[:], 0.0).then_inc(consts_step, 1)
            nc.gpsimd.memset(k.minus_half[:], -0.5).then_inc(consts, 1)
            pool.wait_ge(consts_step, 1)
            nc.gpsimd.affine_select(out=k.ident[:], in_=k.ident[:], compare_op=ALU.not_equal, fill=1.0, base=0,
                                    pattern=[[-1, P]], channel_multiplier=1).then_inc(consts, 1)
            nc.gpsimd.iota(k.slot_no[:], [[1, SLOTS]], base=0, channel_multiplier=0,
                           allow_small_or_imprecise_dtypes=True).then_inc(consts, 1)
            nc.gpsimd.iota(k.expert_rank[:], [[-1, E]], base=E, channel_multiplier=0,
                           allow_small_or_imprecise_dtypes=True).then_inc(consts, 1)
            nc.gpsimd.memset(k.zero[:], 0.0).then_inc(consts, 1)
            nc.gpsimd.iota(k.pair_no[:], [[2 * P, TILES], [1, 2]], base=0, channel_multiplier=2).then_inc(consts, 1)
            nc.gpsimd.iota(k.filler_no[:], [[P, SLOTS]], base=2 * TILES * P, channel_multiplier=1).then_inc(consts, 1)
            nc.gpsimd.memset(k.all_ones[:], 1.0).then_inc(consts, 1)
            pool.wait_ge(consts, 8)
            nc.gpsimd.affine_select(out=k.before[:], in_=k.all_ones[:], compare_op=ALU.is_gt, fill=0.0, base=0,
                                    pattern=[[1, P]], channel_multiplier=-1).then_inc(consts, 1)
            nc.gpsimd.tensor_copy(k.ident_b[:], k.ident[:]).then_inc(consts, 1)
            walk(pool, Moe=moe_pool, SparseMoe=sparse_pool, Attention=attention_pool, Ssm=ssm_pool)

        @block.scalar
        def _(act):
            walk(act, Moe=moe_scalar, SparseMoe=sparse_scalar, Attention=attention_scalar, Ssm=ssm_scalar)

        @block.vector
        def _(dve):
            dve.wait_ge(consts, CONSTS)
            dve.wait_ge(x_first, 16)
            walk(dve, Moe=moe_vector, SparseMoe=sparse_vector, Attention=attention_vector, Ssm=ssm_vector)

        @block.tensor
        def _(pe):
            pe.wait_ge(consts, CONSTS)
            walk(pe, Moe=moe_tensor, SparseMoe=sparse_tensor, Attention=attention_tensor, Ssm=ssm_tensor)


def expert_columns(first, second, per_unit):
    n, d, inter = first.shape
    both = np.stack([first, second]).reshape(2, n // per_unit, per_unit, d, inter)
    return np.ascontiguousarray(both.transpose(3, 1, 0, 2, 4)).reshape(KD, P, n * 2 * inter)


def padded_rows(rows):
    n = rows.shape[0]
    full = np.zeros((-(-n // P) * P, rows.shape[1]), rows.dtype)
    full[:n] = rows
    return full.reshape(-1, P, rows.shape[1])


def layout(i):
    c = np.ascontiguousarray
    arrays = {"x": i["L0_attn_x"].reshape(TILES, P, D)}
    arrays["gate0"] = c(i["L0_ffn_gate_w"].T).reshape(KD, P, E)
    arrays["gate1"] = c(i["L1_ffn_gate_w"].T).reshape(KD, P, E)

    def with_shared(routed, shared):
        return np.concatenate([routed, shared])

    sw1, sw3 = (i[n].reshape(2, 176, D).transpose(0, 2, 1) for n in ("L0_ffn_sw1", "L0_ffn_sw3"))
    arrays["up0"] = expert_columns(with_shared(i["L0_ffn_w1"].transpose(0, 2, 1), sw1),
                                   with_shared(i["L0_ffn_w3"].transpose(0, 2, 1), sw3), 1)
    halves = i["L0_ffn_w2"].transpose(0, 2, 1).reshape(2 * E, -1, D)
    arrays["down0"] = np.concatenate([np.pad(halves, ((0, 0), (0, P - halves.shape[1]), (0, 0))),
                                      padded_rows(i["L0_ffn_sw2"].T)])
    swg, swu = (i[n].reshape(D, 2, P).transpose(1, 0, 2) for n in ("L1_ffn_sWg", "L1_ffn_sWu"))
    arrays["up1"] = expert_columns(with_shared(i["L1_ffn_Wg"], swg), with_shared(i["L1_ffn_Wu"], swu), 2)
    arrays["down1"] = padded_rows(np.concatenate([i["L1_ffn_Wd"].reshape(-1, D), i["L1_ffn_sWd"]]))
    arrays.update(attention_layout(i))
    arrays.update(ssm_layout(i))
    return {n: c(v) for n, v in arrays.items()}


def kernel(**inputs):
    import concourse.bacc as bacc
    from concourse.bass_utils import run_bass_kernel_spmd

    arrays = layout({n: np.asarray(v) for n, v in inputs.items()})
    nc = bacc.Bacc("TRN2", target_bir_lowering=False, num_devices=1)
    handles = {n: nc.dram_tensor("in_" + n, v.shape, mybir.dt.from_np(v.dtype), kind="ExternalInput").ap()
               for n, v in arrays.items()}
    out = nc.dram_tensor("out", (TILES, P, D), F32, kind="ExternalOutput").ap()
    program(nc, handles, out)
    done = run_bass_kernel_spmd(nc, [{"in_" + n: v for n, v in arrays.items()}], core_ids=[0])
    return done.results[0]["out"].reshape(B, S, D)
```
